# Optimizing a Trainium2 kernel written in Bass

```python
import numpy as np
import jax
import jax.numpy as jnp

def _softmax(x, axis=-1):
    return jax.nn.softmax(x, axis=axis)

def _gelu(x):
    return jax.nn.gelu(x, approximate=True)

def _silu(x):
    return jax.nn.silu(x)

def _sigmoid(x):
    return jax.nn.sigmoid(x)

def _layernorm(x, axis=-1, eps=1e-05):
    m = jnp.mean(x, axis=axis, keepdims=True)
    v = jnp.var(x, axis=axis, keepdims=True)
    return (x - m) / jnp.sqrt(v + eps)

def _scatter_add(tgt, idx, src, axis=0):
    return tgt.at[idx].add(src)

def _segment_sum(src, seg, n):
    return jax.ops.segment_sum(src, seg, n)
kernel_name = 'mk_decoder_postln_d1_seqx_r8_d47cce'

def setup_inputs(seed: int=0):
    np.random.seed(seed)
    _w = jnp.asarray

    def _rec_inputs():
        import jax
        import jax.numpy as jnp
        _rk = jax.random.key(seed)
        x = 7.22e-05 + 1 * jax.random.normal(jax.random.fold_in(_rk, 1), (16, 128, 256), jnp.float32)
        _lenS = 128 - jax.random.randint(jax.random.fold_in(_rk, 7), (16,), 0, max(1, 128 // 4) + 1, jnp.int32)
        _lenS2 = 128 - jax.random.randint(jax.random.fold_in(_rk, 8), (16,), 0, max(1, 128 // 4) + 1, jnp.int32)
        _ctx_512P = jax.random.normal(jax.random.fold_in(_rk, 11), (16, 16, 64), jnp.float32)
        _ctx_512c = jax.random.dirichlet(jax.random.fold_in(_rk, 511), 0.3 * jnp.ones((16,), jnp.float32), (16, 128))
        _ctx_512t = jnp.einsum('bsk,bkd->bsd', _ctx_512c, _ctx_512P)
        _ctx_512t = _ctx_512t * jax.lax.rsqrt(jnp.mean(jnp.square(_ctx_512t)) + 1e-12) * 0.953939
        ctx_512 = -0.000514642 + 1.00011 * (_ctx_512t + 0.3 * jax.random.normal(jax.random.fold_in(_rk, 611), (16, 128, 64), jnp.float32))
        return (x, ctx_512)
    x, ctx_512 = _rec_inputs()

    def _L0_attn_setup():
        import jax, jax.numpy as jnp
        import numpy as np
        D_MODEL = 256
        NUM_HEADS = 16
        DILATION = 2
        SEG = 64
        HEAD_DIM = D_MODEL // NUM_HEADS

        def _dilated_attention(x):
            B, N, D = x.shape
            w, r, H, hd = (SEG, DILATION, NUM_HEADS, HEAD_DIM)
            pad = -N % w
            x = jnp.pad(x, ((0, 0), (0, pad), (0, 0)))
            Np = N + pad
            nseg = Np // w
            s = w // r
            xs = x.reshape(B, nseg, w, H, hd).transpose(0, 1, 3, 2, 4)
            offsets = jnp.arange(H) % r
            idx = offsets[:, None] + jnp.arange(s)[None, :] * r
            g = jnp.take_along_axis(xs, idx[None, None, :, :, None], axis=3)
            scale = jnp.asarray(hd, x.dtype) ** (-0.5)
            scores = jnp.einsum('bnhqd,bnhkd->bnhqk', g, g) * scale
            attn = jax.nn.softmax(scores, axis=-1)
            out = jnp.einsum('bnhqk,bnhkd->bnhqd', attn, g)
            out_full = jnp.zeros((B, nseg, H, w, hd), dtype=x.dtype)
            out_full = out_full.at[:, :, jnp.arange(H)[:, None], idx, :].set(out)
            out_full = out_full.transpose(0, 1, 3, 2, 4).reshape(B, Np, D)
            return out_full[:, :N, :]
        key = jax.random.key(seed)
        x = jax.random.normal(key, (4, 1024, D_MODEL), dtype=jnp.float32)
        return {'x': x}
    _L0_attn_all = _L0_attn_setup()
    _L0_attn_in = {k: v for k, v in _L0_attn_all.items() if k in ()}
    del _L0_attn_all

    def _L0_xattn_setup():
        import jax, jax.numpy as jnp
        import numpy as np
        B, S, H, NH, L = (2, 256, 256, 16, 64)
        HD = H // NH
        key = jax.random.key(seed)
        k1, k2, k3, k4, k5 = jax.random.split(key, 5)
        scale = 0.02
        return {'q': jax.random.normal(k1, (B, S, H), dtype=jnp.float32), 'latent_kv': jax.random.normal(k2, (B, S, L), dtype=jnp.float32), 'Wq': jax.random.normal(k3, (H, H), dtype=jnp.float32) * scale, 'Wkv_expand': jax.random.normal(k4, (2 * H, L), dtype=jnp.float32) * scale, 'Wout': jax.random.normal(k5, (H, H), dtype=jnp.float32) * scale}
    _L0_xattn_all = _L0_xattn_setup()
    _L0_xattn_in = {k: v for k, v in _L0_xattn_all.items() if k in ('Wq', 'Wkv_expand', 'Wout')}
    del _L0_xattn_all

    def _L0_ffn_setup():
        import jax, jax.numpy as jnp
        import numpy as np
        HIDDEN = 256
        INTER = 96
        N_EXPERTS = 32
        TOP_K = 8
        key = jax.random.key(seed)
        k = jax.random.split(key, 5)
        s = 1.0 / np.sqrt(HIDDEN)
        return {'hidden_states': jax.random.normal(k[0], (1, 128, HIDDEN), jnp.float32), 'gate_w': jax.random.normal(k[1], (HIDDEN, N_EXPERTS), jnp.float32) * s, 'w_gate': jax.random.normal(k[2], (N_EXPERTS, HIDDEN, INTER), jnp.float32) * s, 'w_up': jax.random.normal(k[3], (N_EXPERTS, HIDDEN, INTER), jnp.float32) * s, 'w_down': jax.random.normal(k[4], (N_EXPERTS, INTER, HIDDEN), jnp.float32) * (1.0 / np.sqrt(INTER))}
    _L0_ffn_all = _L0_ffn_setup()
    _L0_ffn_in = {k: v for k, v in _L0_ffn_all.items() if k in ('gate_w', 'w_gate', 'w_up', 'w_down')}
    del _L0_ffn_all
    return {'x': x, 'ctx_512': ctx_512, 'L0_xattn_Wq': _L0_xattn_in['Wq'], 'L0_xattn_Wkv_expand': _L0_xattn_in['Wkv_expand'], 'L0_xattn_Wout': _L0_xattn_in['Wout'], 'L0_ffn_gate_w': _L0_ffn_in['gate_w'], 'L0_ffn_w_gate': _L0_ffn_in['w_gate'], 'L0_ffn_w_up': _L0_ffn_in['w_up'], 'L0_ffn_w_down': _L0_ffn_in['w_down']}

def reference(x, ctx_512, L0_xattn_Wq, L0_xattn_Wkv_expand, L0_xattn_Wout, L0_ffn_gate_w, L0_ffn_w_gate, L0_ffn_w_up, L0_ffn_w_down):
    import jax
    import jax.numpy as jnp

    def _L0_attn_ref(x):
        import jax, jax.numpy as jnp
        import numpy as np
        D_MODEL = 256
        NUM_HEADS = 16
        DILATION = 2
        SEG = 64
        HEAD_DIM = D_MODEL // NUM_HEADS

        def _dilated_attention(x):
            B, N, D = x.shape
            w, r, H, hd = (SEG, DILATION, NUM_HEADS, HEAD_DIM)
            pad = -N % w
            x = jnp.pad(x, ((0, 0), (0, pad), (0, 0)))
            Np = N + pad
            nseg = Np // w
            s = w // r
            xs = x.reshape(B, nseg, w, H, hd).transpose(0, 1, 3, 2, 4)
            offsets = jnp.arange(H) % r
            idx = offsets[:, None] + jnp.arange(s)[None, :] * r
            g = jnp.take_along_axis(xs, idx[None, None, :, :, None], axis=3)
            scale = jnp.asarray(hd, x.dtype) ** (-0.5)
            scores = jnp.einsum('bnhqd,bnhkd->bnhqk', g, g) * scale
            attn = jax.nn.softmax(scores, axis=-1)
            out = jnp.einsum('bnhqk,bnhkd->bnhqd', attn, g)
            out_full = jnp.zeros((B, nseg, H, w, hd), dtype=x.dtype)
            out_full = out_full.at[:, :, jnp.arange(H)[:, None], idx, :].set(out)
            out_full = out_full.transpose(0, 1, 3, 2, 4).reshape(B, Np, D)
            return out_full[:, :N, :]
        return _dilated_attention(x)

    def _L0_xattn_ref(q, latent_kv, Wq, Wkv_expand, Wout):
        import jax, jax.numpy as jnp
        import numpy as np
        B, S, H, NH, L = (2, 256, 256, 16, 64)
        HD = H // NH
        b, sq, _ = q.shape
        sk = latent_kv.shape[1]
        qp = q @ Wq.T
        kv = latent_kv @ Wkv_expand.T
        k, v = jnp.split(kv, 2, axis=-1)
        qh = qp.reshape(b, sq, NH, HD).transpose(0, 2, 1, 3)
        kh = k.reshape(b, sk, NH, HD).transpose(0, 2, 1, 3)
        vh = v.reshape(b, sk, NH, HD).transpose(0, 2, 1, 3)
        inv_sqrt_d = 1.0 / jnp.sqrt(jnp.float32(HD))
        scores = jnp.einsum('bhqd,bhkd->bhqk', qh, kh) * inv_sqrt_d
        causal = jnp.tril(jnp.ones((sq, sk), dtype=bool))
        scores = jnp.where(causal, scores, jnp.finfo(scores.dtype).min)
        attn = jax.nn.softmax(scores, axis=-1)
        out = jnp.einsum('bhqk,bhkd->bhqd', attn, vh)
        out = out.transpose(0, 2, 1, 3).reshape(b, sq, H)
        return out @ Wout.T

    def _L0_ffn_ref(hidden_states, gate_w, w_gate, w_up, w_down):
        import jax, jax.numpy as jnp
        import numpy as np
        HIDDEN = 256
        INTER = 96
        N_EXPERTS = 32
        TOP_K = 8
        B, S, H = hidden_states.shape
        E = gate_w.shape[1]
        x = hidden_states.reshape(-1, H)
        T = x.shape[0]
        K = TOP_K
        P = T * K
        C = 2 * (P // E)
        probs = jax.nn.softmax(x @ gate_w, axis=-1)
        w, sel = jax.lax.top_k(probs, K)
        w = w / jnp.sum(w, axis=-1, keepdims=True)
        flat_e = sel.reshape(-1)
        flat_t = jnp.repeat(jnp.arange(T), K)
        flat_w = w.reshape(-1)
        order = jnp.argsort(flat_e)
        se = flat_e[order]
        start = jnp.searchsorted(se, jnp.arange(E))
        pos = jnp.arange(P) - start[se]
        slot = jnp.where(pos < C, se * C + pos, E * C)
        slot_pair = jnp.full((E * C,), P, dtype=jnp.int32).at[slot].set(order.astype(jnp.int32), mode='drop')
        t_slot = jnp.concatenate([flat_t, jnp.array([T])])[slot_pair]
        w_slot = jnp.concatenate([flat_w, jnp.zeros((1,), flat_w.dtype)])[slot_pair]
        x_pad = jnp.concatenate([x, jnp.zeros((1, H), x.dtype)], axis=0)
        xg = x_pad[t_slot].reshape(E, C, H)
        g = jnp.einsum('ech,ehi->eci', xg, w_gate)
        u = jnp.einsum('ech,ehi->eci', xg, w_up)
        y = jnp.einsum('eci,eih->ech', jax.nn.silu(g) * u, w_down).reshape(E * C, H)
        out = jnp.zeros((T + 1, H), x.dtype).at[t_slot].add(w_slot[:, None] * y)
        return out[:T].reshape(B, S, H)
    x = _layernorm(x + _L0_attn_ref(x), axis=-1)
    x = _layernorm(x + _L0_xattn_ref(x, ctx_512, L0_xattn_Wq, L0_xattn_Wkv_expand, L0_xattn_Wout), axis=-1)
    x = _layernorm(x + _L0_ffn_ref(x, L0_ffn_gate_w, L0_ffn_w_gate, L0_ffn_w_up, L0_ffn_w_down), axis=-1)
    return x

_drawn_inputs = setup_inputs


def setup_inputs(seed=0):
    import zlib

    import numpy as np

    out = dict(_drawn_inputs(seed))
    spreads = {}
    factors = {'L0_xattn_Wq': 47.91}
    for name, (base, spread) in spreads.items():
        noise = np.random.default_rng([zlib.crc32(name.encode()), seed]).standard_normal(out[name].shape)
        drawn = base * np.exp(spread * noise) if base else spread * noise
        out[name] = jnp.asarray(drawn.astype(out[name].dtype))
    for name, factor in factors.items():
        out[name] = (out[name] * factor).astype(out[name].dtype)
    return out
```

```python
from contextlib import ExitStack

import concourse.bass as bass
from concourse import mybir

F32 = mybir.dt.float32
BF16 = mybir.dt.bfloat16
I32 = mybir.dt.int32
ALU = mybir.AluOpType
ACT = mybir.ActivationFunctionType
AX_X = mybir.AxisListType.X

P = 128
NB, D = 16, 256
NH, HD = 16, 16
SEG, DIL = 64, 2
GR = SEG // DIL
NG = P // GR
PAIRS = D // 32
LAT = 64
NE, INTER, TOPK = 32, 96, 8
CAP = 2 * (NB * P * TOPK // NE)
XW = D + NE
PARTS = 2
PB = NB // PARTS
PT_TOK = PB * P
QT = min(CAP, PT_TOK) // P
STRIDE = (QT + 1) * P
MAXB = PT_TOK * TOPK // P + NE
UN = 4
AHEAD = 3
TAB = MAXB + 2 * UN
IDLE = 10
XG_ROWS = NE * STRIDE + IDLE * P
Y_ROWS = (MAXB + 2) * P
Y_ZERO = (MAXB + 1) * P
FAR = 65536.0
EPS = 1e-5
LOW = -87.3
N_CONST = 45
MAGIC = 1597463007.0

assert MAXB % UN == 0 and PB % 2 == 0


class Steps:

    def __init__(self, sem, names):
        self.sem, self.names = sem, names.split()

    def at(self, tile, name):
        return len(self.names) * tile + self.names.index(name) + 1


def there(tile):
    return not isinstance(tile, int) or tile >= 0


LN = "stats aggr veps shift seed n1 n2 n3 c1 c2 c3 c4 norm"


def first_token(g):
    return SEG * (g // DIL) + g % DIL


def build(nc, x, ctx_in, wq, wkv, wout, gate_w, w_gate, w_up, w_down, out):
    stack = ExitStack()
    with stack:
        def sb(name, shape, dt=F32):
            return stack.enter_context(nc.sbuf_tensor(name, shape, dt))

        def sem(name):
            return stack.enter_context(nc.semaphore(name))

        xg = [nc.dram_tensor(f"queues{h}", (XG_ROWS, XW), F32).ap() for h in range(PARTS)]
        yg = [nc.dram_tensor(f"results{h}", (Y_ROWS, D), F32).ap() for h in range(PARTS)]

        bank = [stack.enter_context(nc.psum_tensor(f"bank{i}", [P, 512], F32)) for i in range(8)]
        pA, pC, pX, pO, pW = bank[0], bank[1], bank[2], bank[3], bank[4]
        pS = [bank[5], bank[6]]
        pT = bank[7]

        xs = sb("xs", [P, NB, D])
        x1 = sb("x1", [P, 2, D])
        x2 = sb("x2", [P, 2, XW])
        ct = sb("ct", [P, 2, P])
        cs = sb("cs", [P, NB, LAT])
        wgu = sb("wgu", [P, NE * 2 * 2 * INTER])
        wd = sb("wd", [INTER, NE * D])
        gw = sb("gw", [P, 2, NE])
        wqT = sb("wqT", [P, 2, D])
        woT = sb("woT", [P, 2, D])
        wkvT = sb("wkvT", [LAT, 2 * D])
        ident = sb("ident", [P, P])
        identb = sb("identb", [P, P], BF16)
        causal = sb("causal", [P, P], BF16)
        before = sb("before", [P, P], BF16)
        onesb = sb("onesb", [P, P], BF16)
        ones32 = sb("ones32", [P, NE])
        own = sb("own", [P, D])
        hmask = sb("hmask", [P, 8])
        rmask = sb("rmask", [P, 4])
        rank_i = sb("rank_i", [P, TOPK * NE], I32)
        rankc = sb("rankc", [P, TOPK, NE])
        eoff_i = sb("eoff_i", [P, NE], I32)
        eoff = sb("eoff", [P, NE])
        zrow_i = sb("zrow_i", [P, 1], I32)
        zrow = sb("zrow", [P, 1])
        blk_i = sb("blk_i", [NE, TAB], I32)
        blk = sb("blk", [NE, TAB])
        thr_i = sb("thr_i", [NE, QT], I32)
        thr = sb("thr", [NE, QT])
        upto = sb("upto", [NE, NE], BF16)
        under = sb("under", [NE, NE], BF16)
        zeros = sb("zeros", [P, XW])
        gm = sb("gm", [P, 2, D])
        gT = sb("gT", [P, 2, P])
        gX = sb("gX", [P, 2, 4, P])
        sA = sb("sA", [P, PAIRS, GR])
        eA = sb("eA", [P, PAIRS, GR])
        eAT = sb("eAT", [P, PAIRS, GR])
        oA = sb("oA", [P, D])
        mA = sb("mA", [P, PAIRS])
        dA = sb("dA", [P, PAIRS])
        rA = sb("rA", [P, PAIRS])
        cT = sb("cT", [LAT, P])
        kT = sb("kT", [P, 2, P])
        kX = sb("kX", [P, 2, 2, 8, P])
        vX = sb("vX", [P, 2, PAIRS, 4, HD])
        x1T = sb("x1T", [P, 2, P])
        qT = sb("qT", [P, 2, P])
        nmax = sb("nmax", [P, NH])
        den = sb("den", [P, NH])
        rden = sb("rden", [P, NH])
        pr = sb("pr", [P, 2, 4, P])
        prT = sb("prT", [P, 2, 4, P])
        rX = sb("rX", [P, NH, HD])
        rT = sb("rT", [P, 2, P])
        oT = sb("oT", [P, 2, P])
        yB = sb("yB", [P, D])
        x2T = sb("x2T", [P, 2, P])
        top = sb("top", [P, 1])
        lc = sb("lc", [P, NE])
        m8 = sb("m8", [P, TOPK])
        lr = sb("lr", [P, NE])
        pick = sb("pick", [P, NE])
        pickb = sb("pickb", [P, NE], BF16)
        seen = sb("seen", [P, NE], BF16)
        er = sb("er", [P, NE])
        rk = sb("rk", [P, NE])
        ew = sb("ew", [P, NE])
        es = sb("es", [P, 1])
        ri = sb("ri", [P, 1])
        posg = sb("posg", [P, NE])
        fits = sb("fits", [P, NE])
        earlier = sb("earlier", [P, NE])
        slot = sb("slot", [P, NB, NE])
        rank = sb("rank", [P, NB, NE])
        eq = sb("eq", [P, TOPK, NE])
        eqs = sb("eqs", [P, TOPK, NE])
        idf = sb("idf", [P, TOPK])
        xidx = sb("xidx", [P, 2, TOPK], I32)
        yidx = sb("yidx", [P, NB, TOPK], I32)
        slz = sb("slz", [P, NE])
        scrap = sb("scrap", [1, 3 + 2 * UN])
        st6 = sb("st6", [P, 6])
        mv = sb("mv", [P, 2])
        ve = sb("ve", [P, 1])
        half = sb("half", [P, 1], I32)
        ry = sb("ry", [P, 1])
        rt = sb("rt", [P, 1])
        rp = sb("rp", [P, 1])
        gone = sb("gone", [NE, 1])
        room = sb("room", [NE, 1])
        took = sb("took", [NE, 1])
        nblk = sb("nblk", [NE, 1])
        nblkb = sb("nblkb", [NE, 1], BF16)
        skipb = sb("skipb", [NE, 1], BF16)
        nund = sb("nund", [NE, NE], BF16)
        junk = sb("junk", [NE, QT])
        cum = sb("cum", [NE, 1])
        past = sb("past", [NE, TAB], BF16)
        tjunk = sb("tjunk", [1, MAXB // UN])
        rnds = sb("rnds", [1, 1])
        tab_e = sb("tab_e", [1, PARTS, TAB], I32)
        tab_x = sb("tab_x", [1, PARTS, TAB], I32)
        tab_p = sb("tab_p", [1, PARTS, NE], I32)
        tab_n = sb("tab_n", [1, PARTS], I32)
        tab_t = sb("tab_t", [1, PARTS], I32)
        tabf = sb("tabf", [1, TAB])
        shift_y = sb("shift_y", [P, PARTS, NE])
        xt = sb("xt", [P, UN, XW])
        xtT = sb("xtT", [P, 2, 2, P])
        th = sb("th", [P, 2, INTER])
        tg = sb("tg", [P, 2, INTER])
        hg = sb("hg", [P, 2, INTER])
        hT = sb("hT", [INTER, 2, P])
        wcol = sb("wcol", [P, UN])
        ys = sb("ys", [P, UN, D])
        fin = sb("fin", [P, 2, D])

        x_in = [sem("x_in0"), sem("x_in1")]
        ctx_loaded = sem("ctx_loaded")
        small_loaded = sem("small_loaded")
        experts_loaded = sem("experts_loaded")
        consts = sem("consts")
        wt_ps, wt_sb = sem("wt_ps"), sem("wt_sb")
        peA = Steps(sem("peA"), "gT cT s kv o")
        actA = Steps(sem("actA"), "gT cT e kT v")
        dveA = Steps(sem("dveA"), "max sub sum inv turn scale add " + LN)
        poolA = Steps(sem("poolA"), "gm ct gX kX")
        kept = sem("kept")
        peB = Steps(sem("peB"), "x1T q S0 S1 T0 S2 T1 V0 S3 T2 V1 T3 V2 V3 rT y")
        actB = Steps(sem("actB"), "x1T q e0 e1 T0 e2 e3 T2 rT")
        dveB = Steps(sem("dveB"), "m0 m1 m2 T1 m3 T3 inv rX oT add " + LN)
        peR = Steps(sem("peR"), "x2T lg pos")
        actR = Steps(sem("actR"), "x2T e")
        dveR = Steps(sem("dveR"), "top clamp m8 mr pick pickb rk rk2 ew ri slot posg fits rank w seen eq eqs sum idx")
        peH = Steps(sem("peH"), "count place table")
        dveH = Steps(sem("dveH"), "room min took nblk nblkb skipb nund gone earlier reset cum past sh tp n n2 tt te tx")
        peF = [{n: sem(f"peF{h}_{n}") for n in ("xT", "gu", "hT", "y")} for h in range(PARTS)]
        actF = [{n: sem(f"actF{h}_{n}") for n in ("xT", "th")} for h in range(PARTS)]
        dveF = [{n: sem(f"dveF{h}_{n}") for n in ("w", "tg", "hg", "hT", "y")} for h in range(PARTS)]
        drained = sem("drained")
        dveY = Steps(sem("dveY"), "slz eq eqs sum idx")
        dveC = Steps(sem("dveC"), LN)
        scattered = [sem(f"scattered{k}") for k in range(2)]
        idle_zero = sem("idle_zero")
        pad_zero = [sem(f"pad_zero{h}") for h in range(PARTS)]
        tail_zero = [sem(f"tail_zero{h}") for h in range(PARTS)]
        results_in = [sem(f"results_in{h}") for h in range(PARTS)]
        xt_in = [[sem(f"xt_in{h}_{k}") for k in range(UN)] for h in range(PARTS)]
        y_out = [[sem(f"y_out{h}_{k}") for k in range(UN)] for h in range(PARTS)]
        added = [sem(f"added{b}") for b in range(NB)]
        stored = [sem(f"stored{k}") for k in range(2)]

        gate_v = w_gate.rearrange("e (p k) i -> p e (k i)", k=2)
        up_v = w_up.rearrange("e (p k) i -> p e (k i)", k=2)
        down_v = w_down.rearrange("e i d -> i e d")
        wgu_v = wgu[:, :].rearrange("p (e g k) -> p e g k", e=NE, g=2)

        block = stack.enter_context(nc.Block())

        def three_stages(eng, step, tables):
            def at(k, par):
                if isinstance(k, int):
                    step(*(t if 0 <= t < NB else None for t in (k, k - 1, k - 2)), par)
                else:
                    step(k, k - 1, k - 2, par)

            at(0, 0)
            at(1, 1)
            with eng.Fori(0, PB // 2) as i:
                at(2 * i + 2, 0)
                at(2 * i + 3, 1)
            tables(0)
            with eng.Fori(0, PB // 2 - 2) as i:
                at(2 * i + (PB + 2), 0)
                at(2 * i + (PB + 3), 1)
            for k in range(NB - 2, NB + 2):
                at(k, k % 2)
            tables(1)

        @block.sync
        def _(sp):
            def load_x(g, b0, b1, s):
                t0 = first_token(g)
                sp.dma_start(xs[GR * g:GR * (g + 1), b0:b1, :],
                             x[b0:b1, t0:t0 + DIL * (GR - 1) + 1:DIL, :].rearrange("b i d -> i b d")
                             ).then_inc(s, 16)

            for g in range(NG):
                load_x(g, 0, 2, x_in[0])
            sp.dma_start(cs[:, :, :], ctx_in.rearrange("b s l -> s b l")).then_inc(ctx_loaded, 16)
            for g in range(NG):
                load_x(g, 2, NB, x_in[1])
            sp.wait_ge(consts, 1)
            for h in range(PARTS):
                for k in range(IDLE):
                    r = NE * STRIDE + k * P
                    sp.dma_start(xg[h][r:r + P, :], zeros[:, :]).then_inc(idle_zero, 16)
            for e in range(0, NE, 8):
                sp.dma_start(wgu_v[:, e:e + 8, 0, :], gate_v[:, e:e + 8, :]).then_inc(experts_loaded, 16)
                sp.dma_start(wgu_v[:, e:e + 8, 1, :], up_v[:, e:e + 8, :]).then_inc(experts_loaded, 16)
                sp.dma_start(wd[:, e * D:(e + 8) * D].rearrange("i (e d) -> i e d", d=D),
                             down_v[:, e:e + 8, :]).then_inc(experts_loaded, 16)

            for h in range(PARTS):
                sp.wait_ge(dveH.sem, dveH.at(h, "tx"))
                with sp.Fori(0, NE) as e:
                    r = sp.value_load(tab_p[0:1, h, bass.ds(e, 1)], min_val=0, max_val=NE * STRIDE - P)
                    sp.dma_start(xg[h][bass.ds(r, P), :], zeros[:, :]).then_inc(pad_zero[h], 16)
                rounds = sp.value_load(tab_n[0:1, h:h + 1], min_val=1, max_val=MAXB // UN)
                with sp.Fori(rounds * UN, MAXB + 1) as t:
                    sp.dma_start(yg[h][bass.ds(t * P, P), :], zeros[:, 0:D]).then_inc(tail_zero[h], 16)
                for k in range(2):
                    sp.wait_ge(scattered[k], 16 * TOPK * PB // 2 * (h + 1))
                sp.wait_ge(pad_zero[h], 16 * NE)
                sp.wait_ge(idle_zero, 16 * IDLE * PARTS)

                def queue_row(t):
                    r = sp.value_load(tab_x[0:1, h, bass.ds(t, 1)], min_val=0, max_val=XG_ROWS // P - 1)
                    return sp.snap(r * P)

                def load_block(t, s):
                    sp.dma_start(xt[:, s, :], xg[h][bass.ds(queue_row(t), P), :]).then_inc(xt_in[h][s], 16)

                for t in range(UN + 2):
                    if t >= UN:
                        sp.wait_ge(peF[h]["xT"], t - UN + 1)
                        sp.wait_ge(dveF[h]["w"], t - UN + 1)
                    load_block(t, t % UN)
                with sp.Fori(0, rounds) as j:
                    for u in range(UN):
                        t = j * UN + u
                        s = (u + 2) % UN
                        row, done = queue_row(t + UN + 2), sp.snap(t * P)
                        turned, written = sp.snap(t + 3), sp.snap(t + 1)
                        sp.wait_ge(peF[h]["xT"], turned)
                        sp.wait_ge(dveF[h]["w"], turned)
                        sp.dma_start(xt[:, s, :], xg[h][bass.ds(row, P), :]).then_inc(xt_in[h][s], 16)
                        sp.wait_ge(dveF[h]["y"], written)
                        sp.dma_start(yg[h][bass.ds(done, P), :], ys[:, u, :]).then_inc(y_out[h][u], 16)
                sp.wait_ge(drained, h + 1)
                sp.dma_start(yg[h][Y_ZERO:Y_ZERO + P, :], zeros[:, 0:D]).then_inc(results_in[h], 16)

            for b in range(NB):
                sp.wait_ge(dveC.sem, dveC.at(b, "norm"))
                for g in range(NG):
                    t0 = first_token(g)
                    sp.dma_start(out[b, t0:t0 + DIL * (GR - 1) + 1:DIL, :],
                                 fin[GR * g:GR * (g + 1), b % 2, :]).then_inc(stored[b % 2], 16)
            for k in range(2):
                sp.wait_ge(stored[k], 16 * NG * NB // 2)

        @block.gpsimd
        def _(pool):
            n = 0

            def put(op, *args, **kw):
                nonlocal n
                if n:
                    pool.wait_ge(consts, n)
                op(*args, **kw).then_inc(consts, 1)
                n += 1

            put(pool.memset, zeros[:, :], 0.0)
            put(pool.memset, own[:, :], 0.0)
            put(pool.memset, ct[:, :, :], 0.0)
            put(pool.memset, ident[:, :], 0.0)
            put(pool.memset, rmask[:, :], 0.0)
            put(pool.memset, causal[:, :], 0.0)
            put(pool.memset, onesb[:, :], 1.0)
            put(pool.memset, ones32[:, :], 1.0)
            put(pool.memset, hmask[:, :], 1.0)
            put(pool.memset, vX[:, :, :, :, :], 0.0)
            put(pool.memset, earlier[:, :], 0.0)
            put(pool.memset, gone[:, :], 0.0)
            put(pool.memset, seen[:, :], 0.0)
            for m in (ident,):
                put(pool.affine_select, out=m[:, :], in_=m[:, :], compare_op=ALU.not_equal, fill=1.0,
                                       base=0, pattern=[[-1, P]], channel_multiplier=1)
            own_v = own[:, :].rearrange("p (j s c) -> p j s c", s=DIL, c=HD)
            for g in range(NG):
                rows = slice(GR * g, GR * (g + 1))
                put(pool.memset, own_v[rows, :, g % DIL, :], 1.0)
                put(pool.memset, rmask[rows, g:g + 1], 1.0)
                put(pool.affine_select, out=causal[rows, :], in_=causal[rows, :], compare_op=ALU.is_ge,
                                       fill=-3e38, base=first_token(g), pattern=[[-1, P]],
                                       channel_multiplier=DIL)
                put(pool.affine_select, out=before[rows, :].rearrange("p (a b i) -> p a b i", a=2, b=2),
                                       in_=onesb[rows, :].rearrange("p (a b i) -> p a b i", a=2, b=2),
                                       compare_op=ALU.is_gt, fill=0.0, base=-first_token(g),
                                       pattern=[[SEG, 2], [1, 2], [DIL, GR]], channel_multiplier=-DIL)
            put(pool.affine_select, out=hmask[:, :], in_=hmask[:, :], compare_op=ALU.is_ge, fill=0.0,
                                   base=0, pattern=[[-HD, 8]], channel_multiplier=1)
            put(pool.affine_select, out=upto[:, :], in_=onesb[0:NE, 0:NE], compare_op=ALU.is_ge, fill=0.0,
                                   base=0, pattern=[[1, NE]], channel_multiplier=-1)
            put(pool.affine_select, out=under[:, :], in_=onesb[0:NE, 0:NE], compare_op=ALU.is_gt, fill=0.0,
                                   base=0, pattern=[[1, NE]], channel_multiplier=-1)
            put(pool.iota, rank_i[:, :], [[1, TOPK], [0, NE]], base=1, channel_multiplier=0)
            put(pool.iota, eoff_i[:, :], [[STRIDE, NE]], base=0, channel_multiplier=0)
            put(pool.iota, zrow_i[:, :], [[0, 1]], base=Y_ZERO, channel_multiplier=1)
            put(pool.iota, blk_i[:, :], [[1, TAB]], base=0, channel_multiplier=0)
            put(pool.iota, thr_i[:, :], [[P, QT]], base=0, channel_multiplier=0)
            put(pool.affine_select, out=hmask[:, :], in_=hmask[:, :], compare_op=ALU.is_ge, fill=0.0,
                                   base=HD - 1, pattern=[[HD, 8]], channel_multiplier=-1)
            put(pool.tensor_copy, identb[:, :], ident[:, :])
            put(pool.tensor_copy, rankc[:, :, :].rearrange("p k e -> p (k e)"), rank_i[:, :])
            put(pool.tensor_copy, eoff[:, :], eoff_i[:, :])
            put(pool.tensor_copy, zrow[:, :], zrow_i[:, :])
            put(pool.tensor_copy, blk[:, :], blk_i[:, :])
            put(pool.tensor_copy, thr[:, :], thr_i[:, :])
            assert n == N_CONST, n

            def mask_x(a, par):
                if there(a - 2):
                    pool.wait_ge(peA.sem, peA.at(a - 2, "o"))
                pool.tensor_tensor(gm[:, par, :], xs[:, bass.ds(a, 1), :].rearrange("p a d -> p (a d)"),
                                   own[:, :], ALU.mult).then_inc(poolA.sem, 1)
                pool.tensor_copy(ct[:, par, 0:LAT], cs[:, bass.ds(a, 1), :].rearrange("p a d -> p (a d)")
                                 ).then_inc(poolA.sem, 1)

            def masked(q, dst, src, mask):
                if q == 0:
                    return pool.tensor_tensor(dst, src, mask.unsqueeze(2).to_broadcast([P, 2, P]), ALU.mult)
                return pool.tensor_scalar(dst, src, mask, None, ALU.mult)

            def step(a, b, r, par):
                if a is not None:
                    if isinstance(a, int) and a == 0:
                        pool.wait_ge(x_in[0], 16 * NG)
                        pool.wait_ge(ctx_loaded, 16)
                    if isinstance(a, int) and a == 1:
                        pool.wait_ge(x_in[1], 16 * NG)
                    mask_x(a, par)
                    pool.wait_ge(actA.sem, actA.at(a, "gT"))
                    if there(a - 1):
                        pool.wait_ge(peA.sem, peA.at(a - 1, "s"))
                    for q in range(4):
                        ins = masked(q, gX[:, :, q, :], gT[:, :, :], rmask[:, q:q + 1])
                    ins.then_inc(poolA.sem, 1)
                    pool.wait_ge(actA.sem, actA.at(a, "kT"))
                    if there(a - 2):
                        pool.wait_ge(peB.sem, peB.at(a - 2, "S3"))
                    for q in range(8):
                        ins = masked(q, kX[:, par, :, q, :], kT[:, :, :], hmask[:, q:q + 1])
                    ins.then_inc(poolA.sem, 1)
                if r is not None:
                    h = part[0]
                    pool.wait_ge(dveR.sem, dveR.at(r, "idx"))
                    pool.tensor_copy(xs[:, bass.ds(r, 1), :].rearrange("p r d -> p (r d)"), x2[:, par, 0:D]
                                     ).then_inc(kept, 1)
                    for k in range(TOPK):
                        pool.indirect_dma_start(
                            xg[h], bass.IndirectOffsetOnAxis(ap=xidx[:, par, k:k + 1], axis=0),
                            x2[:, par, :], None,
                            bounds_check=last_row, oob_is_err=False).then_inc(scattered[par], 16)

            part = [0]
            last_row = pool.to_reg(XG_ROWS - 1)

            def tables(h):
                part[0] = h + 1

            three_stages(pool, step, tables)

            for h in range(PARTS):
                pool.wait_ge(kept, (h + 1) * PB)
                pool.wait_ge(results_in[h], 16)
                for k in range(TOPK):
                    for b in range(h * PB, (h + 1) * PB):
                        if k == 0:
                            pool.wait_ge(dveY.sem, dveY.at(b, "idx"))
                        else:
                            pool.wait_ge(added[b], 16 * k)
                        pool.indirect_dma_start(
                            xs[:, b, :], None, yg[h],
                            bass.IndirectOffsetOnAxis(ap=yidx[:, b, k:k + 1], axis=0),
                            bounds_check=Y_ROWS - 1, oob_is_err=True, compute_op=ALU.add
                        ).then_inc(added[b], 16)

        @block.tensor
        def _(pe):
            pe.wait_ge(consts, N_CONST)
            pe.wait_ge(small_loaded, 16 * 4)
            for m in range(2):
                for kk in range(2):
                    pe.transpose(bank[4][:, (kk * 2 + m) * P:(kk * 2 + m + 1) * P],
                                 pr[:, 0, :, :].rearrange("p a b -> p (a b)")[:, m * D + kk * P:m * D + kk * P + P],
                                 ident[:, :])
                    ins = pe.transpose(bank[5][:, (kk * 2 + m) * P:(kk * 2 + m + 1) * P],
                                 pr[:, 1, :, :].rearrange("p a b -> p (a b)")[:, m * D + kk * P:m * D + kk * P + P],
                                 ident[:, :])
            for m in range(4):
                ins = pe.transpose(bank[6][0:LAT, m * P:(m + 1) * P],
                                   prT[:, 0, :, :].rearrange("p a b -> p (a b)")[:, m * LAT:(m + 1) * LAT],
                                   ident[:, :])
            ins.then_inc(wt_ps, 1)
            pe.wait_ge(wt_sb, 3)

            def scores(b, g, par):
                m = g // 2
                pe.matmul(pS[g % 2][:, :], identb[:, :],
                          causal[:, :].unsqueeze(1).to_broadcast([P, 4, P]),
                          start=True, stop=False)
                pe.matmul(pS[g % 2][:, :], qT[:, m, :],
                          kX[:, par, m, 4 * (g % 2):4 * (g % 2) + 4, :],
                          start=False, stop=True).then_inc(peB.sem, 1)

            def turn_probs(b, g, before_it):
                pe.wait_ge(actB.sem, actB.at(b, f"e{g}"))
                if before_it is not None:
                    pe.wait_ge(*before_it)
                for q in range(4):
                    ins = pe.transpose(pT[:, q * P:(q + 1) * P], pr[:, g % 2, q, :], ident[:, :])
                ins.then_inc(peB.sem, 1)

            def values(b, g, par, ready):
                pe.wait_ge(*ready)
                for q in range(4):
                    hd = 4 * g + q
                    j, s = hd // 2, hd % 2
                    ins = pe.matmul(pO[32 * (j % 4):32 * (j % 4) + 32, (j // 4) * P:(j // 4) * P + P],
                                    vX[:, par, j, 2 * s:2 * s + 2, :].rearrange("p a c -> p (a c)"),
                                    prT[:, g % 2, q, :], start=(s == 0), stop=(s == 1),
                                    tile_position=(0, 32 * (j % 4)))
                ins.then_inc(peB.sem, 1)

            def step(a, b, r, par):
                pb = 1 - par
                if b is not None:
                    pe.wait_ge(dveA.sem, dveA.at(b, "norm"))
                    for kk in range(2):
                        ins = pe.transpose(pX[:, kk * P:(kk + 1) * P],
                                           x1[:, pb, kk * P:(kk + 1) * P], ident[:, :])
                    ins.then_inc(peB.sem, 1)
                if a is not None:
                    pe.wait_ge(poolA.sem, poolA.at(a, "gm"))
                    if there(a - 1):
                        pe.wait_ge(dveA.sem, dveA.at(a - 1, "scale"))
                    for kk in range(2):
                        ins = pe.transpose(pA[:, kk * P:(kk + 1) * P], gm[:, par, kk * P:(kk + 1) * P], ident[:, :])
                    ins.then_inc(peA.sem, 1)
                    if there(a - 1):
                        pe.wait_ge(actA.sem, actA.at(a - 1, "v"))
                    pe.wait_ge(poolA.sem, poolA.at(a, "ct"))
                    pe.transpose(pC[:, 0:P], ct[:, par, :], ident[:, :]).then_inc(peA.sem, 1)
                if b is not None:
                    pe.wait_ge(actB.sem, actB.at(b, "x1T"))
                    for m in range(2):
                        for kk in range(2):
                            ins = pe.matmul(pX[:, m * P:(m + 1) * P], wqT[:, kk, m * P:(m + 1) * P],
                                            x1T[:, kk, :], start=(kk == 0), stop=(kk == 1))
                    ins.then_inc(peB.sem, 1)
                if r is not None:
                    pe.wait_ge(dveB.sem, dveB.at(r, "norm"))
                    if b is not None:
                        pe.wait_ge(actB.sem, actB.at(b, "q"))
                    else:
                        pe.wait_ge(dveR.sem, dveR.at(r - 1, "posg"))
                    for kk in range(2):
                        ins = pe.transpose(pX[:, kk * P:(kk + 1) * P], x2[:, par, kk * P:(kk + 1) * P], ident[:, :])
                    ins.then_inc(peR.sem, 1)
                if a is not None:
                    pe.wait_ge(actA.sem, actA.at(a, "gT"))
                    pe.wait_ge(poolA.sem, poolA.at(a, "gX"))
                    for g in range(NG):
                        for m in range(2):
                            ins = pe.matmul(pA[GR * g:GR * (g + 1), D + m * P:D + (m + 1) * P],
                                            gT[:, m, GR * g:GR * (g + 1)],
                                            gX[:, m, :, GR * g:GR * (g + 1)],
                                            start=True, stop=True, tile_position=(0, GR * g))
                    ins.then_inc(peA.sem, 1)
                if b is not None:
                    pe.wait_ge(actB.sem, actB.at(b, "q"))
                    pe.wait_ge(poolA.sem, poolA.at(b, "kX"))
                    scores(b, 0, pb)
                    scores(b, 1, pb)
                if a is not None:
                    pe.wait_ge(actA.sem, actA.at(a, "cT"))
                    for m in range(2):
                        pe.matmul(pC[:, m * P:(m + 1) * P], wkvT[:, m * P:(m + 1) * P], cT[:, :],
                                  start=True, stop=True)
                    pe.matmul(pC[:, D:2 * D], cT[:, :], wkvT[:, D:2 * D], start=True, stop=True
                              ).then_inc(peA.sem, 1)
                if r is not None:
                    pe.wait_ge(actR.sem, actR.at(r, "x2T"))
                    for kk in range(2):
                        ins = pe.matmul(pX[:, D:D + NE], x2T[:, kk, :], gw[:, kk, :],
                                        start=(kk == 0), stop=(kk == 1))
                    ins.then_inc(peR.sem, 1)
                if b is not None:
                    turn_probs(b, 0, None)
                    scores(b, 2, pb)
                if b is not None:
                    turn_probs(b, 1, (actB.sem, actB.at(b, "T0")))
                    if a is not None:
                        pe.wait_ge(dveA.sem, dveA.at(a, "turn"))
                    values(b, 0, pb, (actB.sem, actB.at(b, "T0")))
                if a is not None:
                    if b is None:
                        pe.wait_ge(dveA.sem, dveA.at(a, "turn"))
                    for j in range(PAIRS):
                        for g in range(NG):
                            ins = pe.matmul(pA[GR * g:GR * (g + 1), j * 32:(j + 1) * 32],
                                            eAT[GR * g:GR * (g + 1), j, :],
                                            gm[GR * g:GR * (g + 1), par, j * 32:(j + 1) * 32],
                                            start=True, stop=True, tile_position=(GR * g, GR * g))
                    ins.then_inc(peA.sem, 1)
                if b is not None:
                    scores(b, 3, pb)
                if r is not None:
                    pe.wait_ge(dveR.sem, dveR.at(r, "pickb"))
                    pe.matmul(pX[:, D + 2 * NE:D + 3 * NE], before[:, :], pickb[:, :], start=True, stop=False)
                    pe.matmul(pX[:, D + 2 * NE:D + 3 * NE], onesb[:, :], seen[:, :], start=False, stop=True
                              ).then_inc(peR.sem, 1)
                if b is not None:
                    turn_probs(b, 2, (dveB.sem, dveB.at(b, "T1")))
                    values(b, 1, pb, (dveB.sem, dveB.at(b, "T1")))
                    turn_probs(b, 3, (actB.sem, actB.at(b, "T2")))
                    values(b, 2, pb, (actB.sem, actB.at(b, "T2")))
                    values(b, 3, pb, (dveB.sem, dveB.at(b, "T3")))
                    pe.wait_ge(dveB.sem, dveB.at(b, "rX"))
                    for m in range(2):
                        ins = pe.transpose(pO[:, D + m * P:D + (m + 1) * P],
                                           rX[:, 8 * m:8 * m + 8, :].rearrange("p h c -> p (h c)"), ident[:, :])
                    ins.then_inc(peB.sem, 1)
                    pe.wait_ge(dveB.sem, dveB.at(b, "oT"))
                    for kk in range(2):
                        ins = pe.matmul(pW[:, 0:D], oT[:, kk, :], woT[:, kk, :], start=(kk == 0), stop=(kk == 1))
                    ins.then_inc(peB.sem, 1)

            def tables(h):
                pe.wait_ge(dveR.sem, dveR.at((h + 1) * PB - 1, "seen"))
                pe.wait_ge(dveB.sem, dveB.at(min((h + 1) * PB, NB - 1), "add"))
                pe.matmul(pW[:, 0:NE], onesb[:, :], seen[:, :], start=True, stop=True)
                pe.matmul(pW[0:NE, NE:NE + 1], seen[:, :], onesb[:, 0:1], start=True, stop=True
                          ).then_inc(peH.sem, 1)
                pe.wait_ge(dveH.sem, dveH.at(h, "earlier"))
                pe.matmul(pW[0:NE, NE + 1:NE + 2], upto[:, :], nblkb[:, :], start=True, stop=True)
                pe.matmul(pW[:, 64:64 + NE], onesb[0:NE, :], nund[:, :], start=True, stop=True)
                pe.matmul(pW[0:1, 96:96 + NE], took[:, :], ident[0:NE, 0:NE], start=True, stop=True)
                pe.matmul(pW[0:1, 130:131], nblkb[:, :], onesb[0:NE, 0:1], start=True, stop=True
                          ).then_inc(peH.sem, 1)
                pe.wait_ge(dveH.sem, dveH.at(h, "n"))
                pe.matmul(pW[0:1, 160:160 + TAB], onesb[0:NE, 0:1], past[:, :], start=True, stop=True)
                pe.matmul(pW[0:1, 300:300 + TAB], skipb[:, :], past[:, :], start=True, stop=True
                          ).then_inc(peH.sem, 1)
                pe.wait_ge(dveH.sem, dveH.at(h, "tx"))

            three_stages(pe, step, tables)

            pe.wait_ge(experts_loaded, 16 * 3 * (NE // 8))
            for h in range(PARTS):
                rounds = pe.value_load(tab_n[0:1, h:h + 1], min_val=1, max_val=MAXB // UN)

                def expert(t):
                    return pe.value_load(tab_e[0:1, h, bass.ds(t, 1)], min_val=0, max_val=NE - 1)

                def xT(t, u, j):
                    s = u % UN
                    pe.wait_ge(xt_in[h][s], 16 * (j + (u // UN + 1)))
                    if there(t - 2):
                        pe.wait_ge(actF[h]["xT"], t - 1)
                    for kk in range(2):
                        ins = pe.transpose(bank[u % 2][:, kk * P:(kk + 1) * P],
                                           xt[:, s, kk:D:2], ident[:, :])
                    ins.then_inc(peF[h]["xT"], 1)

                def gu(t, u):
                    e = pe.snap(expert(t) * (4 * INTER))
                    pe.wait_ge(actF[h]["xT"], t + 1)
                    if there(t - 2):
                        pe.wait_ge(dveF[h]["hg"], t - 1)
                    for kk in range(2):
                        ins = pe.matmul(bank[2 + u % 2][:, 0:2 * INTER].rearrange("p (g i) -> p g i", g=2),
                                        xtT[:, u % 2, kk, :],
                                        wgu[:, bass.ds(e, 4 * INTER)].rearrange(
                                            "p (g k i) -> p g k i", g=2, k=2)[:, :, kk, :],
                                        start=(kk == 0), stop=(kk == 1))
                    ins.then_inc(peF[h]["gu"], 1)

                def turn_h(t, u):
                    pe.wait_ge(dveF[h]["hg"], t + 1)
                    if there(t - 2):
                        pe.wait_ge(dveF[h]["hT"], t - 1)
                    pe.transpose(bank[4 + u % 2][0:INTER, 0:P], hg[:, u % 2, :], ident[:, :]
                                 ).then_inc(peF[h]["hT"], 1)

                def down(t, u):
                    e = pe.snap(expert(t) * D)
                    pe.wait_ge(dveF[h]["hT"], t + 1)
                    pe.matmul(bank[6 + u % 2][:, 0:D], hT[:, u % 2, :], wd[:, bass.ds(e, D)],
                              start=True, stop=True).then_inc(peF[h]["y"], 1)

                for t in range(3):
                    xT(t, t, 0)
                for t in range(2):
                    gu(t, t)
                turn_h(0, 0)
                with pe.Fori(0, rounds) as j:
                    for u in range(UN):
                        t = j * UN + u
                        xT(t + 3, u + 3, j)
                        gu(t + 2, u)
                        turn_h(t + 1, u + 1)
                        down(t, u)

        @block.scalar
        def _(act):
            act.dma_start(pr[:, 0, :, :].rearrange("p a b -> p (a b)").rearrange("p (m d) -> p m d", m=2),
                          wq.rearrange("(m p) d -> p m d", p=P)).then_inc(small_loaded, 16)
            act.dma_start(pr[:, 1, :, :].rearrange("p a b -> p (a b)").rearrange("p (m d) -> p m d", m=2),
                          wout.rearrange("(m p) d -> p m d", p=P)).then_inc(small_loaded, 16)
            act.dma_start(prT[:, 0, 0:2, :].rearrange("p a b -> p (a b)").rearrange("p (m l) -> p m l", m=4),
                          wkv.rearrange("(m p) l -> p m l", p=P)).then_inc(small_loaded, 16)
            act.dma_start(gw[:, :, :], gate_w.rearrange("(k p) e -> p k e", p=P)).then_inc(small_loaded, 16)
            act.wait_ge(wt_ps, 1)
            act.copy(wqT[:, :, :].rearrange("p a b -> p (a b)"), bank[4][:, :]).then_inc(wt_sb, 1)
            act.copy(woT[:, :, :].rearrange("p a b -> p (a b)"), bank[5][:, :]).then_inc(wt_sb, 1)
            act.copy(wkvT[:, :], bank[6][0:LAT, :]).then_inc(wt_sb, 1)

            def exps(b, g):
                act.wait_ge(dveB.sem, dveB.at(b, f"m{g}"))
                for q in range(4):
                    hd = 4 * g + q
                    ins = act.activation(pr[:, g % 2, q, :], pS[g % 2][:, q * P:(q + 1) * P], ACT.Exp,
                                         bias=nmax[:, hd:hd + 1], accum_out=den[:, hd:hd + 1])
                ins.then_inc(actB.sem, 1)

            def probs_T(b, g):
                act.wait_ge(peB.sem, peB.at(b, f"T{g}"))
                act.copy(prT[:, g % 2, :, :].rearrange("p a b -> p (a b)"), pT[:, :]).then_inc(actB.sem, 1)

            def flat2(t):
                return t[:, :, :].rearrange("p a b -> p (a b)")

            def step(a, b, r, par):
                if b is not None:
                    act.wait_ge(peB.sem, peB.at(b, "x1T"))
                    act.copy(flat2(x1T), pX[:, 0:D]).then_inc(actB.sem, 1)
                if a is not None:
                    act.wait_ge(peA.sem, peA.at(a, "gT"))
                    act.copy(flat2(gT), pA[:, 0:D]).then_inc(actA.sem, 1)
                    act.wait_ge(peA.sem, peA.at(a, "cT"))
                    act.copy(cT[:, :], pC[0:LAT, 0:P]).then_inc(actA.sem, 1)
                if b is not None:
                    act.wait_ge(peB.sem, peB.at(b, "q"))
                    act.mul(flat2(qT), pX[:, 0:D], float(HD) ** -0.5).then_inc(actB.sem, 1)
                if r is not None:
                    act.wait_ge(peR.sem, peR.at(r, "x2T"))
                    act.copy(flat2(x2T), pX[:, 0:D]).then_inc(actR.sem, 1)
                if a is not None:
                    act.wait_ge(dveA.sem, dveA.at(a, "sub"))
                    act.activation(flat2(eA), flat2(sA), ACT.Exp, scale=float(HD) ** -0.5).then_inc(actA.sem, 1)
                if b is not None:
                    exps(b, 0)
                    exps(b, 1)
                if a is not None:
                    act.wait_ge(peA.sem, peA.at(a, "kv"))
                    if there(a - 1):
                        act.wait_ge(poolA.sem, poolA.at(a - 1, "kX"))
                    act.copy(flat2(kT), pC[:, 0:D]).then_inc(actA.sem, 1)
                    act.copy(vX[:, par, :, 0:4:3, :],
                             pC[:, D:2 * D].rearrange("p (j s c) -> p j s c", s=2, c=HD)).then_inc(actA.sem, 1)
                if r is not None:
                    act.wait_ge(dveR.sem, dveR.at(r, "clamp"))
                    act.activation(er[:, :], lc[:, :], ACT.Exp).then_inc(actR.sem, 1)
                if b is not None:
                    probs_T(b, 0)
                    exps(b, 2)
                    exps(b, 3)
                    probs_T(b, 2)
                    act.wait_ge(peB.sem, peB.at(b, "rT"))
                    act.copy(flat2(rT), pO[:, D:2 * D]).then_inc(actB.sem, 1)

            three_stages(act, step, lambda h: None)

            for h in range(PARTS):
                if h == 0:
                    act.wait_ge(dveH.sem, dveH.at(PARTS - 1, "tx"))
                rounds = act.value_load(tab_n[0:1, h:h + 1], min_val=1, max_val=MAXB // UN)

                def xT(t, u):
                    act.wait_ge(peF[h]["xT"], t + 1)
                    if there(t - 2):
                        act.wait_ge(peF[h]["gu"], t - 1)
                    act.copy(xtT[:, u % 2, :, :].rearrange("p a b -> p (a b)"), bank[u % 2][:, 0:D]
                             ).then_inc(actF[h]["xT"], 1)

                def tanh(t, u):
                    act.wait_ge(peF[h]["gu"], t + 1)
                    if there(t - 2):
                        act.wait_ge(dveF[h]["tg"], t - 1)
                    act.activation(th[:, u % 2, :], bank[2 + u % 2][:, 0:INTER], ACT.Tanh, scale=0.5
                                   ).then_inc(actF[h]["th"], 1)

                for t in range(3):
                    xT(t, t)
                for t in range(2):
                    tanh(t, t)
                with act.Fori(0, rounds) as j:
                    for u in range(UN):
                        t = j * UN + u
                        xT(t + 3, u + 3)
                        tanh(t + 2, u)

        @block.vector
        def _(dve):
            dve.wait_ge(consts, N_CONST)

            def hold(k=0):
                return dve.memset(scrap[0:1, k:k + 1], 0.0)

            def norm(steps, t, src, dst, free=None):
                s = steps.sem

                def then(ins):
                    ins.then_inc(s, 1)

                then(dve.bn_stats(st6[:, :], src))
                dve.wait_ge(s, steps.at(t, "stats"))
                hold()
                then(dve.bn_aggr(mv[:, :], st6[:, :]))
                dve.wait_ge(s, steps.at(t, "aggr"))
                then(dve.tensor_scalar(ve[:, :], mv[:, 1:2], EPS, None, ALU.add))
                dve.wait_ge(s, steps.at(t, "veps"))
                then(dve.tensor_scalar(half[:, :], ve[:, :].bitcast(I32), 1, None, ALU.arith_shift_right))
                dve.wait_ge(s, steps.at(t, "shift"))
                then(dve.tensor_scalar(ry[:, :].bitcast(I32), half[:, :], -1.0, MAGIC, ALU.mult, ALU.add))
                dve.wait_ge(s, steps.at(t, "seed"))
                then(dve.scalar_tensor_tensor(rt[:, :], ry[:, :], ve[:, 0:1], ry[:, :], ALU.mult, ALU.mult))
                dve.wait_ge(s, steps.at(t, "n1"))
                then(dve.tensor_scalar(rt[:, :], rt[:, :], -0.5, 1.5, ALU.mult, ALU.add))
                dve.wait_ge(s, steps.at(t, "n2"))
                then(dve.tensor_tensor(ry[:, :], ry[:, :], rt[:, :], ALU.mult))
                dve.wait_ge(s, steps.at(t, "n3"))
                then(dve.scalar_tensor_tensor(rt[:, :], ry[:, :], ve[:, 0:1], ry[:, :], ALU.mult, ALU.mult))
                dve.wait_ge(s, steps.at(t, "c1"))
                then(dve.tensor_scalar(rp[:, :], rt[:, :], 0.375, -1.25, ALU.mult, ALU.add))
                dve.wait_ge(s, steps.at(t, "c2"))
                then(dve.tensor_tensor(rt[:, :], rt[:, :], rp[:, :], ALU.mult))
                dve.wait_ge(s, steps.at(t, "c3"))
                then(dve.scalar_tensor_tensor(ry[:, :], rt[:, :], 1.875, ry[:, :], ALU.add, ALU.mult))
                dve.wait_ge(s, steps.at(t, "c4"))
                if free:
                    free()
                then(dve.tensor_scalar(dst, src, mv[:, 0:1], ry[:, 0:1], ALU.subtract, ALU.mult))

            def xrow(t):
                return xs[:, bass.ds(t, 1), 0:D].rearrange("p t d -> p (t d)")

            def flat2(t):
                return t[:, :, :].rearrange("p a b -> p (a b)")

            def maxes(b, g):
                dve.wait_ge(peB.sem, peB.at(b, f"S{g}"))
                dve.tensor_reduce(nmax[:, 4 * g:4 * g + 4],
                                  pS[g % 2][:, :].rearrange("p (h k) -> p h k", h=4),
                                  AX_X, ALU.max, negate=True).then_inc(dveB.sem, 1)

            def probs_T(b, g):
                dve.wait_ge(peB.sem, peB.at(b, f"T{g}"))
                dve.tensor_copy(prT[:, g % 2, :, :].rearrange("p a b -> p (a b)"), pT[:, :]).then_inc(dveB.sem, 1)

            def step(a, b, r, par):
                if a is not None:
                    A, s = (lambda name: dveA.at(a, name)), dveA.sem
                    dve.wait_ge(peA.sem, peA.at(a, "s"))
                    scr = pA[:, D:2 * D].rearrange("p (j k) -> p j k", j=PAIRS)
                    dve.tensor_reduce(mA[:, :], scr, AX_X, ALU.max).then_inc(s, 1)
                    dve.wait_ge(s, A("max"))
                    dve.tensor_tensor(sA[:, :, :], scr, mA[:, :].unsqueeze(2).to_broadcast([P, PAIRS, GR]),
                                      ALU.subtract).then_inc(s, 1)
                if b is not None:
                    maxes(b, 0)
                    maxes(b, 1)
                if a is not None:
                    dve.wait_ge(actA.sem, actA.at(a, "e"))
                    dve.tensor_reduce(dA[:, :], eA[:, :, :], AX_X, ALU.add).then_inc(s, 1)
                    dve.wait_ge(s, A("sum"))
                    dve.reciprocal(rA[:, :], dA[:, :]).then_inc(s, 1)
                    dve.transpose(flat2(eAT), flat2(eA)).then_inc(s, 1)
                if r is not None:
                    R, t = (lambda name: dveR.at(r, name)), dveR.sem
                    dve.wait_ge(peR.sem, peR.at(r, "lg"))
                    lg = pX[:, D:D + NE]
                    dve.tensor_reduce(top[:, :], lg, AX_X, ALU.max).then_inc(t, 1)
                    dve.wait_ge(t, R("top"))
                    dve.tensor_scalar(lc[:, :], lg, top[:, 0:1], LOW, ALU.subtract, ALU.max).then_inc(t, 1)
                    dve.wait_ge(t, R("clamp"))
                    hold()
                    dve.max(m8[:, :], lc[:, :]).then_inc(t, 1)
                    dve.wait_ge(t, R("m8"))
                    hold()
                    dve.match_replace(lr[:, :], m8[:, :], lc[:, :], 1.0).then_inc(t, 1)
                    dve.wait_ge(t, R("mr"))
                    dve.tensor_scalar(pick[:, :], lr[:, :], 0.5, None, ALU.is_gt).then_inc(t, 1)
                    dve.tensor_scalar(pickb[:, :], lr[:, :], 0.5, None, ALU.is_gt).then_inc(t, 1)
                    dve.wait_ge(t, R("pick"))
                    dve.tensor_tensor_scan(rk[:, :], ones32[:, :], pick[:, :], 0.0, ALU.mult, ALU.add).then_inc(t, 1)
                    dve.wait_ge(t, R("rk"))
                    dve.tensor_tensor(rk[:, :], rk[:, :], pick[:, :], ALU.mult).then_inc(t, 1)
                    dve.wait_ge(actR.sem, actR.at(r, "e"))
                    dve.scalar_tensor_tensor(ew[:, :], er[:, :], 1.0, pick[:, :], ALU.mult, ALU.mult,
                                             accum_out=es[:, :]).then_inc(t, 1)
                    dve.wait_ge(t, R("ew"))
                    dve.reciprocal(ri[:, :], es[:, :]).then_inc(t, 1)
                if b is not None:
                    maxes(b, 2)
                if a is not None:
                    dve.wait_ge(peA.sem, peA.at(a, "o"))
                    dve.tensor_tensor(oA[:, :].rearrange("p (j c) -> p j c", j=PAIRS),
                                      pA[:, 0:D].rearrange("p (j c) -> p j c", j=PAIRS),
                                      rA[:, :].unsqueeze(2).to_broadcast([P, PAIRS, 32]), ALU.mult).then_inc(s, 1)
                if b is not None:
                    probs_T(b, 1)
                    maxes(b, 3)
                if a is not None:
                    dve.wait_ge(s, A("scale"))
                    dve.tensor_tensor(oA[:, :], oA[:, :], xrow(a), ALU.add).then_inc(s, 1)
                    dve.wait_ge(s, A("add"))
                    norm(dveA, a, oA[:, :], x1[:, par, :])
                if r is not None:
                    dve.wait_ge(peR.sem, peR.at(r, "pos"))
                    pos = pX[:, D + 2 * NE:D + 3 * NE]
                    sl = slot[:, bass.ds(r, 1), :].rearrange("p r e -> p (r e)")
                    rr = rank[:, bass.ds(r, 1), :].rearrange("p r e -> p (r e)")
                    dve.tensor_tensor(sl, pos, eoff[:, :], ALU.add).then_inc(t, 1)
                    dve.tensor_tensor(posg[:, :], pos, earlier[:, :], ALU.add).then_inc(t, 1)
                if b is not None:
                    probs_T(b, 3)
                if r is not None:
                    dve.wait_ge(t, R("posg"))
                    dve.tensor_scalar(fits[:, :], posg[:, :], float(CAP), None, ALU.is_lt).then_inc(t, 1)
                    dve.wait_ge(t, R("fits"))
                    dve.tensor_tensor(rr, rk[:, :], fits[:, :], ALU.mult).then_inc(t, 1)
                    dve.scalar_tensor_tensor(x2[:, par, D:XW],
                                             ew[:, :], ri[:, 0:1], fits[:, :], ALU.mult, ALU.mult).then_inc(t, 1)
                    dve.tensor_tensor(seen[:, :], seen[:, :], pickb[:, :], ALU.add).then_inc(t, 1)
                    dve.wait_ge(t, R("rank"))
                    dve.tensor_tensor(eq[:, :, :], rr.unsqueeze(1).to_broadcast([P, TOPK, NE]), rankc[:, :, :],
                                      ALU.is_equal).then_inc(t, 1)
                    dve.wait_ge(t, R("eq"))
                    dve.scalar_tensor_tensor(eqs[:, :, :], sl.unsqueeze(1).to_broadcast([P, TOPK, NE]), -FAR,
                                             eq[:, :, :], ALU.add, ALU.mult).then_inc(t, 1)
                    dve.wait_ge(t, R("eqs"))
                    dve.tensor_reduce(idf[:, :], eqs[:, :, :], AX_X, ALU.add).then_inc(t, 1)
                    dve.wait_ge(t, R("sum"))
                    dve.tensor_scalar(xidx[:, par, :], idf[:, :], FAR, None, ALU.add).then_inc(t, 1)
                if b is not None:
                    B, v = (lambda name: dveB.at(b, name)), dveB.sem
                    dve.wait_ge(actB.sem, actB.at(b, "e3"))
                    dve.reciprocal(rden[:, :], den[:, :]).then_inc(v, 1)
                    dve.wait_ge(v, B("inv"))
                    dve.tensor_copy(rX[:, :, :], rden[:, :].unsqueeze(2).to_broadcast([P, NH, HD])).then_inc(v, 1)
                    dve.wait_ge(actB.sem, actB.at(b, "rT"))
                    dve.tensor_tensor(flat2(oT), pO[:, 0:D], flat2(rT), ALU.mult).then_inc(v, 1)
                    dve.wait_ge(peB.sem, peB.at(b, "y"))
                    dve.tensor_tensor(yB[:, :], pW[:, 0:D], x1[:, 1 - par, :], ALU.add).then_inc(v, 1)
                    dve.wait_ge(v, B("add"))
                    norm(dveB, b, yB[:, :], x2[:, 1 - par, 0:D],
                         lambda: (dve.wait_ge(scattered[1 - par], 16 * TOPK // 2 * (b - (1 - par))),
                                  dve.wait_ge(kept, b - 1) if there(b - 2) else None))

            def tables(h):
                H, s = (lambda name: dveH.at(h, name)), dveH.sem
                dve.wait_ge(peH.sem, peH.at(h, "count"))
                cnt = pW[0:NE, NE:NE + 1]
                dve.tensor_scalar(room[:, :], gone[:, :], -1.0, float(CAP), ALU.mult, ALU.add).then_inc(s, 1)
                dve.wait_ge(s, H("room"))
                dve.tensor_tensor(took[:, :], cnt, room[:, :], ALU.min).then_inc(s, 1)
                dve.wait_ge(s, H("min"))
                dve.tensor_scalar(took[:, :], took[:, :], 0.0, None, ALU.max).then_inc(s, 1)
                dve.wait_ge(s, H("took"))
                dve.tensor_scalar(junk[:, :], blk128(QT), took[:, 0:1], 0.0, ALU.is_lt, ALU.add,
                                  accum_out=nblk[:, :]).then_inc(s, 1)
                dve.wait_ge(s, H("nblk"))
                dve.tensor_copy(nblkb[:, :], nblk[:, :]).then_inc(s, 1)
                dve.tensor_scalar(skipb[:, :], nblk[:, :], -1.0, float(STRIDE // P), ALU.mult, ALU.add).then_inc(s, 1)
                dve.tensor_scalar(nund[:, :], under[:, :], nblk[:, 0:1], None, ALU.mult).then_inc(s, 1)
                dve.tensor_tensor(gone[:, :], gone[:, :], cnt, ALU.add).then_inc(s, 1)
                dve.tensor_tensor(earlier[:, :], earlier[:, :], pW[:, 0:NE], ALU.add).then_inc(s, 1)
                dve.memset(seen[:, :], 0.0).then_inc(s, 1)
                dve.wait_ge(peH.sem, peH.at(h, "place"))
                dve.tensor_copy(cum[:, :], pW[0:NE, NE + 1:NE + 2]).then_inc(s, 1)
                dve.wait_ge(s, H("cum"))
                dve.tensor_scalar(past[:, :], blk[:, :], cum[:, 0:1], None, ALU.is_ge).then_inc(s, 1)
                dve.scalar_tensor_tensor(shift_y[:, h, :], pW[:, 64:64 + NE], float(P), eoff[:, :],
                                         ALU.mult, ALU.subtract).then_inc(s, 1)
                dve.tensor_tensor(tab_p[0:1, h, :], pW[0:1, 96:96 + NE], eoff[0:1, :], ALU.add).then_inc(s, 1)
                dve.tensor_scalar(tjunk[:, :], blk4(), pW[0:1, 130:131], 0.0, ALU.is_lt, ALU.add,
                                  accum_out=rnds[:, :]).then_inc(s, 1)
                dve.wait_ge(s, H("n"))
                dve.tensor_scalar(tab_n[0:1, h:h + 1], rnds[:, :], 1.0, None, ALU.max).then_inc(s, 1)
                dve.wait_ge(s, H("n2"))
                dve.tensor_scalar(tab_t[0:1, h:h + 1], tab_n[0:1, h:h + 1], -16.0 * UN, 16.0 * (MAXB + 1),
                                  ALU.mult, ALU.add).then_inc(s, 1)
                dve.wait_ge(peH.sem, peH.at(h, "table"))
                dve.tensor_scalar(tab_e[0:1, h, :], pW[0:1, 160:160 + TAB], float(NE - 1), None, ALU.min
                                  ).then_inc(s, 1)
                dve.tensor_tensor(tab_x[0:1, h, :], pW[0:1, 300:300 + TAB], blk[0:1, :], ALU.add).then_inc(s, 1)

            def blk128(n):
                return thr[:, 0:n]

            def blk4():
                return blk[0:1, 0:MAXB:UN]

            three_stages(dve, step, tables)

            def result_rows(b, h):
                s = dveY.sem
                dve.scalar_tensor_tensor(slz[:, :], slot[:, b, :], zrow[:, 0:1], shift_y[:, h, :],
                                         ALU.subtract, ALU.add).then_inc(s, 1)
                dve.tensor_tensor(eq[:, :, :], rank[:, b, :].unsqueeze(1).to_broadcast([P, TOPK, NE]),
                                  rankc[:, :, :], ALU.is_equal).then_inc(s, 1)
                dve.wait_ge(s, dveY.at(b, "eq"))
                dve.tensor_tensor(eqs[:, :, :], slz[:, :].unsqueeze(1).to_broadcast([P, TOPK, NE]), eq[:, :, :],
                                  ALU.mult).then_inc(s, 1)
                dve.wait_ge(s, dveY.at(b, "eqs"))
                dve.tensor_reduce(idf[:, :], eqs[:, :, :], AX_X, ALU.add).then_inc(s, 1)
                dve.wait_ge(s, dveY.at(b, "sum"))
                dve.tensor_scalar(yidx[:, b, :], idf[:, :], zrow[:, 0:1], None, ALU.add).then_inc(s, 1)

            for h in range(PARTS):
                rounds = dve.value_load(tab_n[0:1, h:h + 1], min_val=1, max_val=MAXB // UN)
                tail = dve.value_load(tab_t[0:1, h:h + 1], min_val=16, max_val=16 * (MAXB + 1))

                def weights(t, u, j):
                    e = dve.value_load(tab_e[0:1, h, bass.ds(t, 1)], min_val=0, max_val=NE - 1)
                    if there(t - UN):
                        dve.wait_ge(dveF[h]["y"], t - UN + 1)
                    dve.wait_ge(xt_in[h][u % UN], 16 * (j + (u // UN + 1)))
                    dve.tensor_copy(wcol[:, u % UN:u % UN + 1], xt[:, u % UN, bass.ds(e + D, 1)]
                                    ).then_inc(dveF[h]["w"], 1)

                def gate(t, u):
                    if there(t - 2):
                        dve.wait_ge(peF[h]["hT"], t - 1)
                    dve.wait_ge(actF[h]["th"], t + 1)
                    ps = bank[2 + u % 2]
                    dve.scalar_tensor_tensor(tg[:, u % 2, :], th[:, u % 2, :], 1.0, ps[:, 0:INTER], ALU.add, ALU.mult
                                             ).then_inc(dveF[h]["tg"], 1)
                    dve.wait_ge(dveF[h]["tg"], t + 1)
                    dve.tensor_tensor(hg[:, u % 2, :], tg[:, u % 2, :], ps[:, INTER:2 * INTER], ALU.mult
                                      ).then_inc(dveF[h]["hg"], 1)

                def h_T(t, u):
                    dve.wait_ge(peF[h]["hT"], t + 1)
                    if there(t - 2):
                        dve.wait_ge(peF[h]["y"], t - 1)
                    dve.tensor_copy(hT[:, u % 2, :], bank[4 + u % 2][0:INTER, 0:P]).then_inc(dveF[h]["hT"], 1)

                def y(t, u, j):
                    dve.wait_ge(peF[h]["y"], t + 1)
                    dve.wait_ge(y_out[h][u], 16 * j)
                    dve.wait_ge(dveF[h]["w"], t + 1)
                    dve.tensor_scalar(ys[:, u, :], bank[6 + u % 2][:, 0:D], wcol[:, u:u + 1], 0.5,
                                      ALU.mult, ALU.mult).then_inc(dveF[h]["y"], 1)

                for t in range(3):
                    weights(t, t, 0)
                for t in range(2):
                    gate(t, t)
                h_T(0, 0)
                with dve.Fori(0, rounds) as j:
                    for u in range(UN):
                        t = j * UN + u
                        weights(t + 3, u + 3, j)
                        gate(t + 2, u)
                        h_T(t + 1, u + 1)
                        y(t, u, j)
                for u in range(UN):
                    dve.wait_ge(xt_in[h][u], rounds * 16 + (32 if u < 2 else 16))
                    hold(1 + u)
                    dve.wait_ge(y_out[h][u], rounds * 16)
                    hold(1 + UN + u)
                dve.wait_ge(peF[h]["xT"], rounds * UN + AHEAD)
                hold(1 + 2 * UN)
                dve.wait_ge(tail_zero[h], tail)
                hold(2 + 2 * UN).then_inc(drained, 1)
                for b in range(h * PB, (h + 1) * PB):
                    result_rows(b, h)

            for b in range(NB):
                dve.wait_ge(added[b], 16 * TOPK)
                if b >= 2:
                    dve.wait_ge(stored[b % 2], 16 * NG * (b // 2))
                norm(dveC, b, xs[:, b, :], fin[:, b % 2, :])


_INS = ["x", "ctx_512", "L0_xattn_Wq", "L0_xattn_Wkv_expand", "L0_xattn_Wout", "L0_ffn_gate_w",
        "L0_ffn_w_gate", "L0_ffn_w_up", "L0_ffn_w_down"]


def kernel(**inputs):
    import numpy as np
    import concourse.bacc as bacc
    from concourse.bass_utils import run_bass_kernel_spmd

    nc = bacc.Bacc("TRN2", target_bir_lowering=False, num_devices=1)
    arrays, args = {}, []
    for name in _INS:
        a = np.ascontiguousarray(inputs[name])
        arrays[f"in_{name}"] = a
        args.append(nc.dram_tensor(f"in_{name}", a.shape, mybir.dt.from_np(a.dtype), kind="ExternalInput").ap())
    out = nc.dram_tensor("out_0", (NB, P, D), F32, kind="ExternalOutput").ap()
    build(nc, *args, out)
    r = run_bass_kernel_spmd(nc, [arrays], core_ids=[0])
    return r.results[0]["out_0"]
```

```python
from contextlib import ExitStack

import concourse.bass as bass
from concourse import mybir

F32 = mybir.dt.float32
BF16 = mybir.dt.bfloat16
I32 = mybir.dt.int32
ALU = mybir.AluOpType
ACT = mybir.ActivationFunctionType
ET = mybir.EngineType
AX_X = mybir.AxisListType.X

P = 128
NB, D = 16, 256
NH, HD = 16, 16
SEG, DIL = 64, 2
GR = SEG // DIL
NG = P // GR
PAIRS = D // 32
LAT = 64
NE, INTER, TOPK = 32, 96, 8
CAP = 2 * (NB * P * TOPK // NE)
XW = D + NE
PART = (10, NB - 10)
PARTS = len(PART)
START = [sum(PART[:h]) for h in range(PARTS + 1)]
PT_TOK = max(PART) * P
QT = min(CAP, PT_TOK) // P
STRIDE = (QT + 1) * P
MAXB = PT_TOK * TOPK // P + NE
UN = 4
AHEAD = 3
TAB = MAXB + 2 * UN
LEAD = 2
IDLE = 10
XG_ROWS = NE * STRIDE + IDLE * P
Y_ROWS = (MAXB + 2) * P
Y_ZERO = (MAXB + 1) * P
FAR = 65536.0
EPS = 1e-5
LOW = -87.3
N_CONST = 48
MAGIC = 1597463007.0

assert MAXB % UN == 0 and all(n % 2 == 0 for n in PART)


class Steps:

    def __init__(self, sem, names):
        self.sem, self.names = sem, names.split()

    def at(self, tile, name):
        return len(self.names) * tile + self.names.index(name) + 1


def there(tile):
    return not isinstance(tile, int) or tile >= 0


LN = "stats aggr veps shift seed n1 n2 n3 c1 c2 c3 c4 norm"


def first_token(g):
    return SEG * (g // DIL) + g % DIL


def build(nc, x, ctx_in, wq, wkv, wout, gate_w, w_gate, w_up, w_down, out):
    stack = ExitStack()
    with stack:
        def sb(name, shape, dt=F32):
            return stack.enter_context(nc.sbuf_tensor(name, shape, dt))

        def sem(name):
            return stack.enter_context(nc.semaphore(name))

        xg = [nc.dram_tensor(f"queues{h}", (XG_ROWS, XW), F32).ap() for h in range(PARTS)]
        yg = [nc.dram_tensor(f"results{h}", (Y_ROWS, D), F32).ap() for h in range(PARTS)]

        bank = [stack.enter_context(nc.psum_tensor(f"bank{i}", [P, 512], F32)) for i in range(8)]
        pA, pC, pX, pO, pW = bank[0], bank[1], bank[2], bank[3], bank[4]
        pS = [bank[5], bank[6]]
        pT = bank[7]

        xs = sb("xs", [P, NB, D])
        x1 = sb("x1", [P, 2, D])
        x2 = sb("x2", [P, 2, XW])
        ct = sb("ct", [P, 2, P])
        cs = sb("cs", [P, NB, LAT])
        wgu = sb("wgu", [P, NE * 2 * 2 * INTER])
        wd = sb("wd", [INTER, NE * D])
        gw = sb("gw", [P, 2, NE])
        wqT = sb("wqT", [P, 2, D])
        woT = sb("woT", [P, 2, D])
        wkvT = sb("wkvT", [LAT, 2 * D])
        ident = sb("ident", [P, P])
        identb = sb("identb", [P, P], BF16)
        causal = sb("causal", [P, P], BF16)
        before = sb("before", [P, P], BF16)
        onesb = sb("onesb", [P, P], BF16)
        ones32 = sb("ones32", [P, NE])
        own = sb("own", [P, D])
        hmask = sb("hmask", [P, 8])
        rmask = sb("rmask", [P, 4])
        rank_i = sb("rank_i", [P, TOPK * NE], I32)
        rankc = sb("rankc", [P, TOPK, NE])
        eoff_i = sb("eoff_i", [P, NE], I32)
        eoff = sb("eoff", [P, NE])
        zrow_i = sb("zrow_i", [P, 1], I32)
        zrow = sb("zrow", [P, 1])
        blk_i = sb("blk_i", [NE, TAB], I32)
        blk = sb("blk", [NE, TAB])
        thr_i = sb("thr_i", [NE, QT], I32)
        thr = sb("thr", [NE, QT])
        upto = sb("upto", [NE, NE], BF16)
        under = sb("under", [NE, NE], BF16)
        zeros = sb("zeros", [P, XW])
        gm = sb("gm", [P, 2, D])
        gT = sb("gT", [P, 2, P])
        gX = sb("gX", [P, 2, 4, P])
        sA = sb("sA", [P, PAIRS, GR])
        eA = sb("eA", [P, PAIRS, GR])
        eAT = sb("eAT", [P, PAIRS, GR])
        oA = sb("oA", [P, D])
        mA = sb("mA", [P, PAIRS])
        dA = sb("dA", [P, PAIRS])
        rA = sb("rA", [P, PAIRS])
        cT = sb("cT", [LAT, P])
        kT = sb("kT", [P, 2, P])
        kX = sb("kX", [P, 2, 2, 8, P])
        vX = sb("vX", [P, 2, PAIRS, 4, HD])
        x1T = sb("x1T", [P, 2, P])
        qT = sb("qT", [P, 2, P])
        nmax = sb("nmax", [P, NH])
        den = sb("den", [P, NH])
        rden = sb("rden", [P, NH])
        pr = sb("pr", [P, 2, 4, P])
        prT = sb("prT", [P, 2, 4, P])
        rX = sb("rX", [P, NH, HD])
        rT = sb("rT", [P, 2, P])
        oT = sb("oT", [P, 2, P])
        yB = sb("yB", [P, D])
        x2T = sb("x2T", [P, 2, P])
        top = sb("top", [P, 1])
        lc = sb("lc", [P, NE])
        m8 = sb("m8", [P, TOPK])
        lr = sb("lr", [P, NE])
        pick = sb("pick", [P, NE])
        pickb = sb("pickb", [P, NE], BF16)
        seen = sb("seen", [P, NE], BF16)
        er = sb("er", [P, NE])
        rk = sb("rk", [P, NE])
        ew = sb("ew", [P, NE])
        es = sb("es", [P, 1])
        ri = sb("ri", [P, 1])
        posg = sb("posg", [P, NE])
        fits = sb("fits", [P, NE])
        earlier = sb("earlier", [P, NE])
        slot = sb("slot", [P, NB, NE])
        rank = sb("rank", [P, NE])
        eq = sb("eq", [P, NB, TOPK, NE], BF16)
        eqs = sb("eqs", [P, TOPK, NE])
        idf = sb("idf", [P, TOPK])
        xidx = sb("xidx", [P, 2, TOPK], I32)
        yidx = sb("yidx", [P, NB, TOPK], I32)
        slz = sb("slz", [P, 2, NE])
        eqsY = sb("eqsY", [P, TOPK, NE])
        scrap = sb("scrap", [1, 3 + (2 + PARTS) * UN])
        st6 = sb("st6", [P, 6])
        mv = sb("mv", [P, 2])
        ve = sb("ve", [P, 1])
        half = sb("half", [P, 1], I32)
        ry = sb("ry", [P, 1])
        rt = sb("rt", [P, 1])
        rp = sb("rp", [P, 1])
        gone = sb("gone", [NE, 1])
        room = sb("room", [NE, 1])
        took = sb("took", [NE, 1])
        nblk = sb("nblk", [NE, 1])
        nblkb = sb("nblkb", [NE, 1], BF16)
        skipb = sb("skipb", [NE, 1], BF16)
        nund = sb("nund", [NE, NE], BF16)
        junk = sb("junk", [NE, QT])
        cum = sb("cum", [NE, 1])
        past = sb("past", [NE, TAB], BF16)
        tjunk = sb("tjunk", [1, MAXB // UN])
        rnds = sb("rnds", [1, 1])
        tab_g = sb("tab_g", [1, PARTS, TAB + 2 * LEAD], I32)
        tab_w = sb("tab_w", [1, PARTS, TAB + 2 * LEAD], I32)
        tab_x = sb("tab_x", [1, PARTS, TAB + 2 * LEAD], I32)
        tab_d = sb("tab_d", [1, PARTS, TAB], I32)
        tab_p = sb("tab_p", [1, PARTS, NE], I32)
        tab_n = sb("tab_n", [1, PARTS], I32)
        tab_t = sb("tab_t", [1, PARTS], I32)
        tab_f = sb("tab_f", [1, 2, TAB])
        shift_y = sb("shift_y", [P, PARTS, NE])
        xt = sb("xt", [P, UN, XW])
        xtT = sb("xtT", [P, 2, 2, P])
        th = sb("th", [P, 2, INTER])
        tg = sb("tg", [P, 2, INTER])
        hg = sb("hg", [P, 2, INTER])
        hT = sb("hT", [INTER, 2, P])
        wcol = sb("wcol", [P, UN])
        ys = sb("ys", [P, UN, D])
        fin = sb("fin", [P, 2, D])

        x_in = [sem("x_in0"), sem("x_in1")]
        ctx_loaded = sem("ctx_loaded")
        small_loaded = sem("small_loaded")
        experts_loaded = sem("experts_loaded")
        consts = sem("consts")
        wt_ps, wt_sb = sem("wt_ps"), sem("wt_sb")
        peA = Steps(sem("peA"), "gT cT s kv o")
        actA = Steps(sem("actA"), "gT cT e kT v")
        dveA = Steps(sem("dveA"), "max sub sum inv turn scale add " + LN)
        poolA = Steps(sem("poolA"), "gm ct gX kX")
        kept = sem("kept")
        peB = Steps(sem("peB"), "x1T q S0 S1 T0 S2 T1 V0 S3 T2 V1 T3 V2 V3 rT y")
        actB = Steps(sem("actB"), "x1T q e0 e1 T0 e2 e3 T2 rT")
        dveB = Steps(sem("dveB"), "m0 m1 m2 T1 m3 T3 inv rX oT add " + LN)
        peR = Steps(sem("peR"), "x2T lg pos")
        actR = Steps(sem("actR"), "x2T e")
        dveR = Steps(sem("dveR"), "top clamp m8 mr pick pickb rk rk2 ew ri slot posg fits rank w seen eq eqs sum idx")
        peH = Steps(sem("peH"), "count place table")
        dveH = Steps(sem("dveH"), "room min took nblk nblkb skipb nund gone earlier reset cum past sh tp n n2 tt fe fx tg tw td tx")
        peF = [{n: sem(f"peF{h}_{n}") for n in ("xT", "gu", "hT", "y")} for h in range(PARTS)]
        actF = [{n: sem(f"actF{h}_{n}") for n in ("xT", "th")} for h in range(PARTS)]
        dveF = [{n: sem(f"dveF{h}_{n}") for n in ("w", "tg", "hg", "hT", "y")} for h in range(PARTS)]
        drained = sem("drained")
        xt_free = sem("xt_free")
        poolY = Steps(sem("poolY"), "slot row eqs sum16 sum8 sum4 sum2 sum1 idx")
        dveC = Steps(sem("dveC"), LN)
        scattered = [sem(f"scattered{k}") for k in range(2)]
        idle_zero = sem("idle_zero")
        pad_zero = [sem(f"pad_zero{h}") for h in range(PARTS)]
        tail_zero = [sem(f"tail_zero{h}") for h in range(PARTS)]
        results_in = [sem(f"results_in{h}") for h in range(PARTS)]
        xt_in = [[sem(f"xt_in{h}_{k}") for k in range(UN)] for h in range(PARTS)]
        y_out = [[sem(f"y_out{h}_{k}") for k in range(UN // 2)] for h in range(PARTS)]
        added = [sem(f"added{b}") for b in range(NB)]
        stored = [sem(f"stored{k}") for k in range(2)]

        gate_v = w_gate.rearrange("e (p k) i -> p e (k i)", k=2)
        up_v = w_up.rearrange("e (p k) i -> p e (k i)", k=2)
        down_v = w_down.rearrange("e i d -> i e d")
        wgu_v = wgu[:, :].rearrange("p (e g k) -> p e g k", e=NE, g=2)

        block = stack.enter_context(nc.Block())

        def three_stages(eng, step, tables):
            def at(k, par):
                if isinstance(k, int):
                    step(*(t if 0 <= t < NB else None for t in (k, k - 1, k - 2)), par)
                else:
                    step(k, k - 1, k - 2, par)

            for k in range(4):
                at(k, k % 2)
            with eng.Fori(0, PART[0] // 2 - 1) as i:
                at(2 * i + 4, 0)
                at(2 * i + 5, 1)
            tables(0)
            for k in range(PART[0] + 2, NB + 2):
                at(k, k % 2)
            tables(1)

        def four(engine, entries, most):
            return nc.values_load_multi_w_load_instructions(
                entries, engines=(engine,), min_val=0, max_val=most,
                skip_runtime_bounds_check_because="the tables hold rows and columns of these arrays only")[1]

        def pad_queues(eng, h):
            with eng.Fori(0, NE) as e:
                r = eng.value_load(tab_p[0:1, h, bass.ds(e, 1)], min_val=0, max_val=NE * STRIDE - P)
                eng.dma_start(xg[h][bass.ds(r, P), :], zeros[:, :]).then_inc(pad_zero[h], 16)
            rounds = eng.value_load(tab_n[0:1, h:h + 1], min_val=1, max_val=MAXB // UN)
            with eng.Fori(rounds * UN, MAXB + 1) as t:
                eng.dma_start(yg[h][bass.ds(t * P, P), :], zeros[:, 0:D]).then_inc(tail_zero[h], 16)

        @block.sync
        def _(sp):
            def load_x(g, b0, b1, s):
                t0 = first_token(g)
                sp.dma_start(xs[GR * g:GR * (g + 1), b0:b1, :],
                             x[b0:b1, t0:t0 + DIL * (GR - 1) + 1:DIL, :].rearrange("b i d -> i b d")
                             ).then_inc(s, 16)

            def finish_results(h):
                sp.wait_ge(drained, h + 1)
                sp.dma_start(yg[h][Y_ZERO:Y_ZERO + P, :], zeros[:, 0:D]).then_inc(results_in[h], 16)

            for g in range(NG):
                load_x(g, 0, 2, x_in[0])
            sp.dma_start(cs[:, :, :], ctx_in.rearrange("b s l -> s b l")).then_inc(ctx_loaded, 16)
            for g in range(NG):
                load_x(g, 2, NB, x_in[1])
            sp.wait_ge(consts, 1)
            for h in range(PARTS):
                for k in range(IDLE):
                    r = NE * STRIDE + k * P
                    sp.dma_start(xg[h][r:r + P, :], zeros[:, :]).then_inc(idle_zero, 16)
            for e in range(0, NE, 8):
                sp.dma_start(wgu_v[:, e:e + 8, 0, :], gate_v[:, e:e + 8, :]).then_inc(experts_loaded, 16)
                sp.dma_start(wgu_v[:, e:e + 8, 1, :], up_v[:, e:e + 8, :]).then_inc(experts_loaded, 16)
                sp.dma_start(wd[:, e * D:(e + 8) * D].rearrange("i (e d) -> i e d", d=D),
                             down_v[:, e:e + 8, :]).then_inc(experts_loaded, 16)

            sp.wait_ge(dveH.sem, dveH.at(0, "tx"))
            pad_queues(sp, 0)
            for h in range(PARTS):
                if h:
                    sp.wait_ge(dveH.sem, dveH.at(h, "tx"))
                rounds = sp.value_load(tab_n[0:1, h:h + 1], min_val=1, max_val=MAXB // UN)
                for k in range(2):
                    sp.wait_ge(scattered[k], 16 * TOPK * START[h + 1] // 2)
                sp.wait_ge(pad_zero[h], 16 * NE)
                sp.wait_ge(idle_zero, 16 * IDLE * PARTS)
                if h:
                    sp.wait_ge(xt_free, h)

                def load_block(t, s, row):
                    sp.dma_start(xt[:, s, :], xg[h][bass.ds(row, P), :]).then_inc(xt_in[h][s], 16)

                def rows_of(first):
                    return four(ET.SP, tab_x[0:1, h, bass.ds(first, UN)], XG_ROWS - P)

                for t, row in zip((0, 1), rows_of(0)[LEAD:]):
                    load_block(t, t, row)
                for t, row in zip((2, 3, 4, 5), rows_of(UN)):
                    if t >= UN:
                        sp.wait_ge(peF[h]["xT"], t - UN + 1)
                        sp.wait_ge(dveF[h]["w"], t - UN + 1)
                    load_block(t, t % UN, row)
                if h:
                    finish_results(h - 1)
                with sp.Fori(0, rounds) as j:
                    rows = rows_of(j * UN + 2 * UN)
                    for u in range(UN):
                        t = j * UN + u
                        turned, written = sp.snap(t + 3), sp.snap(t + 1)
                        sp.wait_ge(peF[h]["xT"], turned)
                        sp.wait_ge(dveF[h]["w"], turned)
                        load_block(t, (u + 2) % UN, rows[u])
                        if u % 2:
                            first = sp.snap((t - 1) * P)
                            sp.wait_ge(dveF[h]["y"], written)
                            sp.dma_start(yg[h][bass.ds(first, 2 * P), :].rearrange("(s p) d -> p s d", p=P),
                                         ys[:, u - 1:u + 1, :]).then_inc(y_out[h][u // 2], 16)
            finish_results(PARTS - 1)

            for b in range(NB):
                sp.wait_ge(dveC.sem, dveC.at(b, "norm"))
                for g in range(NG):
                    t0 = first_token(g)
                    sp.dma_start(out[b, t0:t0 + DIL * (GR - 1) + 1:DIL, :],
                                 fin[GR * g:GR * (g + 1), b % 2, :]).then_inc(stored[b % 2], 16)
            for k in range(2):
                sp.wait_ge(stored[k], 16 * NG * NB // 2)

        @block.gpsimd
        def _(pool):
            n = 0

            def put(op, *args, **kw):
                nonlocal n
                if n:
                    pool.wait_ge(consts, n)
                op(*args, **kw).then_inc(consts, 1)
                n += 1

            put(pool.memset, zeros[:, :], 0.0)
            put(pool.memset, own[:, :], 0.0)
            put(pool.memset, ct[:, :, :], 0.0)
            put(pool.memset, ident[:, :], 0.0)
            put(pool.memset, rmask[:, :], 0.0)
            put(pool.memset, causal[:, :], 0.0)
            put(pool.memset, onesb[:, :], 1.0)
            put(pool.memset, ones32[:, :], 1.0)
            put(pool.memset, hmask[:, :], 1.0)
            put(pool.memset, vX[:, :, :, :, :], 0.0)
            put(pool.memset, earlier[:, :], 0.0)
            put(pool.memset, gone[:, :], 0.0)
            put(pool.memset, seen[:, :], 0.0)
            for tab in (tab_g, tab_w, tab_x):
                put(pool.memset, tab[:, :, :], 0)
            for m in (ident,):
                put(pool.affine_select, out=m[:, :], in_=m[:, :], compare_op=ALU.not_equal, fill=1.0,
                                       base=0, pattern=[[-1, P]], channel_multiplier=1)
            own_v = own[:, :].rearrange("p (j s c) -> p j s c", s=DIL, c=HD)
            for g in range(NG):
                rows = slice(GR * g, GR * (g + 1))
                put(pool.memset, own_v[rows, :, g % DIL, :], 1.0)
                put(pool.memset, rmask[rows, g:g + 1], 1.0)
                put(pool.affine_select, out=causal[rows, :], in_=causal[rows, :], compare_op=ALU.is_ge,
                                       fill=-3e38, base=first_token(g), pattern=[[-1, P]],
                                       channel_multiplier=DIL)
                put(pool.affine_select, out=before[rows, :].rearrange("p (a b i) -> p a b i", a=2, b=2),
                                       in_=onesb[rows, :].rearrange("p (a b i) -> p a b i", a=2, b=2),
                                       compare_op=ALU.is_gt, fill=0.0, base=-first_token(g),
                                       pattern=[[SEG, 2], [1, 2], [DIL, GR]], channel_multiplier=-DIL)
            put(pool.affine_select, out=hmask[:, :], in_=hmask[:, :], compare_op=ALU.is_ge, fill=0.0,
                                   base=0, pattern=[[-HD, 8]], channel_multiplier=1)
            put(pool.affine_select, out=upto[:, :], in_=onesb[0:NE, 0:NE], compare_op=ALU.is_ge, fill=0.0,
                                   base=0, pattern=[[1, NE]], channel_multiplier=-1)
            put(pool.affine_select, out=under[:, :], in_=onesb[0:NE, 0:NE], compare_op=ALU.is_gt, fill=0.0,
                                   base=0, pattern=[[1, NE]], channel_multiplier=-1)
            put(pool.iota, rank_i[:, :], [[1, TOPK], [0, NE]], base=1, channel_multiplier=0)
            put(pool.iota, eoff_i[:, :], [[STRIDE, NE]], base=0, channel_multiplier=0)
            put(pool.iota, zrow_i[:, :], [[0, 1]], base=Y_ZERO, channel_multiplier=1)
            put(pool.iota, blk_i[:, :], [[1, TAB]], base=0, channel_multiplier=0)
            put(pool.iota, thr_i[:, :], [[P, QT]], base=0, channel_multiplier=0)
            put(pool.affine_select, out=hmask[:, :], in_=hmask[:, :], compare_op=ALU.is_ge, fill=0.0,
                                   base=HD - 1, pattern=[[HD, 8]], channel_multiplier=-1)
            put(pool.tensor_copy, identb[:, :], ident[:, :])
            put(pool.tensor_copy, rankc[:, :, :].rearrange("p k e -> p (k e)"), rank_i[:, :])
            put(pool.tensor_copy, eoff[:, :], eoff_i[:, :])
            put(pool.tensor_copy, zrow[:, :], zrow_i[:, :])
            put(pool.tensor_copy, blk[:, :], blk_i[:, :])
            put(pool.tensor_copy, thr[:, :], thr_i[:, :])
            assert n == N_CONST, n

            def mask_x(a, par):
                if there(a - 2):
                    pool.wait_ge(peA.sem, peA.at(a - 2, "o"))
                pool.tensor_tensor(gm[:, par, :], xs[:, bass.ds(a, 1), :].rearrange("p a d -> p (a d)"),
                                   own[:, :], ALU.mult).then_inc(poolA.sem, 1)
                pool.tensor_copy(ct[:, par, 0:LAT], cs[:, bass.ds(a, 1), :].rearrange("p a d -> p (a d)")
                                 ).then_inc(poolA.sem, 1)

            def masked(q, dst, src, mask):
                if q == 0:
                    return pool.tensor_tensor(dst, src, mask.unsqueeze(2).to_broadcast([P, 2, P]), ALU.mult)
                return pool.tensor_scalar(dst, src, mask, None, ALU.mult)

            def step(a, b, r, par):
                if a is not None:
                    if isinstance(a, int) and a == 0:
                        pool.wait_ge(x_in[0], 16 * NG)
                        pool.wait_ge(ctx_loaded, 16)
                    if isinstance(a, int) and a == 1:
                        pool.wait_ge(x_in[1], 16 * NG)
                    mask_x(a, par)
                    pool.wait_ge(actA.sem, actA.at(a, "gT"))
                    if there(a - 1):
                        pool.wait_ge(peA.sem, peA.at(a - 1, "s"))
                    for q in range(4):
                        ins = masked(q, gX[:, :, q, :], gT[:, :, :], rmask[:, q:q + 1])
                    ins.then_inc(poolA.sem, 1)
                    pool.wait_ge(actA.sem, actA.at(a, "kT"))
                    if there(a - 2):
                        pool.wait_ge(peB.sem, peB.at(a - 2, "S3"))
                    for q in range(8):
                        ins = masked(q, kX[:, par, :, q, :], kT[:, :, :], hmask[:, q:q + 1])
                    ins.then_inc(poolA.sem, 1)
                if r is not None:
                    h = part[0]
                    pool.wait_ge(dveR.sem, dveR.at(r, "idx"))
                    pool.tensor_copy(xs[:, bass.ds(r, 1), :].rearrange("p r d -> p (r d)"), x2[:, par, 0:D]
                                     ).then_inc(kept, 1)
                    for k in range(TOPK):
                        pool.indirect_dma_start(
                            xg[h], bass.IndirectOffsetOnAxis(ap=xidx[:, par, k:k + 1], axis=0),
                            x2[:, par, :], None,
                            bounds_check=last_row, oob_is_err=False).then_inc(scattered[par], 16)

            part = [0]
            last_row = pool.to_reg(XG_ROWS - 1)

            def tables(h):
                part[0] = h + 1

            three_stages(pool, step, tables)

            pool.wait_ge(dveH.sem, dveH.at(1, "tx"))
            pad_queues(pool, 1)

            for h in range(PARTS):
                for b in range(START[h], START[h + 1]):
                    s = poolY.sem
                    pool.tensor_scalar(slz[:, 0, :], slot[:, b, :], zrow[:, 0:1], None, ALU.subtract).then_inc(s, 1)
                    pool.wait_ge(s, poolY.at(b, "slot"))
                    pool.tensor_tensor(slz[:, 1, :], slz[:, 0, :], shift_y[:, h, :], ALU.add).then_inc(s, 1)
                    pool.wait_ge(s, poolY.at(b, "row"))
                    pool.tensor_tensor(eqsY[:, :, :], slz[:, 1, :].unsqueeze(1).to_broadcast([P, TOPK, NE]),
                                       eq[:, b, :, :], ALU.mult).then_inc(s, 1)
                    for n in (16, 8, 4, 2, 1):
                        pool.wait_ge(s, poolY.at(b, {16: "eqs", 8: "sum16", 4: "sum8", 2: "sum4", 1: "sum2"}[n]))
                        pool.tensor_tensor(eqsY[:, :, 0:n], eqsY[:, :, 0:n], eqsY[:, :, n:2 * n], ALU.add
                                           ).then_inc(s, 1)
                    pool.wait_ge(s, poolY.at(b, "sum1"))
                    pool.tensor_scalar(yidx[:, b, :], eqsY[:, :, 0], zrow[:, 0:1], None, ALU.add).then_inc(s, 1)
                    pool.wait_ge(s, poolY.at(b, "idx"))

            for h in range(PARTS):
                pool.wait_ge(kept, START[h + 1])
                pool.wait_ge(results_in[h], 16)
                for k in range(TOPK):
                    for b in range(START[h], START[h + 1]):
                        if k:
                            pool.wait_ge(added[b], 16 * k)
                        pool.indirect_dma_start(
                            xs[:, b, :], None, yg[h],
                            bass.IndirectOffsetOnAxis(ap=yidx[:, b, k:k + 1], axis=0),
                            bounds_check=Y_ROWS - 1, oob_is_err=True, compute_op=ALU.add
                        ).then_inc(added[b], 16)

        @block.tensor
        def _(pe):
            pe.wait_ge(consts, N_CONST)
            pe.wait_ge(small_loaded, 16 * 4)
            for m in range(2):
                for kk in range(2):
                    pe.transpose(bank[4][:, (kk * 2 + m) * P:(kk * 2 + m + 1) * P],
                                 pr[:, 0, :, :].rearrange("p a b -> p (a b)")[:, m * D + kk * P:m * D + kk * P + P],
                                 ident[:, :])
                    ins = pe.transpose(bank[5][:, (kk * 2 + m) * P:(kk * 2 + m + 1) * P],
                                 pr[:, 1, :, :].rearrange("p a b -> p (a b)")[:, m * D + kk * P:m * D + kk * P + P],
                                 ident[:, :])
            for m in range(4):
                ins = pe.transpose(bank[6][0:LAT, m * P:(m + 1) * P],
                                   prT[:, 0, :, :].rearrange("p a b -> p (a b)")[:, m * LAT:(m + 1) * LAT],
                                   ident[:, :])
            ins.then_inc(wt_ps, 1)
            pe.wait_ge(wt_sb, 3)

            def scores(b, g, par):
                m = g // 2
                pe.matmul(pS[g % 2][:, :], identb[:, :],
                          causal[:, :].unsqueeze(1).to_broadcast([P, 4, P]),
                          start=True, stop=False)
                pe.matmul(pS[g % 2][:, :], qT[:, m, :],
                          kX[:, par, m, 4 * (g % 2):4 * (g % 2) + 4, :],
                          start=False, stop=True).then_inc(peB.sem, 1)

            def turn_probs(b, g, before_it):
                pe.wait_ge(actB.sem, actB.at(b, f"e{g}"))
                if before_it is not None:
                    pe.wait_ge(*before_it)
                for q in range(4):
                    ins = pe.transpose(pT[:, q * P:(q + 1) * P], pr[:, g % 2, q, :], ident[:, :])
                ins.then_inc(peB.sem, 1)

            def values(b, g, par, ready):
                pe.wait_ge(*ready)
                for q in range(4):
                    hd = 4 * g + q
                    j, s = hd // 2, hd % 2
                    ins = pe.matmul(pO[32 * (j % 4):32 * (j % 4) + 32, (j // 4) * P:(j // 4) * P + P],
                                    vX[:, par, j, 2 * s:2 * s + 2, :].rearrange("p a c -> p (a c)"),
                                    prT[:, g % 2, q, :], start=(s == 0), stop=(s == 1),
                                    tile_position=(0, 32 * (j % 4)))
                ins.then_inc(peB.sem, 1)

            def step(a, b, r, par):
                pb = 1 - par
                if b is not None:
                    pe.wait_ge(dveA.sem, dveA.at(b, "norm"))
                    for kk in range(2):
                        ins = pe.transpose(pX[:, kk * P:(kk + 1) * P],
                                           x1[:, pb, kk * P:(kk + 1) * P], ident[:, :])
                    ins.then_inc(peB.sem, 1)
                if a is not None:
                    pe.wait_ge(poolA.sem, poolA.at(a, "gm"))
                    if there(a - 1):
                        pe.wait_ge(dveA.sem, dveA.at(a - 1, "scale"))
                    for kk in range(2):
                        ins = pe.transpose(pA[:, kk * P:(kk + 1) * P], gm[:, par, kk * P:(kk + 1) * P], ident[:, :])
                    ins.then_inc(peA.sem, 1)
                    if there(a - 1):
                        pe.wait_ge(actA.sem, actA.at(a - 1, "v"))
                    pe.wait_ge(poolA.sem, poolA.at(a, "ct"))
                    pe.transpose(pC[:, 0:P], ct[:, par, :], ident[:, :]).then_inc(peA.sem, 1)
                if b is not None:
                    pe.wait_ge(actB.sem, actB.at(b, "x1T"))
                    for m in range(2):
                        for kk in range(2):
                            ins = pe.matmul(pX[:, m * P:(m + 1) * P], wqT[:, kk, m * P:(m + 1) * P],
                                            x1T[:, kk, :], start=(kk == 0), stop=(kk == 1))
                    ins.then_inc(peB.sem, 1)
                if r is not None:
                    pe.wait_ge(dveB.sem, dveB.at(r, "norm"))
                    if b is not None:
                        pe.wait_ge(actB.sem, actB.at(b, "q"))
                    else:
                        pe.wait_ge(dveR.sem, dveR.at(r - 1, "posg"))
                    for kk in range(2):
                        ins = pe.transpose(pX[:, kk * P:(kk + 1) * P], x2[:, par, kk * P:(kk + 1) * P], ident[:, :])
                    ins.then_inc(peR.sem, 1)
                if a is not None:
                    pe.wait_ge(actA.sem, actA.at(a, "gT"))
                    pe.wait_ge(poolA.sem, poolA.at(a, "gX"))
                    for g in range(NG):
                        for m in range(2):
                            ins = pe.matmul(pA[GR * g:GR * (g + 1), D + m * P:D + (m + 1) * P],
                                            gT[:, m, GR * g:GR * (g + 1)],
                                            gX[:, m, :, GR * g:GR * (g + 1)],
                                            start=True, stop=True, tile_position=(0, GR * g))
                    ins.then_inc(peA.sem, 1)
                if b is not None:
                    pe.wait_ge(actB.sem, actB.at(b, "q"))
                    pe.wait_ge(poolA.sem, poolA.at(b, "kX"))
                    scores(b, 0, pb)
                    scores(b, 1, pb)
                if a is not None:
                    pe.wait_ge(actA.sem, actA.at(a, "cT"))
                    for m in range(2):
                        pe.matmul(pC[:, m * P:(m + 1) * P], wkvT[:, m * P:(m + 1) * P], cT[:, :],
                                  start=True, stop=True)
                    pe.matmul(pC[:, D:2 * D], cT[:, :], wkvT[:, D:2 * D], start=True, stop=True
                              ).then_inc(peA.sem, 1)
                if r is not None:
                    pe.wait_ge(actR.sem, actR.at(r, "x2T"))
                    for kk in range(2):
                        ins = pe.matmul(pX[:, D:D + NE], x2T[:, kk, :], gw[:, kk, :],
                                        start=(kk == 0), stop=(kk == 1))
                    ins.then_inc(peR.sem, 1)
                if b is not None:
                    turn_probs(b, 0, None)
                    scores(b, 2, pb)
                if b is not None:
                    turn_probs(b, 1, (actB.sem, actB.at(b, "T0")))
                    if a is not None:
                        pe.wait_ge(dveA.sem, dveA.at(a, "turn"))
                    values(b, 0, pb, (actB.sem, actB.at(b, "T0")))
                if a is not None:
                    if b is None:
                        pe.wait_ge(dveA.sem, dveA.at(a, "turn"))
                    for j in range(PAIRS):
                        for g in range(NG):
                            ins = pe.matmul(pA[GR * g:GR * (g + 1), j * 32:(j + 1) * 32],
                                            eAT[GR * g:GR * (g + 1), j, :],
                                            gm[GR * g:GR * (g + 1), par, j * 32:(j + 1) * 32],
                                            start=True, stop=True, tile_position=(GR * g, GR * g))
                    ins.then_inc(peA.sem, 1)
                if b is not None:
                    scores(b, 3, pb)
                if r is not None:
                    pe.wait_ge(dveR.sem, dveR.at(r, "pickb"))
                    pe.matmul(pX[:, D + 2 * NE:D + 3 * NE], before[:, :], pickb[:, :], start=True, stop=False)
                    pe.matmul(pX[:, D + 2 * NE:D + 3 * NE], onesb[:, :], seen[:, :], start=False, stop=True
                              ).then_inc(peR.sem, 1)
                if b is not None:
                    turn_probs(b, 2, (dveB.sem, dveB.at(b, "T1")))
                    values(b, 1, pb, (dveB.sem, dveB.at(b, "T1")))
                    turn_probs(b, 3, (actB.sem, actB.at(b, "T2")))
                    values(b, 2, pb, (actB.sem, actB.at(b, "T2")))
                    values(b, 3, pb, (dveB.sem, dveB.at(b, "T3")))
                    pe.wait_ge(dveB.sem, dveB.at(b, "rX"))
                    for m in range(2):
                        ins = pe.transpose(pO[:, D + m * P:D + (m + 1) * P],
                                           rX[:, 8 * m:8 * m + 8, :].rearrange("p h c -> p (h c)"), ident[:, :])
                    ins.then_inc(peB.sem, 1)
                    pe.wait_ge(dveB.sem, dveB.at(b, "oT"))
                    for kk in range(2):
                        ins = pe.matmul(pW[:, 0:D], oT[:, kk, :], woT[:, kk, :], start=(kk == 0), stop=(kk == 1))
                    ins.then_inc(peB.sem, 1)

            def tables(h):
                pe.wait_ge(dveR.sem, dveR.at(START[h + 1] - 1, "seen"))
                pe.wait_ge(dveB.sem, dveB.at(min(START[h + 1], NB - 1), "add"))
                pe.matmul(pW[:, 0:NE], onesb[:, :], seen[:, :], start=True, stop=True)
                pe.matmul(pW[0:NE, NE:NE + 1], seen[:, :], onesb[:, 0:1], start=True, stop=True
                          ).then_inc(peH.sem, 1)
                pe.wait_ge(dveH.sem, dveH.at(h, "earlier"))
                pe.matmul(pW[0:NE, NE + 1:NE + 2], upto[:, :], nblkb[:, :], start=True, stop=True)
                pe.matmul(pW[:, 64:64 + NE], onesb[0:NE, :], nund[:, :], start=True, stop=True)
                pe.matmul(pW[0:1, 96:96 + NE], took[:, :], ident[0:NE, 0:NE], start=True, stop=True)
                pe.matmul(pW[0:1, 130:131], nblkb[:, :], onesb[0:NE, 0:1], start=True, stop=True
                          ).then_inc(peH.sem, 1)
                pe.wait_ge(dveH.sem, dveH.at(h, "n"))
                pe.matmul(pW[0:1, 160:160 + TAB], onesb[0:NE, 0:1], past[:, :], start=True, stop=True)
                pe.matmul(pW[0:1, 300:300 + TAB], skipb[:, :], past[:, :], start=True, stop=True
                          ).then_inc(peH.sem, 1)
                pe.wait_ge(dveH.sem, dveH.at(h, "tx"))

            three_stages(pe, step, tables)

            pe.wait_ge(experts_loaded, 16 * 3 * (NE // 8))
            for h in range(PARTS):
                rounds = pe.value_load(tab_n[0:1, h:h + 1], min_val=1, max_val=MAXB // UN)

                def xT(t, u, j):
                    s = u % UN
                    pe.wait_ge(xt_in[h][s], 16 * (j + (u // UN + 1)))
                    if there(t - 2):
                        pe.wait_ge(actF[h]["xT"], t - 1)
                    for kk in range(2):
                        ins = pe.transpose(bank[u % 2][:, kk * P:(kk + 1) * P],
                                           xt[:, s, kk:D:2], ident[:, :])
                    ins.then_inc(peF[h]["xT"], 1)

                def gu(t, u, e):
                    pe.wait_ge(actF[h]["xT"], t + 1)
                    if there(t - 2):
                        pe.wait_ge(dveF[h]["hg"], t - 1)
                    for kk in range(2):
                        ins = pe.matmul(bank[2 + u % 2][:, 0:2 * INTER].rearrange("p (g i) -> p g i", g=2),
                                        xtT[:, u % 2, kk, :],
                                        wgu[:, bass.ds(e, 4 * INTER)].rearrange(
                                            "p (g k i) -> p g k i", g=2, k=2)[:, :, kk, :],
                                        start=(kk == 0), stop=(kk == 1))
                    ins.then_inc(peF[h]["gu"], 1)

                def turn_h(t, u):
                    pe.wait_ge(dveF[h]["hg"], t + 1)
                    pe.transpose(bank[4 + u % 2][0:INTER, 0:P], hg[:, u % 2, :], ident[:, :]
                                 ).then_inc(peF[h]["hT"], 1)

                def down(t, u, e):
                    pe.wait_ge(dveF[h]["hT"], t + 1)
                    pe.matmul(bank[6 + u % 2][:, 0:D], hT[:, u % 2, :], wd[:, bass.ds(e, D)],
                              start=True, stop=True).then_inc(peF[h]["y"], 1)

                for t in range(3):
                    xT(t, t, 0)
                for t, e in zip((0, 1), four(ET.PE, tab_g[0:1, h, 0:UN], (NE - 1) * 4 * INTER)[LEAD:]):
                    gu(t, t, e)
                turn_h(0, 0)
                with pe.Fori(0, rounds) as j:
                    e_gu = four(ET.PE, tab_g[0:1, h, bass.ds(j * UN + UN, UN)], (NE - 1) * 4 * INTER)
                    e_down = four(ET.PE, tab_d[0:1, h, bass.ds(j * UN, UN)], (NE - 1) * D)
                    for u in range(UN):
                        t = j * UN + u
                        xT(t + 3, u + 3, j)
                        gu(t + 2, u, e_gu[u])
                        turn_h(t + 1, u + 1)
                        down(t, u, e_down[u])

        @block.scalar
        def _(act):
            act.dma_start(pr[:, 0, :, :].rearrange("p a b -> p (a b)").rearrange("p (m d) -> p m d", m=2),
                          wq.rearrange("(m p) d -> p m d", p=P)).then_inc(small_loaded, 16)
            act.dma_start(pr[:, 1, :, :].rearrange("p a b -> p (a b)").rearrange("p (m d) -> p m d", m=2),
                          wout.rearrange("(m p) d -> p m d", p=P)).then_inc(small_loaded, 16)
            act.dma_start(prT[:, 0, 0:2, :].rearrange("p a b -> p (a b)").rearrange("p (m l) -> p m l", m=4),
                          wkv.rearrange("(m p) l -> p m l", p=P)).then_inc(small_loaded, 16)
            act.dma_start(gw[:, :, :], gate_w.rearrange("(k p) e -> p k e", p=P)).then_inc(small_loaded, 16)
            act.wait_ge(wt_ps, 1)
            act.copy(wqT[:, :, :].rearrange("p a b -> p (a b)"), bank[4][:, :]).then_inc(wt_sb, 1)
            act.copy(woT[:, :, :].rearrange("p a b -> p (a b)"), bank[5][:, :]).then_inc(wt_sb, 1)
            act.copy(wkvT[:, :], bank[6][0:LAT, :]).then_inc(wt_sb, 1)

            def exps(b, g):
                act.wait_ge(dveB.sem, dveB.at(b, f"m{g}"))
                for q in range(4):
                    hd = 4 * g + q
                    ins = act.activation(pr[:, g % 2, q, :], pS[g % 2][:, q * P:(q + 1) * P], ACT.Exp,
                                         bias=nmax[:, hd:hd + 1], accum_out=den[:, hd:hd + 1])
                ins.then_inc(actB.sem, 1)

            def probs_T(b, g):
                act.wait_ge(peB.sem, peB.at(b, f"T{g}"))
                act.copy(prT[:, g % 2, :, :].rearrange("p a b -> p (a b)"), pT[:, :]).then_inc(actB.sem, 1)

            def flat2(t):
                return t[:, :, :].rearrange("p a b -> p (a b)")

            def step(a, b, r, par):
                if b is not None:
                    act.wait_ge(peB.sem, peB.at(b, "x1T"))
                    act.copy(flat2(x1T), pX[:, 0:D]).then_inc(actB.sem, 1)
                if a is not None:
                    act.wait_ge(peA.sem, peA.at(a, "gT"))
                    act.copy(flat2(gT), pA[:, 0:D]).then_inc(actA.sem, 1)
                    act.wait_ge(peA.sem, peA.at(a, "cT"))
                    act.copy(cT[:, :], pC[0:LAT, 0:P]).then_inc(actA.sem, 1)
                if b is not None:
                    act.wait_ge(peB.sem, peB.at(b, "q"))
                    act.mul(flat2(qT), pX[:, 0:D], float(HD) ** -0.5).then_inc(actB.sem, 1)
                if r is not None:
                    act.wait_ge(peR.sem, peR.at(r, "x2T"))
                    act.copy(flat2(x2T), pX[:, 0:D]).then_inc(actR.sem, 1)
                if a is not None:
                    act.wait_ge(dveA.sem, dveA.at(a, "sub"))
                    act.activation(flat2(eA), flat2(sA), ACT.Exp, scale=float(HD) ** -0.5).then_inc(actA.sem, 1)
                if b is not None:
                    exps(b, 0)
                    exps(b, 1)
                if a is not None:
                    act.wait_ge(peA.sem, peA.at(a, "kv"))
                    if there(a - 1):
                        act.wait_ge(poolA.sem, poolA.at(a - 1, "kX"))
                    act.copy(flat2(kT), pC[:, 0:D]).then_inc(actA.sem, 1)
                    act.copy(vX[:, par, :, 0:4:3, :],
                             pC[:, D:2 * D].rearrange("p (j s c) -> p j s c", s=2, c=HD)).then_inc(actA.sem, 1)
                if r is not None:
                    act.wait_ge(dveR.sem, dveR.at(r, "clamp"))
                    act.activation(er[:, :], lc[:, :], ACT.Exp).then_inc(actR.sem, 1)
                if b is not None:
                    probs_T(b, 0)
                    exps(b, 2)
                    exps(b, 3)
                    probs_T(b, 2)
                    act.wait_ge(peB.sem, peB.at(b, "rT"))
                    act.copy(flat2(rT), pO[:, D:2 * D]).then_inc(actB.sem, 1)

            three_stages(act, step, lambda h: None)

            for h in range(PARTS):
                if h == 0:
                    act.wait_ge(dveH.sem, dveH.at(PARTS - 1, "tx"))
                rounds = act.value_load(tab_n[0:1, h:h + 1], min_val=1, max_val=MAXB // UN)

                def xT(t, u):
                    act.wait_ge(peF[h]["xT"], t + 1)
                    if there(t - 2):
                        act.wait_ge(peF[h]["gu"], t - 1)
                    act.copy(xtT[:, u % 2, :, :].rearrange("p a b -> p (a b)"), bank[u % 2][:, 0:D]
                             ).then_inc(actF[h]["xT"], 1)

                def tanh(t, u):
                    act.wait_ge(peF[h]["gu"], t + 1)
                    if there(t - 2):
                        act.wait_ge(dveF[h]["tg"], t - 1)
                    act.activation(th[:, u % 2, :], bank[2 + u % 2][:, 0:INTER], ACT.Tanh, scale=0.5
                                   ).then_inc(actF[h]["th"], 1)

                for t in range(3):
                    xT(t, t)
                for t in range(2):
                    tanh(t, t)
                with act.Fori(0, rounds) as j:
                    for u in range(UN):
                        t = j * UN + u
                        xT(t + 3, u + 3)
                        tanh(t + 2, u)

        @block.vector
        def _(dve):
            dve.wait_ge(consts, N_CONST)

            def hold(k=0):
                return dve.memset(scrap[0:1, k:k + 1], 0.0)

            def norm(steps, t, src, dst, free=None):
                s = steps.sem

                def then(ins):
                    ins.then_inc(s, 1)

                then(dve.bn_stats(st6[:, :], src))
                dve.wait_ge(s, steps.at(t, "stats"))
                hold()
                then(dve.bn_aggr(mv[:, :], st6[:, :]))
                dve.wait_ge(s, steps.at(t, "aggr"))
                then(dve.tensor_scalar(ve[:, :], mv[:, 1:2], EPS, None, ALU.add))
                dve.wait_ge(s, steps.at(t, "veps"))
                then(dve.tensor_scalar(half[:, :], ve[:, :].bitcast(I32), 1, None, ALU.arith_shift_right))
                dve.wait_ge(s, steps.at(t, "shift"))
                then(dve.tensor_scalar(ry[:, :].bitcast(I32), half[:, :], -1.0, MAGIC, ALU.mult, ALU.add))
                dve.wait_ge(s, steps.at(t, "seed"))
                then(dve.scalar_tensor_tensor(rt[:, :], ry[:, :], ve[:, 0:1], ry[:, :], ALU.mult, ALU.mult))
                dve.wait_ge(s, steps.at(t, "n1"))
                then(dve.tensor_scalar(rt[:, :], rt[:, :], -0.5, 1.5, ALU.mult, ALU.add))
                dve.wait_ge(s, steps.at(t, "n2"))
                then(dve.tensor_tensor(ry[:, :], ry[:, :], rt[:, :], ALU.mult))
                dve.wait_ge(s, steps.at(t, "n3"))
                then(dve.scalar_tensor_tensor(rt[:, :], ry[:, :], ve[:, 0:1], ry[:, :], ALU.mult, ALU.mult))
                dve.wait_ge(s, steps.at(t, "c1"))
                then(dve.tensor_scalar(rp[:, :], rt[:, :], 0.375, -1.25, ALU.mult, ALU.add))
                dve.wait_ge(s, steps.at(t, "c2"))
                then(dve.tensor_tensor(rt[:, :], rt[:, :], rp[:, :], ALU.mult))
                dve.wait_ge(s, steps.at(t, "c3"))
                then(dve.scalar_tensor_tensor(ry[:, :], rt[:, :], 1.875, ry[:, :], ALU.add, ALU.mult))
                dve.wait_ge(s, steps.at(t, "c4"))
                if free:
                    free()
                then(dve.tensor_scalar(dst, src, mv[:, 0:1], ry[:, 0:1], ALU.subtract, ALU.mult))

            def xrow(t):
                return xs[:, bass.ds(t, 1), 0:D].rearrange("p t d -> p (t d)")

            def flat2(t):
                return t[:, :, :].rearrange("p a b -> p (a b)")

            def maxes(b, g):
                dve.wait_ge(peB.sem, peB.at(b, f"S{g}"))
                dve.tensor_reduce(nmax[:, 4 * g:4 * g + 4],
                                  pS[g % 2][:, :].rearrange("p (h k) -> p h k", h=4),
                                  AX_X, ALU.max, negate=True).then_inc(dveB.sem, 1)

            def probs_T(b, g):
                dve.wait_ge(peB.sem, peB.at(b, f"T{g}"))
                dve.tensor_copy(prT[:, g % 2, :, :].rearrange("p a b -> p (a b)"), pT[:, :]).then_inc(dveB.sem, 1)

            def step(a, b, r, par):
                if a is not None:
                    A, s = (lambda name: dveA.at(a, name)), dveA.sem
                    dve.wait_ge(peA.sem, peA.at(a, "s"))
                    scr = pA[:, D:2 * D].rearrange("p (j k) -> p j k", j=PAIRS)
                    dve.tensor_reduce(mA[:, :], scr, AX_X, ALU.max).then_inc(s, 1)
                    dve.wait_ge(s, A("max"))
                    dve.tensor_tensor(sA[:, :, :], scr, mA[:, :].unsqueeze(2).to_broadcast([P, PAIRS, GR]),
                                      ALU.subtract).then_inc(s, 1)
                if b is not None:
                    maxes(b, 0)
                    maxes(b, 1)
                if a is not None:
                    dve.wait_ge(actA.sem, actA.at(a, "e"))
                    dve.tensor_reduce(dA[:, :], eA[:, :, :], AX_X, ALU.add).then_inc(s, 1)
                    dve.wait_ge(s, A("sum"))
                    dve.reciprocal(rA[:, :], dA[:, :]).then_inc(s, 1)
                    dve.transpose(flat2(eAT), flat2(eA)).then_inc(s, 1)
                if r is not None:
                    R, t = (lambda name: dveR.at(r, name)), dveR.sem
                    dve.wait_ge(peR.sem, peR.at(r, "lg"))
                    lg = pX[:, D:D + NE]
                    dve.tensor_reduce(top[:, :], lg, AX_X, ALU.max).then_inc(t, 1)
                    dve.wait_ge(t, R("top"))
                    dve.tensor_scalar(lc[:, :], lg, top[:, 0:1], LOW, ALU.subtract, ALU.max).then_inc(t, 1)
                    dve.wait_ge(t, R("clamp"))
                    hold()
                    dve.max(m8[:, :], lc[:, :]).then_inc(t, 1)
                    dve.wait_ge(t, R("m8"))
                    hold()
                    dve.match_replace(lr[:, :], m8[:, :], lc[:, :], 1.0).then_inc(t, 1)
                    dve.wait_ge(t, R("mr"))
                    dve.tensor_scalar(pick[:, :], lr[:, :], 0.5, None, ALU.is_gt).then_inc(t, 1)
                    dve.tensor_scalar(pickb[:, :], lr[:, :], 0.5, None, ALU.is_gt).then_inc(t, 1)
                    dve.wait_ge(t, R("pick"))
                    dve.tensor_tensor_scan(rk[:, :], ones32[:, :], pick[:, :], 0.0, ALU.mult, ALU.add).then_inc(t, 1)
                    dve.wait_ge(t, R("rk"))
                    dve.tensor_tensor(rk[:, :], rk[:, :], pick[:, :], ALU.mult).then_inc(t, 1)
                    dve.wait_ge(actR.sem, actR.at(r, "e"))
                    dve.scalar_tensor_tensor(ew[:, :], er[:, :], 1.0, pick[:, :], ALU.mult, ALU.mult,
                                             accum_out=es[:, :]).then_inc(t, 1)
                    dve.wait_ge(t, R("ew"))
                    dve.reciprocal(ri[:, :], es[:, :]).then_inc(t, 1)
                if b is not None:
                    maxes(b, 2)
                if a is not None:
                    dve.wait_ge(peA.sem, peA.at(a, "o"))
                    dve.tensor_tensor(oA[:, :].rearrange("p (j c) -> p j c", j=PAIRS),
                                      pA[:, 0:D].rearrange("p (j c) -> p j c", j=PAIRS),
                                      rA[:, :].unsqueeze(2).to_broadcast([P, PAIRS, 32]), ALU.mult).then_inc(s, 1)
                if b is not None:
                    probs_T(b, 1)
                    maxes(b, 3)
                if a is not None:
                    dve.wait_ge(s, A("scale"))
                    dve.tensor_tensor(oA[:, :], oA[:, :], xrow(a), ALU.add).then_inc(s, 1)
                    dve.wait_ge(s, A("add"))
                    norm(dveA, a, oA[:, :], x1[:, par, :])
                if r is not None:
                    dve.wait_ge(peR.sem, peR.at(r, "pos"))
                    pos = pX[:, D + 2 * NE:D + 3 * NE]
                    sl = slot[:, bass.ds(r, 1), :].rearrange("p r e -> p (r e)")
                    eqr = eq[:, bass.ds(r, 1), :, :].rearrange("p r k e -> p (r k) e")
                    dve.tensor_tensor(sl, pos, eoff[:, :], ALU.add).then_inc(t, 1)
                    dve.tensor_tensor(posg[:, :], pos, earlier[:, :], ALU.add).then_inc(t, 1)
                if b is not None:
                    probs_T(b, 3)
                if r is not None:
                    dve.wait_ge(t, R("posg"))
                    dve.tensor_scalar(fits[:, :], posg[:, :], float(CAP), None, ALU.is_lt).then_inc(t, 1)
                    dve.wait_ge(t, R("fits"))
                    dve.tensor_tensor(rank[:, :], rk[:, :], fits[:, :], ALU.mult).then_inc(t, 1)
                    dve.scalar_tensor_tensor(x2[:, par, D:XW],
                                             ew[:, :], ri[:, 0:1], fits[:, :], ALU.mult, ALU.mult).then_inc(t, 1)
                    dve.tensor_tensor(seen[:, :], seen[:, :], pickb[:, :], ALU.add).then_inc(t, 1)
                    dve.wait_ge(t, R("rank"))
                    dve.tensor_tensor(eqr, rank[:, :].unsqueeze(1).to_broadcast([P, TOPK, NE]), rankc[:, :, :],
                                      ALU.is_equal).then_inc(t, 1)
                    dve.wait_ge(t, R("eq"))
                    dve.scalar_tensor_tensor(eqs[:, :, :], sl.unsqueeze(1).to_broadcast([P, TOPK, NE]), -FAR,
                                             eqr, ALU.add, ALU.mult).then_inc(t, 1)
                    dve.wait_ge(t, R("eqs"))
                    dve.tensor_reduce(idf[:, :], eqs[:, :, :], AX_X, ALU.add).then_inc(t, 1)
                    dve.wait_ge(t, R("sum"))
                    dve.tensor_scalar(xidx[:, par, :], idf[:, :], FAR, None, ALU.add).then_inc(t, 1)
                if b is not None:
                    B, v = (lambda name: dveB.at(b, name)), dveB.sem
                    dve.wait_ge(actB.sem, actB.at(b, "e3"))
                    dve.reciprocal(rden[:, :], den[:, :]).then_inc(v, 1)
                    dve.wait_ge(v, B("inv"))
                    dve.tensor_copy(rX[:, :, :], rden[:, :].unsqueeze(2).to_broadcast([P, NH, HD])).then_inc(v, 1)
                    dve.wait_ge(actB.sem, actB.at(b, "rT"))
                    dve.tensor_tensor(flat2(oT), pO[:, 0:D], flat2(rT), ALU.mult).then_inc(v, 1)
                    dve.wait_ge(peB.sem, peB.at(b, "y"))
                    dve.tensor_tensor(yB[:, :], pW[:, 0:D], x1[:, 1 - par, :], ALU.add).then_inc(v, 1)
                    dve.wait_ge(v, B("add"))
                    norm(dveB, b, yB[:, :], x2[:, 1 - par, 0:D],
                         lambda: (dve.wait_ge(scattered[1 - par], 16 * TOPK // 2 * (b - (1 - par))),
                                  dve.wait_ge(kept, b - 1)) if there(b - 2) else None)

            def tables(h):
                H, s = (lambda name: dveH.at(h, name)), dveH.sem
                dve.wait_ge(peH.sem, peH.at(h, "count"))
                cnt = pW[0:NE, NE:NE + 1]
                dve.tensor_scalar(room[:, :], gone[:, :], -1.0, float(CAP), ALU.mult, ALU.add).then_inc(s, 1)
                dve.wait_ge(s, H("room"))
                dve.tensor_tensor(took[:, :], cnt, room[:, :], ALU.min).then_inc(s, 1)
                dve.wait_ge(s, H("min"))
                dve.tensor_scalar(took[:, :], took[:, :], 0.0, None, ALU.max).then_inc(s, 1)
                dve.wait_ge(s, H("took"))
                dve.tensor_scalar(junk[:, :], blk128(QT), took[:, 0:1], 0.0, ALU.is_lt, ALU.add,
                                  accum_out=nblk[:, :]).then_inc(s, 1)
                dve.wait_ge(s, H("nblk"))
                dve.tensor_copy(nblkb[:, :], nblk[:, :]).then_inc(s, 1)
                dve.tensor_scalar(skipb[:, :], nblk[:, :], -1.0, float(STRIDE // P), ALU.mult, ALU.add).then_inc(s, 1)
                dve.tensor_scalar(nund[:, :], under[:, :], nblk[:, 0:1], None, ALU.mult).then_inc(s, 1)
                dve.tensor_tensor(gone[:, :], gone[:, :], cnt, ALU.add).then_inc(s, 1)
                dve.tensor_tensor(earlier[:, :], earlier[:, :], pW[:, 0:NE], ALU.add).then_inc(s, 1)
                dve.memset(seen[:, :], 0.0).then_inc(s, 1)
                dve.wait_ge(peH.sem, peH.at(h, "place"))
                dve.tensor_copy(cum[:, :], pW[0:NE, NE + 1:NE + 2]).then_inc(s, 1)
                dve.wait_ge(s, H("cum"))
                dve.tensor_scalar(past[:, :], blk[:, :], cum[:, 0:1], None, ALU.is_ge).then_inc(s, 1)
                dve.scalar_tensor_tensor(shift_y[:, h, :], pW[:, 64:64 + NE], float(P), eoff[:, :],
                                         ALU.mult, ALU.subtract).then_inc(s, 1)
                dve.tensor_tensor(tab_p[0:1, h, :], pW[0:1, 96:96 + NE], eoff[0:1, :], ALU.add).then_inc(s, 1)
                dve.tensor_scalar(tjunk[:, :], blk4(), pW[0:1, 130:131], 0.0, ALU.is_lt, ALU.add,
                                  accum_out=rnds[:, :]).then_inc(s, 1)
                dve.wait_ge(s, H("n"))
                dve.tensor_scalar(tab_n[0:1, h:h + 1], rnds[:, :], 1.0, None, ALU.max).then_inc(s, 1)
                dve.wait_ge(s, H("n2"))
                dve.tensor_scalar(tab_t[0:1, h:h + 1], tab_n[0:1, h:h + 1], -16.0 * UN, 16.0 * (MAXB + 1),
                                  ALU.mult, ALU.add).then_inc(s, 1)
                dve.wait_ge(peH.sem, peH.at(h, "table"))
                dve.tensor_scalar(tab_f[0:1, 0, :], pW[0:1, 160:160 + TAB], float(NE - 1), None, ALU.min
                                  ).then_inc(s, 1)
                dve.tensor_tensor(tab_f[0:1, 1, :], pW[0:1, 300:300 + TAB], blk[0:1, :], ALU.add).then_inc(s, 1)
                dve.wait_ge(s, H("fe"))
                for tab, first, times, plus in ((tab_g, LEAD, 4 * INTER, 0), (tab_w, LEAD, 1, D), (tab_d, 0, D, 0)):
                    dve.tensor_scalar(tab[0:1, h, first:first + TAB], tab_f[0:1, 0, :], float(times), float(plus),
                                      ALU.mult, ALU.add).then_inc(s, 1)
                dve.wait_ge(s, H("fx"))
                dve.tensor_scalar(tab_x[0:1, h, LEAD:LEAD + TAB], tab_f[0:1, 1, :], float(P), None, ALU.mult
                                  ).then_inc(s, 1)

            def blk128(n):
                return thr[:, 0:n]

            def blk4():
                return blk[0:1, 0:MAXB:UN]

            three_stages(dve, step, tables)

            for h in range(PARTS):
                rounds = dve.value_load(tab_n[0:1, h:h + 1], min_val=1, max_val=MAXB // UN)
                tail = dve.value_load(tab_t[0:1, h:h + 1], min_val=16, max_val=16 * (MAXB + 1))

                for k in range(UN // 2):
                    hold(3 + 2 * UN + h * UN + k).then_inc(y_out[h][k], 1)

                def weights(t, u, j, column):
                    dve.wait_ge(xt_in[h][u % UN], 16 * (j + (u // UN + 1)))
                    dve.tensor_copy(wcol[:, u % UN:u % UN + 1], xt[:, u % UN, bass.ds(column, 1)]
                                    ).then_inc(dveF[h]["w"], 1)

                def gate(t, u):
                    if there(t - 2):
                        dve.wait_ge(peF[h]["hT"], t - 1)
                    dve.wait_ge(actF[h]["th"], t + 1)
                    ps = bank[2 + u % 2]
                    dve.scalar_tensor_tensor(tg[:, u % 2, :], th[:, u % 2, :], 1.0, ps[:, 0:INTER], ALU.add, ALU.mult
                                             ).then_inc(dveF[h]["tg"], 1)
                    dve.wait_ge(dveF[h]["tg"], t + 1)
                    dve.tensor_tensor(hg[:, u % 2, :], tg[:, u % 2, :], ps[:, INTER:2 * INTER], ALU.mult
                                      ).then_inc(dveF[h]["hg"], 1)

                def h_T(t, u):
                    dve.wait_ge(peF[h]["hT"], t + 1)
                    dve.tensor_copy(hT[:, u % 2, :], bank[4 + u % 2][0:INTER, 0:P]).then_inc(dveF[h]["hT"], 1)

                def y(t, u, j):
                    dve.wait_ge(peF[h]["y"], t + 1)
                    if u % 2 == 0:
                        dve.wait_ge(y_out[h][u // 2], 16 * j + 1)
                    dve.wait_ge(dveF[h]["w"], t + 1)
                    dve.tensor_scalar(ys[:, u, :], bank[6 + u % 2][:, 0:D], wcol[:, u:u + 1], 0.5,
                                      ALU.mult, ALU.mult).then_inc(dveF[h]["y"], 1)

                for t, column in zip((0, 1), four(ET.DVE, tab_w[0:1, h, 0:UN], XW - 1)[LEAD:]):
                    weights(t, t, 0, column)
                for t in range(2):
                    gate(t, t)
                h_T(0, 0)
                with dve.Fori(0, rounds) as j:
                    columns = four(ET.DVE, tab_w[0:1, h, bass.ds(j * UN + UN, UN)], XW - 1)
                    for u in range(UN):
                        t = j * UN + u
                        weights(t + 2, u + 2, j, columns[u])
                        gate(t + 2, u)
                        h_T(t + 1, u + 1)
                        y(t, u, j)
                for u in range(UN):
                    dve.wait_ge(xt_in[h][u], rounds * 16 + (32 if u < 2 else 16))
                    hold(1 + u)
                dve.wait_ge(peF[h]["xT"], rounds * UN + AHEAD)
                hold(1 + UN).then_inc(xt_free, 1)
                for k in range(UN // 2):
                    dve.wait_ge(y_out[h][k], rounds * 16 + 1)
                    hold(2 + UN + k)
                dve.wait_ge(tail_zero[h], tail)
                hold(2 + 2 * UN).then_inc(drained, 1)

            for b in range(NB):
                dve.wait_ge(added[b], 16 * TOPK)
                if b >= 2:
                    dve.wait_ge(stored[b % 2], 16 * NG * (b // 2))
                norm(dveC, b, xs[:, b, :], fin[:, b % 2, :])


_INS = ["x", "ctx_512", "L0_xattn_Wq", "L0_xattn_Wkv_expand", "L0_xattn_Wout", "L0_ffn_gate_w",
        "L0_ffn_w_gate", "L0_ffn_w_up", "L0_ffn_w_down"]


def kernel(**inputs):
    import numpy as np
    import concourse.bacc as bacc
    from concourse.bass_utils import run_bass_kernel_spmd

    nc = bacc.Bacc("TRN2", target_bir_lowering=False, num_devices=1)
    arrays, args = {}, []
    for name in _INS:
        a = np.ascontiguousarray(inputs[name])
        arrays[f"in_{name}"] = a
        args.append(nc.dram_tensor(f"in_{name}", a.shape, mybir.dt.from_np(a.dtype), kind="ExternalInput").ap())
    out = nc.dram_tensor("out_0", (NB, P, D), F32, kind="ExternalOutput").ap()
    build(nc, *args, out)
    r = run_bass_kernel_spmd(nc, [arrays], core_ids=[0])
    return r.results[0]["out_0"]
```

```python
from contextlib import ExitStack

import concourse.bass as bass
from concourse import mybir

F32 = mybir.dt.float32
BF16 = mybir.dt.bfloat16
I32 = mybir.dt.int32
ALU = mybir.AluOpType
ACT = mybir.ActivationFunctionType
ET = mybir.EngineType
AX_X = mybir.AxisListType.X

P = 128
NB, D = 16, 256
NH, HD = 16, 16
SEG, DIL = 64, 2
GR = SEG // DIL
NG = P // GR
PAIRS = D // 32
LAT = 64
NE, INTER, TOPK = 32, 96, 8
CAP = 2 * (NB * P * TOPK // NE)
XW = D + NE
PART = (10, NB - 10)
PARTS = len(PART)
START = [sum(PART[:h]) for h in range(PARTS + 1)]
PT_TOK = max(PART) * P
QT = min(CAP, PT_TOK) // P
STRIDE = (QT + 1) * P
MAXB = PT_TOK * TOPK // P + NE
UN = 8
YS = 4
AHEAD = 3
TAB = MAXB + 2 * UN
LEAD = UN - 2
IDLE = 2 * UN + 2
XG_ROWS = NE * STRIDE + IDLE * P
Y_ROWS = (MAXB + 2) * P
Y_ZERO = (MAXB + 1) * P
FAR = 65536.0
EPS = 1e-5
LOW = -87.3
FIRST_CONST = 3
B_CONST = FIRST_CONST + 23
N_CONST = 53
MAGIC = 1597463007.0

assert MAXB % UN == 0


class Steps:

    def __init__(self, sem, names):
        self.sem, self.names = sem, names.split()

    def at(self, tile, name):
        return len(self.names) * tile + self.names.index(name) + 1


def there(tile):
    return not isinstance(tile, int) or tile >= 0


ROOT = "veps half shift seed n1 n2 n3 z c1 c2 c3 c4"


def first_token(g):
    return SEG * (g // DIL) + g % DIL


def build(nc, x, ctx_in, wq, wkv, wout, gate_w, w_gate, w_up, w_down, out):
    stack = ExitStack()
    with stack:
        def sb(name, shape, dt=F32):
            return stack.enter_context(nc.sbuf_tensor(name, shape, dt))

        def sem(name):
            return stack.enter_context(nc.semaphore(name))

        xg = [nc.dram_tensor(f"queues{h}", (XG_ROWS, XW), F32).ap() for h in range(PARTS)]
        yg = [nc.dram_tensor(f"results{h}", (Y_ROWS, D), F32).ap() for h in range(PARTS)]

        bank = [stack.enter_context(nc.psum_tensor(f"bank{i}", [P, 512], F32)) for i in range(8)]
        pA, pC, pX, pO, pW = bank[0], bank[1], bank[2], bank[3], bank[4]
        pS = [bank[5], bank[6]]
        pT = [bank[7], pW]

        xs = sb("xs", [P, NB, D])
        x1 = sb("x1", [P, 2, D])
        x2 = sb("x2", [P, 2, XW])
        ct = sb("ct", [P, 2, P])
        cs = sb("cs", [P, NB, LAT])
        wgu = sb("wgu", [P, NE * 2 * 2 * INTER])
        wd = sb("wd", [INTER, NE * D])
        gw = sb("gw", [P, 2, NE])
        wqT = sb("wqT", [P, 2, D])
        woT = sb("woT", [P, 2, D])
        wkvT = sb("wkvT", [P, 2 * D])
        ident = sb("ident", [P, P])
        identb = sb("identb", [P, P], BF16)
        causal = sb("causal", [P, P], BF16)
        before = sb("before", [P, P], BF16)
        onesb = sb("onesb", [P, P], BF16)
        ones32 = sb("ones32", [P, NE])
        own = sb("own", [P, D])
        qmask = sb("qmask", [P, 2])
        rank_i = sb("rank_i", [P, TOPK * NE], I32)
        rankc = sb("rankc", [P, TOPK, NE])
        eoff_i = sb("eoff_i", [P, NE], I32)
        eoff = sb("eoff", [P, NE])
        eoff_far = sb("eoff_far", [P, NE])
        zrow_i = sb("zrow_i", [P, 1], I32)
        zrow = sb("zrow", [P, 1])
        blk_i = sb("blk_i", [NE, TAB], I32)
        blk = sb("blk", [NE, TAB])
        thr_i = sb("thr_i", [NE, QT], I32)
        thr = sb("thr", [NE, QT])
        upto = sb("upto", [NE, NE], BF16)
        under = sb("under", [NE, NE], BF16)
        zeros = sb("zeros", [P, XW])
        gm = sb("gm", [P, 2, D])
        gT = sb("gT", [P, D])
        sA = sb("sA", [P, PAIRS, GR])
        eA = sb("eA", [P, PAIRS, GR])
        eAT = sb("eAT", [P, PAIRS, GR])
        oA = sb("oA", [P, D])
        mA = sb("mA", [P, PAIRS])
        dA = sb("dA", [P, PAIRS])
        rA = sb("rA", [P, PAIRS])
        cT = sb("cT", [P, P])
        kP = sb("kP", [P, 2, 2, 4, P])
        vX = sb("vX", [P, 2, PAIRS, 4, HD])
        xT = sb("xT", [P, 2, 2, P])
        qS = sb("qS", [P, 2, 2, P])
        nmax = sb("nmax", [P, NH])
        den = sb("den", [P, NH])
        rden = sb("rden", [P, NH])
        pr = sb("pr", [P, 2, 4, P])
        prT = sb("prT", [P, 2, 4, P])
        rX = sb("rX", [P, NH, HD])
        rT = sb("rT", [P, 2, P])
        oT = sb("oT", [P, 2, P])
        yB = sb("yB", [P, D])
        top = sb("top", [P, 1])
        lc = sb("lc", [P, NE])
        m8 = sb("m8", [P, TOPK])
        lr = sb("lr", [P, NE])
        pick = sb("pick", [P, NE])
        pickb = sb("pickb", [P, NE], BF16)
        seen = sb("seen", [P, NE], BF16)
        er = sb("er", [P, NE])
        rk = sb("rk", [P, NE])
        ew = sb("ew", [P, NE])
        es = sb("es", [P, 1])
        ri = sb("ri", [P, 1])
        posg = sb("posg", [P, NE])
        fits = sb("fits", [P, NE])
        earlier = sb("earlier", [P, NE])
        slot = sb("slot", [P, NB, NE])
        rank = sb("rank", [P, NE])
        eq = sb("eq", [P, NB, TOPK, NE], BF16)
        eqs = sb("eqs", [P, TOPK, NE])
        idf = sb("idf", [P, TOPK])
        pscrap = sb("pscrap", [1, 1])
        farc = sb("farc", [P, TOPK])
        xidx = sb("xidx", [P, 2, TOPK], I32)
        yidx = sb("yidx", [P, NB, TOPK], I32)
        slz = sb("slz", [P, 2, NE])
        scrap = sb("scrap", [1, 3 + (2 + PARTS) * UN])
        st6 = sb("st6", [P, 2, 6])
        mv = sb("mv", [P, 2, 2])
        ve = sb("ve", [P, 2])
        nh = sb("nh", [P, 2])
        half = sb("half", [P, 2], I32)
        ry = sb("ry", [P, 2])
        rt = sb("rt", [P, 2])
        rz = sb("rz", [P, 2])
        gone = sb("gone", [NE, 1])
        room = sb("room", [NE, 1])
        took = sb("took", [NE, 1])
        nblk = sb("nblk", [NE, 1])
        nblkb = sb("nblkb", [NE, 1], BF16)
        skipb = sb("skipb", [NE, 1], BF16)
        nund = sb("nund", [NE, NE], BF16)
        junk = sb("junk", [NE, QT])
        cum = sb("cum", [NE, 1])
        past = sb("past", [NE, TAB], BF16)
        tjunk = sb("tjunk", [1, MAXB // UN])
        rnds = sb("rnds", [1, 1])
        tab_g = sb("tab_g", [1, PARTS, TAB + 2 * LEAD], I32)
        tab_w = sb("tab_w", [1, PARTS, TAB + 2 * LEAD], I32)
        tab_x = sb("tab_x", [1, PARTS, TAB + 2 * LEAD], I32)
        tab_d = sb("tab_d", [1, PARTS, TAB], I32)
        tab_p = sb("tab_p", [1, PARTS, NE], I32)
        tab_n = sb("tab_n", [1, PARTS], I32)
        tab_t = sb("tab_t", [1, PARTS], I32)
        tab_f = sb("tab_f", [1, 2, TAB])
        shift_y = sb("shift_y", [P, PARTS, NE])
        xt = sb("xt", [P, UN, XW])
        xtT = sb("xtT", [P, 2, 2, P])
        th = sb("th", [P, 2, INTER])
        tg = sb("tg", [P, 2, INTER])
        hg = sb("hg", [P, 2, INTER])
        hT = sb("hT", [INTER, 2, P])
        wcol = sb("wcol", [P, UN])
        ys = sb("ys", [P, UN, D])
        fin = sb("fin", [P, 2, D])

        x_in = [sem("x_in0"), sem("x_in1")]
        ctx_loaded = [sem("ctx_loaded0"), sem("ctx_loaded1")]
        small_loaded = sem("small_loaded")
        experts_loaded = sem("experts_loaded")
        consts = sem("consts")
        wt_ps, wt_sb = sem("wt_ps"), sem("wt_sb")
        peA = Steps(sem("peA"), "cT s o kv x1T q")
        actA = Steps(sem("actA"), "cT e v q")
        actX = Steps(sem("actX"), "xT")
        dveA = Steps(sem("dveA"), "gT max sub sum inv turn scale add stats aggr")
        poolA = Steps(sem("poolA"), "gm ct")
        kept = sem("kept")
        peS = Steps(sem("peS"), "S0 S1")
        peB = Steps(sem("peB"), "T0 S2 V0 T1 S3 V1 T2 V2 T3 V3 rT y")
        actE = Steps(sem("actE"), "e0")
        actB = Steps(sem("actB"), "e1 T0 T1 e2 T2 e3 T3 rT")
        dveM = Steps(sem("dveM"), "m0")
        dveB = Steps(sem("dveB"), "m1 m2 m3 inv rX oT")
        dveY = Steps(sem("dveY"), "add stats aggr")
        dveN = Steps(sem("dveN"), ROOT + " x1 x2")
        peR = Steps(sem("peR"), "x2T lg pos")
        actR = Steps(sem("actR"), "e")
        dveR = Steps(sem("dveR"), "top clamp m8 mr pick pickb rk rk2 ew ri slot posg fits rank w seen eq")
        poolR = Steps(sem("poolR"), "eqs sum16 sum8 sum4 sum2 sum1 far held idx")
        peH = Steps(sem("peH"), "count place table")
        dveH = Steps(sem("dveH"), "room min took nblk nblkb skipb nund gone earlier reset cum past sh tp n n2 tt fe fx tg tw td tx")
        peF = [{n: sem(f"peF{h}_{n}") for n in ("xT", "gu", "hT", "y")} for h in range(PARTS)]
        actF = [{n: sem(f"actF{h}_{n}") for n in ("xT", "th")} for h in range(PARTS)]
        dveF = [{n: sem(f"dveF{h}_{n}") for n in ("w", "tg", "hg", "hT", "y")} for h in range(PARTS)]
        drained = sem("drained")
        xt_free = sem("xt_free")
        poolY = Steps(sem("poolY"), "slot row eqs sum16 sum8 sum4 sum2 sum1 idx")
        dveC = Steps(sem("dveC"), f"s0 a0 s1 a1 {ROOT} y0 y1")
        scattered = [sem(f"scattered{k}") for k in range(2)]
        idle_zero = sem("idle_zero")
        pad_zero = [sem(f"pad_zero{h}") for h in range(PARTS)]
        tail_zero = [sem(f"tail_zero{h}") for h in range(PARTS)]
        xt_in = [[sem(f"xt_in{h}_{k}") for k in range(UN)] for h in range(PARTS)]
        y_out = [[sem(f"y_out{h}_{k}") for k in range(UN // YS)] for h in range(PARTS)]
        added = [sem(f"added{b}") for b in range(NB)]
        stored = [sem(f"stored{k}") for k in range(2)]

        gate_v = w_gate.rearrange("e (p k) i -> p e (k i)", k=2)
        up_v = w_up.rearrange("e (p k) i -> p e (k i)", k=2)
        down_v = w_down.rearrange("e i d -> i e d")
        wgu_v = wgu[:, :].rearrange("p (e g k) -> p e g k", e=NE, g=2)

        block = stack.enter_context(nc.Block())

        def three_stages(eng, step, tables):
            def at(k, par):
                if isinstance(k, int):
                    step(*(t if 0 <= t < NB else None for t in (k, k - 1, k - 2)), par)
                else:
                    step(k, k - 1, k - 2, par)

            for k in range(4):
                at(k, k % 2)
            pairs = PART[0] // 2 - 1
            with eng.Fori(0, pairs) as i:
                at(2 * i + 4, 0)
                at(2 * i + 5, 1)
            for k in range(4 + 2 * pairs, PART[0] + 2):
                at(k, k % 2)
            tables(0)
            for k in range(PART[0] + 2, NB + 2):
                at(k, k % 2)
            tables(1)

        def neighbours(engine, entries, most):
            return nc.values_load_multi_w_load_instructions(
                entries, engines=(engine,), min_val=0, max_val=most,
                skip_runtime_bounds_check_because="the tables hold rows and columns of these arrays only")[1]

        def pad_queues(eng, h):
            with eng.Fori(0, NE) as e:
                r = eng.value_load(tab_p[0:1, h, bass.ds(e, 1)], min_val=0, max_val=NE * STRIDE - P)
                eng.dma_start(xg[h][bass.ds(r, P), :], zeros[:, :]).then_inc(pad_zero[h], 16)
            rounds = eng.value_load(tab_n[0:1, h:h + 1], min_val=1, max_val=MAXB // UN)
            with eng.Fori(rounds * UN, MAXB + 2) as t:
                eng.dma_start(yg[h][bass.ds(t * P, P), :], zeros[:, 0:D]).then_inc(tail_zero[h], 16)

        @block.sync
        def _(sp):
            def load_x(g, b0, b1, s):
                t0 = first_token(g)
                sp.dma_start(xs[GR * g:GR * (g + 1), b0:b1, :],
                             x[b0:b1, t0:t0 + DIL * (GR - 1) + 1:DIL, :].rearrange("b i d -> i b d")
                             ).then_inc(s, 16)

            for g in range(NG):
                load_x(g, 0, 2, x_in[0])
            sp.dma_start(cs[:, 0:2, :], ctx_in[0:2].rearrange("b s l -> s b l")).then_inc(ctx_loaded[0], 16)
            sp.dma_start(cs[:, 2:NB, :], ctx_in[2:NB].rearrange("b s l -> s b l")).then_inc(ctx_loaded[1], 16)
            for g in range(NG):
                load_x(g, 2, NB, x_in[1])
            for e in range(0, NE, 8):
                sp.dma_start(wgu_v[:, e:e + 8, 0, :], gate_v[:, e:e + 8, :]).then_inc(experts_loaded, 16)
                sp.dma_start(wgu_v[:, e:e + 8, 1, :], up_v[:, e:e + 8, :]).then_inc(experts_loaded, 16)
                sp.dma_start(wd[:, e * D:(e + 8) * D].rearrange("i (e d) -> i e d", d=D),
                             down_v[:, e:e + 8, :]).then_inc(experts_loaded, 16)

            sp.wait_ge(consts, N_CONST)
            for h in range(PARTS):
                for k in range(IDLE):
                    r = NE * STRIDE + k * P
                    sp.dma_start(xg[h][r:r + P, :], zeros[:, :]).then_inc(idle_zero, 16)
            sp.wait_ge(dveH.sem, dveH.at(0, "tx"))
            pad_queues(sp, 0)
            for h in range(PARTS):
                if h:
                    sp.wait_ge(dveH.sem, dveH.at(h, "tx"))
                rounds = sp.value_load(tab_n[0:1, h:h + 1], min_val=1, max_val=MAXB // UN)
                for k in range(2):
                    sp.wait_ge(scattered[k], 16 * TOPK * ((START[h + 1] + 1 - k) // 2))
                sp.wait_ge(pad_zero[h], 16 * NE)
                sp.wait_ge(idle_zero, 16 * IDLE * PARTS)
                if h:
                    sp.wait_ge(xt_free, h)

                def load_block(t, s, row):
                    sp.dma_start(xt[:, s, :], xg[h][bass.ds(row, P), :]).then_inc(xt_in[h][s], 16)

                def rows_of(first):
                    return neighbours(ET.SP, tab_x[0:1, h, bass.ds(first, UN)], XG_ROWS - P)

                for t, row in zip((0, 1), rows_of(0)[LEAD:]):
                    load_block(t, t, row)
                for t, row in zip(range(2, UN + 2), rows_of(UN)):
                    if t >= UN:
                        sp.wait_ge(peF[h]["xT"], t - UN + 1)
                        sp.wait_ge(dveF[h]["w"], t - UN + 1)
                    load_block(t, t % UN, row)
                with sp.Fori(0, rounds) as j:
                    rows = rows_of(j * UN + 2 * UN)
                    for u in range(UN):
                        t = j * UN + u
                        turned, written = sp.snap(t + 3), sp.snap(t + 1)
                        sp.wait_ge(peF[h]["xT"], turned)
                        sp.wait_ge(dveF[h]["w"], turned)
                        load_block(t, (u + 2) % UN, rows[u])
                        if u % YS == YS - 1:
                            first = sp.snap((t - (YS - 1)) * P)
                            sp.wait_ge(dveF[h]["y"], written)
                            sp.dma_start(yg[h][bass.ds(first, YS * P), :].rearrange("(s p) d -> p s d", p=P),
                                         ys[:, u - YS + 1:u + 1, :]).then_inc(y_out[h][u // YS], 16)

            for b in range(NB):
                sp.wait_ge(dveC.sem, dveC.at(b // 2, f"y{b % 2}"))
                for g in range(NG):
                    t0 = first_token(g)
                    sp.dma_start(out[b, t0:t0 + DIL * (GR - 1) + 1:DIL, :],
                                 fin[GR * g:GR * (g + 1), b % 2, :]).then_inc(stored[b % 2], 16)
            for k in range(2):
                sp.wait_ge(stored[k], 16 * NG * NB // 2)

        @block.gpsimd
        def _(pool):
            n = 0

            def put(op, *args, **kw):
                nonlocal n
                if n:
                    pool.wait_ge(consts, n)
                op(*args, **kw).then_inc(consts, 1)
                n += 1

            def picked_rows(steps, t, rows, chosen):
                s = steps.sem
                pool.tensor_tensor(eqs[:, :, :], rows.unsqueeze(1).to_broadcast([P, TOPK, NE]), chosen,
                                   ALU.mult).then_inc(s, 1)
                for n, before_it in ((16, "eqs"), (8, "sum16"), (4, "sum8"), (2, "sum4"), (1, "sum2")):
                    pool.wait_ge(s, steps.at(t, before_it))
                    pool.tensor_tensor(eqs[:, :, 0:n], eqs[:, :, 0:n], eqs[:, :, n:2 * n], ALU.add).then_inc(s, 1)
                pool.wait_ge(s, steps.at(t, "sum1"))

            def mask_x(a, par):
                if isinstance(a, int) and a in (0, 2):
                    pool.wait_ge(x_in[a // 2], 16 * NG)
                    pool.wait_ge(ctx_loaded[a // 2], 16)
                if there(a - 2):
                    pool.wait_ge(peA.sem, peA.at(a - 2, "o"))
                pool.tensor_tensor(gm[:, par, :], xs[:, bass.ds(a, 1), :].rearrange("p a d -> p (a d)"),
                                   own[:, :], ALU.mult).then_inc(poolA.sem, 1)
                pool.tensor_copy(ct[:, par, 0:LAT], cs[:, bass.ds(a, 1), :].rearrange("p a d -> p (a d)")
                                 ).then_inc(poolA.sem, 1)

            put(pool.memset, ident[:, :], 0.0)
            put(pool.affine_select, out=ident[:, :], in_=ident[:, :], compare_op=ALU.not_equal, fill=1.0,
                base=0, pattern=[[-1, P]], channel_multiplier=1)
            put(pool.memset, wkvT[:, :], 0.0)
            assert n == FIRST_CONST
            put(pool.memset, own[:, :], 0.0)
            own_v = own[:, :].rearrange("p (j s c) -> p j s c", s=DIL, c=HD)
            for g in range(NG):
                put(pool.memset, own_v[GR * g:GR * (g + 1), :, g % DIL, :], 1.0)
            put(pool.memset, ct[:, :, :], 0.0)
            pool.wait_ge(consts, n)
            mask_x(0, 0)
            put(pool.memset, kP[:, :, :, :, :].rearrange("p a m q k -> p (a m q k)"), 0.0)
            put(pool.memset, vX[:, :, :, :, :], 0.0)
            put(pool.memset, causal[:, :], 0.0)
            put(pool.memset, qmask[:, :], float(HD) ** -0.5)
            put(pool.tensor_copy, identb[:, :], ident[:, :])
            for g in range(NG):
                rows = slice(GR * g, GR * (g + 1))
                for k, most in ((0, HD - 1), (1, -HD)):
                    put(pool.affine_select, out=qmask[rows, k:k + 1], in_=qmask[rows, k:k + 1],
                        compare_op=ALU.is_ge, fill=0.0, base=most, pattern=[[0, 1]],
                        channel_multiplier=-1 if k == 0 else 1)
                put(pool.affine_select, out=causal[rows, :], in_=causal[rows, :], compare_op=ALU.is_ge,
                    fill=-3e38, base=first_token(g), pattern=[[-1, P]], channel_multiplier=DIL)
            assert n == B_CONST, n
            pool.wait_ge(consts, n)

            def late_constants():
                put(pool.memset, zeros[:, :], 0.0)
                put(pool.memset, onesb[:, :], 1.0)
                put(pool.memset, ones32[:, :], 1.0)
                put(pool.memset, earlier[:, :], 0.0)
                put(pool.memset, gone[:, :], 0.0)
                put(pool.memset, seen[:, :], 0.0)
                for tab in (tab_g, tab_w, tab_x):
                    put(pool.memset, tab[:, :, :], 0)
                for g in range(NG):
                    rows = slice(GR * g, GR * (g + 1))
                    put(pool.affine_select, out=before[rows, :].rearrange("p (a b i) -> p a b i", a=2, b=2),
                                           in_=onesb[rows, :].rearrange("p (a b i) -> p a b i", a=2, b=2),
                                           compare_op=ALU.is_gt, fill=0.0, base=-first_token(g),
                                           pattern=[[SEG, 2], [1, 2], [DIL, GR]], channel_multiplier=-DIL)
                put(pool.affine_select, out=upto[:, :], in_=onesb[0:NE, 0:NE], compare_op=ALU.is_ge, fill=0.0,
                                       base=0, pattern=[[1, NE]], channel_multiplier=-1)
                put(pool.affine_select, out=under[:, :], in_=onesb[0:NE, 0:NE], compare_op=ALU.is_gt, fill=0.0,
                                       base=0, pattern=[[1, NE]], channel_multiplier=-1)
                put(pool.iota, rank_i[:, :], [[1, TOPK], [0, NE]], base=1, channel_multiplier=0)
                put(pool.iota, eoff_i[:, :], [[STRIDE, NE]], base=0, channel_multiplier=0)
                put(pool.iota, zrow_i[:, :], [[0, 1]], base=Y_ZERO, channel_multiplier=1)
                put(pool.iota, blk_i[:, :], [[1, TAB]], base=0, channel_multiplier=0)
                put(pool.iota, thr_i[:, :], [[P, QT]], base=0, channel_multiplier=0)
                put(pool.tensor_copy, rankc[:, :, :].rearrange("p k e -> p (k e)"), rank_i[:, :])
                put(pool.tensor_copy, eoff[:, :], eoff_i[:, :])
                put(pool.memset, farc[:, :], FAR)
                put(pool.tensor_scalar, eoff_far[:, :], eoff_i[:, :], -FAR, None, ALU.add)
                put(pool.tensor_copy, zrow[:, :], zrow_i[:, :])
                put(pool.tensor_copy, blk[:, :], blk_i[:, :])
                put(pool.tensor_copy, thr[:, :], thr_i[:, :])
                assert n == N_CONST, n

            def step(a, b, r, par):
                if isinstance(a, int) and a == 0:
                    mask_x(1, 1)
                    late_constants()
                    pool.wait_ge(consts, n)
                if a is not None and not (isinstance(a, int) and a >= NB - 2):
                    mask_x(a + 2, par)
                if r is not None:
                    pool.wait_ge(dveR.sem, dveR.at(r, "eq"))
                    picked_rows(poolR, r, slot[:, bass.ds(r, 1), :].rearrange("p r e -> p (r e)"),
                                eq[:, bass.ds(r, 1), :, :].rearrange("p r k e -> p (r k) e"))
                    pool.tensor_tensor(idf[:, :], eqs[:, :, 0], farc[:, :], ALU.add).then_inc(poolR.sem, 1)
                    pool.wait_ge(poolR.sem, poolR.at(r, "far"))
                    pool.tensor_tensor(pscrap[0:1, :], farc[0:1, 0:1], farc[0:1, 0:1], ALU.add).then_inc(poolR.sem, 1)
                    pool.tensor_copy(xidx[:, par, :], idf[:, :]).then_inc(poolR.sem, 1)
                    pool.wait_ge(poolR.sem, poolR.at(r, "idx"))
                    pool.tensor_copy(xs[:, bass.ds(r, 1), :].rearrange("p r d -> p (r d)"), x2[:, par, 0:D]
                                     ).then_inc(kept, 1)
                    for k in range(TOPK):
                        pool.indirect_dma_start(
                            xg[1 if isinstance(r, int) and r >= START[1] else 0],
                            bass.IndirectOffsetOnAxis(ap=xidx[:, par, k:k + 1], axis=0),
                            x2[:, par, :], None,
                            bounds_check=last_row, oob_is_err=False).then_inc(scattered[par], 16)

            last_row = pool.to_reg(XG_ROWS - 1)
            three_stages(pool, step, lambda h: None)

            pool.wait_ge(dveH.sem, dveH.at(1, "tx"))
            for h in range(PARTS):
                for b in range(START[h], START[h + 1]):
                    s = poolY.sem
                    pool.tensor_scalar(slz[:, 0, :], slot[:, b, :], zrow[:, 0:1], None, ALU.subtract).then_inc(s, 1)
                    pool.wait_ge(s, poolY.at(b, "slot"))
                    pool.tensor_tensor(slz[:, 1, :], slz[:, 0, :], shift_y[:, h, :], ALU.add).then_inc(s, 1)
                    pool.wait_ge(s, poolY.at(b, "row"))
                    picked_rows(poolY, b, slz[:, 1, :], eq[:, b, :, :])
                    pool.tensor_scalar(yidx[:, b, :], eqs[:, :, 0], zrow[:, 0:1], None, ALU.add).then_inc(s, 1)
                    pool.wait_ge(s, poolY.at(b, "idx"))

            pad_queues(pool, 1)

            for h in range(PARTS):
                pool.wait_ge(kept, START[h + 1])
                pool.wait_ge(drained, h + 1)
                turns = [(k, b) for b in range(START[h], START[h + 1]) for k in range(TOPK)]
                for k, b in sorted(turns, key=lambda kb: (kb[0] + (kb[1] - START[h]) // 2, kb[1])):
                    if k:
                        pool.wait_ge(added[b], 16 * k)
                    pool.indirect_dma_start(
                        xs[:, b, :], None, yg[h],
                        bass.IndirectOffsetOnAxis(ap=yidx[:, b, k:k + 1], axis=0),
                        bounds_check=Y_ROWS - 1, oob_is_err=True, compute_op=ALU.add
                    ).then_inc(added[b], 16)

        @block.tensor
        def _(pe):
            pe.wait_ge(consts, FIRST_CONST)
            pe.wait_ge(small_loaded, 16 * 4)
            for m in range(2):
                for kk in range(2):
                    pe.transpose(bank[4][:, (kk * 2 + m) * P:(kk * 2 + m + 1) * P],
                                 pr[:, 0, :, :].rearrange("p a b -> p (a b)")[:, m * D + kk * P:m * D + kk * P + P],
                                 ident[:, :])
                    ins = pe.transpose(bank[5][:, (kk * 2 + m) * P:(kk * 2 + m + 1) * P],
                                 pr[:, 1, :, :].rearrange("p a b -> p (a b)")[:, m * D + kk * P:m * D + kk * P + P],
                                 ident[:, :])
            for m in range(4):
                ins = pe.transpose(bank[6][0:LAT, m * P:(m + 1) * P],
                                   prT[:, 0, :, :].rearrange("p a b -> p (a b)")[:, m * LAT:(m + 1) * LAT],
                                   ident[:, :])
            ins.then_inc(wt_ps, 1)
            pe.wait_ge(wt_sb, 3)

            def scores(b, g, par):
                m = g // 2
                pe.matmul(pS[g % 2][:, :], identb[:, :],
                          causal[:, :].unsqueeze(1).to_broadcast([P, 4, P]),
                          start=True, stop=False)
                pe.matmul(pS[g % 2][:, :], qS[:, g % 2, m, :], kP[:, par, m, :, :],
                          start=False, stop=True).then_inc((peS if g < 2 else peB).sem, 1)

            def turn_probs(b, g, bank_read):
                exp_done = actB if g else actE
                pe.wait_ge(exp_done.sem, exp_done.at(b, f"e{g}"))
                if bank_read is not None:
                    pe.wait_ge(*bank_read)
                for q in range(4):
                    ins = pe.transpose(pT[g % 2][:, q * P:(q + 1) * P], pr[:, g % 2, q, :], ident[:, :])
                ins.then_inc(peB.sem, 1)

            def values(b, g, par):
                pe.wait_ge(actB.sem, actB.at(b, f"T{g}"))
                m, s = g // 2, g % 2
                for q in range(4):
                    ins = pe.matmul(pO[32 * q:32 * q + 32, m * P:(m + 1) * P],
                                    vX[:, par, 4 * m + q, 2 * s:2 * s + 2, :].rearrange("p a c -> p (a c)"),
                                    prT[:, s, q, :], start=(s == 0), stop=(s == 1),
                                    tile_position=(0, 32 * q))
                ins.then_inc(peB.sem, 1)

            def front(a, par, r=None):
                if there(a - 1):
                    pe.wait_ge(dveA.sem, dveA.at(a - 1, "scale"))
                    pe.wait_ge(actA.sem, actA.at(a - 1, "v"))
                if r is not None:
                    pe.wait_ge(dveR.sem, dveR.at(r, "posg"))
                pe.wait_ge(poolA.sem, poolA.at(a, "ct"))
                pe.wait_ge(dveA.sem, dveA.at(a, "gT"))
                pe.transpose(pC[:, 0:P], ct[:, par, :], ident[:, :]).then_inc(peA.sem, 1)
                for j in range(PAIRS):
                    for g in range(NG):
                        blk32 = gT[GR * g:GR * (g + 1), j * 32:(j + 1) * 32]
                        ins = pe.matmul(pA[GR * g:GR * (g + 1), D + j * 32:D + (j + 1) * 32], blk32, blk32,
                                        start=True, stop=True, tile_position=(GR * g, GR * g))
                ins.then_inc(peA.sem, 1)

            def step(a, b, r, par):
                pb = 1 - par
                if b is not None:
                    turn_probs(b, 0, None)
                    scores(b, 2, pb)
                if a is not None:
                    pe.wait_ge(dveA.sem, dveA.at(a, "turn"))
                if b is not None:
                    if there(b - 1):
                        pe.wait_ge(dveY.sem, dveY.at(b - 1, "add"))
                    values(b, 0, pb)
                if a is not None:
                    for j in range(PAIRS):
                        for g in range(NG):
                            ins = pe.matmul(pA[GR * g:GR * (g + 1), j * 32:(j + 1) * 32],
                                            eAT[GR * g:GR * (g + 1), j, :],
                                            gm[GR * g:GR * (g + 1), par, j * 32:(j + 1) * 32],
                                            start=True, stop=True, tile_position=(GR * g, GR * g))
                    ins.then_inc(peA.sem, 1)
                if b is not None:
                    turn_probs(b, 1, None)
                    scores(b, 3, pb)
                    values(b, 1, pb)
                    turn_probs(b, 2, (actB.sem, actB.at(b, "T0")))
                if a is not None:
                    pe.wait_ge(actA.sem, actA.at(a, "cT"))
                    for m in range(2):
                        pe.matmul(pC[:, m * P:(m + 1) * P], wkvT[:, m * P:(m + 1) * P], cT[:, :],
                                  start=True, stop=True)
                    pe.matmul(pC[:, D:2 * D], cT[:, :], wkvT[:, D:2 * D], start=True, stop=True
                              ).then_inc(peA.sem, 1)
                if a is not None:
                    pe.wait_ge(dveN.sem, dveN.at(a, "x1"))
                    for kk in range(2):
                        ins = pe.transpose(pX[:, kk * P:(kk + 1) * P], x1[:, par, kk * P:(kk + 1) * P], ident[:, :])
                    ins.then_inc(peA.sem, 1)
                if r is not None:
                    pe.wait_ge(dveN.sem, dveN.at(r + 2, "x2"))
                    for kk in range(2):
                        ins = pe.transpose(pX[:, D + kk * P:D + (kk + 1) * P], x2[:, par, kk * P:(kk + 1) * P],
                                           ident[:, :])
                    ins.then_inc(peR.sem, 1)
                if b is not None:
                    values(b, 2, pb)
                if a is not None or r is not None:
                    pe.wait_ge(actX.sem, actX.at(a if a is not None else r + 2, "xT"))
                if r is not None:
                    for kk in range(2):
                        ins = pe.matmul(pA[:, 0:NE], xT[:, 1, kk, :], gw[:, kk, :],
                                        start=(kk == 0), stop=(kk == 1))
                    ins.then_inc(peR.sem, 1)
                if a is not None:
                    for m in range(2):
                        for kk in range(2):
                            ins = pe.matmul(pX[:, m * P:(m + 1) * P], wqT[:, kk, m * P:(m + 1) * P],
                                            xT[:, 0, kk, :], start=(kk == 0), stop=(kk == 1))
                    ins.then_inc(peA.sem, 1)
                if r is not None:
                    pe.wait_ge(dveR.sem, dveR.at(r, "pickb"))
                    pe.matmul(pA[:, NE:2 * NE], before[:, :], pickb[:, :], start=True, stop=False)
                    pe.matmul(pA[:, NE:2 * NE], onesb[:, :], seen[:, :], start=False, stop=True
                              ).then_inc(peR.sem, 1)
                if b is not None:
                    turn_probs(b, 3, (actB.sem, actB.at(b, "T1")))
                if a is not None:
                    pe.wait_ge(actA.sem, actA.at(a, "q"))
                    scores(a, 0, par)
                if a is not None and not (isinstance(a, int) and a == NB - 1):
                    front(a + 1, 1 - par, r)
                if b is not None:
                    values(b, 3, pb)
                if b is not None:
                    pe.wait_ge(dveB.sem, dveB.at(b, "rX"))
                    for m in range(2):
                        ins = pe.transpose(pO[:, D + m * P:D + (m + 1) * P],
                                           rX[:, 8 * m:8 * m + 8, :].rearrange("p h c -> p (h c)"), ident[:, :])
                    ins.then_inc(peB.sem, 1)
                if a is not None:
                    if b is not None:
                        pe.wait_ge(actB.sem, actB.at(b, "e3"))
                    scores(a, 1, par)
                if b is not None:
                    pe.wait_ge(dveB.sem, dveB.at(b, "oT"))
                    for kk in range(2):
                        ins = pe.matmul(pO[:, D:2 * D], oT[:, kk, :], woT[:, kk, :],
                                        start=(kk == 0), stop=(kk == 1))
                    ins.then_inc(peB.sem, 1)

            front(0, 0)
            pe.wait_ge(consts, B_CONST)

            def tables(h):
                pe.wait_ge(dveR.sem, dveR.at(START[h + 1] - 1, "seen"))
                pe.wait_ge(actB.sem, actB.at(min(START[h + 1], NB - 1), "T3"))
                pe.matmul(pW[:, 0:NE], onesb[:, :], seen[:, :], start=True, stop=True)
                pe.matmul(pW[0:NE, NE:NE + 1], seen[:, :], onesb[:, 0:1], start=True, stop=True
                          ).then_inc(peH.sem, 1)
                pe.wait_ge(dveH.sem, dveH.at(h, "earlier"))
                pe.matmul(pW[0:NE, NE + 1:NE + 2], upto[:, :], nblkb[:, :], start=True, stop=True)
                pe.matmul(pW[:, 64:64 + NE], onesb[0:NE, :], nund[:, :], start=True, stop=True)
                pe.matmul(pW[0:1, 96:96 + NE], took[:, :], ident[0:NE, 0:NE], start=True, stop=True)
                pe.matmul(pW[0:1, 130:131], nblkb[:, :], onesb[0:NE, 0:1], start=True, stop=True
                          ).then_inc(peH.sem, 1)
                pe.wait_ge(dveH.sem, dveH.at(h, "n"))
                pe.matmul(pW[0:1, 160:160 + TAB], onesb[0:NE, 0:1], past[:, :], start=True, stop=True)
                pe.matmul(pW[0:1, 300:300 + TAB], skipb[:, :], past[:, :], start=True, stop=True
                          ).then_inc(peH.sem, 1)
                pe.wait_ge(dveH.sem, dveH.at(h, "tx"))

            three_stages(pe, step, tables)

            pe.wait_ge(experts_loaded, 16 * 3 * (NE // 8))
            for h in range(PARTS):
                rounds = pe.value_load(tab_n[0:1, h:h + 1], min_val=1, max_val=MAXB // UN)

                def block_T(t, u, j):
                    s = u % UN
                    pe.wait_ge(xt_in[h][s], 16 * (j + (u // UN + 1)))
                    if there(t - 2):
                        pe.wait_ge(actF[h]["xT"], t - 1)
                    for kk in range(2):
                        ins = pe.transpose(bank[u % 2][:, kk * P:(kk + 1) * P],
                                           xt[:, s, kk:D:2], ident[:, :])
                    ins.then_inc(peF[h]["xT"], 1)

                def gu(t, u, e):
                    pe.wait_ge(actF[h]["xT"], t + 1)
                    if there(t - 2):
                        pe.wait_ge(dveF[h]["hg"], t - 1)
                    for kk in range(2):
                        ins = pe.matmul(bank[2 + u % 2][:, 0:2 * INTER].rearrange("p (g i) -> p g i", g=2),
                                        xtT[:, u % 2, kk, :],
                                        wgu[:, bass.ds(e, 4 * INTER)].rearrange(
                                            "p (g k i) -> p g k i", g=2, k=2)[:, :, kk, :],
                                        start=(kk == 0), stop=(kk == 1))
                    ins.then_inc(peF[h]["gu"], 1)

                def turn_h(t, u):
                    pe.wait_ge(dveF[h]["hg"], t + 1)
                    pe.transpose(bank[4 + u % 2][0:INTER, 0:P], hg[:, u % 2, :], ident[:, :]
                                 ).then_inc(peF[h]["hT"], 1)

                def down(t, u, e):
                    pe.wait_ge(dveF[h]["hT"], t + 1)
                    pe.matmul(bank[6 + u % 2][:, 0:D], hT[:, u % 2, :], wd[:, bass.ds(e, D)],
                              start=True, stop=True).then_inc(peF[h]["y"], 1)

                for t in range(3):
                    block_T(t, t, 0)
                for t, e in zip((0, 1), neighbours(ET.PE, tab_g[0:1, h, 0:UN], (NE - 1) * 4 * INTER)[LEAD:]):
                    gu(t, t, e)
                turn_h(0, 0)
                with pe.Fori(0, rounds) as j:
                    e_gu = neighbours(ET.PE, tab_g[0:1, h, bass.ds(j * UN + UN, UN)], (NE - 1) * 4 * INTER)
                    e_down = neighbours(ET.PE, tab_d[0:1, h, bass.ds(j * UN, UN)], (NE - 1) * D)
                    for u in range(UN):
                        t = j * UN + u
                        block_T(t + 3, u + 3, j)
                        gu(t + 2, u, e_gu[u])
                        turn_h(t + 1, u + 1)
                        down(t, u, e_down[u])

        @block.scalar
        def _(act):
            act.dma_start(pr[:, 0, :, :].rearrange("p a b -> p (a b)").rearrange("p (m d) -> p m d", m=2),
                          wq.rearrange("(m p) d -> p m d", p=P)).then_inc(small_loaded, 16)
            act.dma_start(pr[:, 1, :, :].rearrange("p a b -> p (a b)").rearrange("p (m d) -> p m d", m=2),
                          wout.rearrange("(m p) d -> p m d", p=P)).then_inc(small_loaded, 16)
            act.dma_start(prT[:, 0, 0:2, :].rearrange("p a b -> p (a b)").rearrange("p (m l) -> p m l", m=4),
                          wkv.rearrange("(m p) l -> p m l", p=P)).then_inc(small_loaded, 16)
            act.dma_start(gw[:, :, :], gate_w.rearrange("(k p) e -> p k e", p=P)).then_inc(small_loaded, 16)
            act.wait_ge(consts, FIRST_CONST)
            act.wait_ge(wt_ps, 1)
            act.copy(wqT[:, :, :].rearrange("p a b -> p (a b)"), bank[4][:, :]).then_inc(wt_sb, 1)
            act.copy(woT[:, :, :].rearrange("p a b -> p (a b)"), bank[5][:, :]).then_inc(wt_sb, 1)
            act.copy(wkvT[0:LAT, :], bank[6][0:LAT, :]).then_inc(wt_sb, 1)

            def exps(b, g):
                max_done = dveB if g else dveM
                act.wait_ge(max_done.sem, max_done.at(b, f"m{g}"))
                for q in range(4):
                    hd = 8 * (g // 2) + 2 * q + g % 2
                    ins = act.activation(pr[:, g % 2, q, :], pS[g % 2][:, q * P:(q + 1) * P], ACT.Exp,
                                         bias=nmax[:, 4 * g + q:4 * g + q + 1], accum_out=den[:, hd:hd + 1])
                ins.then_inc((actB if g else actE).sem, 1)

            def probs_T(b, g):
                act.wait_ge(peB.sem, peB.at(b, f"T{g}"))
                act.copy(prT[:, g % 2, :, :].rearrange("p a b -> p (a b)"), pT[g % 2][:, :]).then_inc(actB.sem, 1)

            def flat2(t):
                return t.rearrange("p a b -> p (a b)")

            def exps_A(a):
                act.wait_ge(dveA.sem, dveA.at(a, "sub"))
                act.activation(flat2(eA[:, :, :]), flat2(sA[:, :, :]), ACT.Exp, scale=float(HD) ** -0.5
                               ).then_inc(actA.sem, 1)

            def turned_context(a):
                act.wait_ge(peA.sem, peA.at(a, "cT"))
                act.copy(cT[:, :], pC[:, 0:P]).then_inc(actA.sem, 1)

            def step(a, b, r, par):
                if b is not None:
                    exps(b, 1)
                    probs_T(b, 0)
                    probs_T(b, 1)
                    exps(b, 2)
                if isinstance(a, int) and a == 0:
                    act.wait_ge(consts, B_CONST)
                if b is not None:
                    probs_T(b, 2)
                if a is not None:
                    act.wait_ge(peA.sem, peA.at(a, "kv"))
                    for q in range(4):
                        rows = slice(32 * q, 32 * q + 32)
                        act.copy(kP[rows, par, :, q, :], pC[rows, 0:D].rearrange("p (m k) -> p m k", m=2))
                if a is not None or r is not None:
                    if a is not None:
                        act.wait_ge(peA.sem, peA.at(a, "x1T"))
                    if r is not None:
                        act.wait_ge(peR.sem, peR.at(r, "x2T"))
                    n0, n1 = (0 if a is not None else 1), (2 if r is not None else 1)
                    act.copy(xT[:, n0:n1, :, :].rearrange("p n a b -> p (n a b)"), pX[:, n0 * D:n1 * D]
                             ).then_inc(actX.sem, 1)
                if b is not None:
                    exps(b, 3)
                if r is not None:
                    act.wait_ge(dveR.sem, dveR.at(r, "clamp"))
                    act.activation(er[:, :], lc[:, :], ACT.Exp).then_inc(actR.sem, 1)
                if a is not None:
                    act.copy(vX[:, par, :, 0:4:3, :],
                             pC[:, D:2 * D].rearrange("p (j s c) -> p j s c", s=2, c=HD)).then_inc(actA.sem, 1)
                    act.wait_ge(peA.sem, peA.at(a, "q"))
                    for s in range(2):
                        ins = act.activation(flat2(qS[:, s, :, :]), pX[:, 0:D], ACT.Copy, scale=qmask[:, s:s + 1])
                    ins.then_inc(actA.sem, 1)
                if b is not None:
                    probs_T(b, 3)
                if a is not None and not (isinstance(a, int) and a == NB - 1):
                    turned_context(a + 1)
                if a is not None:
                    exps(a, 0)
                if b is not None:
                    act.wait_ge(peB.sem, peB.at(b, "rT"))
                    act.copy(flat2(rT[:, :, :]), pO[:, D:2 * D]).then_inc(actB.sem, 1)
                if a is not None and not (isinstance(a, int) and a == NB - 1):
                    exps_A(a + 1)

            turned_context(0)
            exps_A(0)
            three_stages(act, step, lambda h: None)

            for h in range(PARTS):
                if h == 0:
                    act.wait_ge(dveH.sem, dveH.at(PARTS - 1, "tx"))
                rounds = act.value_load(tab_n[0:1, h:h + 1], min_val=1, max_val=MAXB // UN)

                def block_T(t, u):
                    act.wait_ge(peF[h]["xT"], t + 1)
                    if there(t - 2):
                        act.wait_ge(peF[h]["gu"], t - 1)
                    act.copy(xtT[:, u % 2, :, :].rearrange("p a b -> p (a b)"), bank[u % 2][:, 0:D]
                             ).then_inc(actF[h]["xT"], 1)

                def tanh(t, u):
                    act.wait_ge(peF[h]["gu"], t + 1)
                    if there(t - 2):
                        act.wait_ge(dveF[h]["tg"], t - 1)
                    act.activation(th[:, u % 2, :], bank[2 + u % 2][:, 0:INTER], ACT.Tanh, scale=0.5
                                   ).then_inc(actF[h]["th"], 1)

                for t in range(3):
                    block_T(t, t)
                for t in range(2):
                    tanh(t, t)
                with act.Fori(0, rounds) as j:
                    for u in range(UN):
                        t = j * UN + u
                        block_T(t + 3, u + 3)
                        tanh(t + 2, u)

        @block.vector
        def _(dve):
            def hold(k=0):
                return dve.memset(scrap[0:1, k:k + 1], 0.0)

            def stats(steps, t, names, i, src):
                dve.bn_stats(st6[:, i, :], src).then_inc(steps.sem, 1)
                dve.wait_ge(steps.sem, steps.at(t, names[0]))
                hold()
                dve.bn_aggr(mv[:, i, :], st6[:, i, :]).then_inc(steps.sem, 1)

            def root(steps, t, i0, i1):
                s, n = steps.sem, slice(i0, i1)
                var = mv[:, n, 1:2].rearrange("p n o -> p (n o)")

                def after(name):
                    dve.wait_ge(s, steps.at(t, name))

                dve.tensor_scalar(ve[:, n], var, EPS, None, ALU.add).then_inc(s, 1)
                dve.tensor_scalar(nh[:, n], var, EPS, -0.5, ALU.add, ALU.mult).then_inc(s, 1)
                after("veps")
                dve.tensor_scalar(half[:, n], ve[:, n].bitcast(I32), 1, None, ALU.arith_shift_right).then_inc(s, 1)
                after("shift")
                dve.tensor_scalar(ry[:, n].bitcast(I32), half[:, n], -1.0, MAGIC, ALU.mult, ALU.add).then_inc(s, 1)
                after("seed")
                dve.tensor_tensor(rt[:, n], ry[:, n], nh[:, n], ALU.mult).then_inc(s, 1)
                after("n1")
                dve.tensor_tensor(rt[:, n], rt[:, n], ry[:, n], ALU.mult).then_inc(s, 1)
                after("n2")
                dve.scalar_tensor_tensor(ry[:, n], rt[:, n], 1.5, ry[:, n], ALU.add, ALU.mult).then_inc(s, 1)
                after("n3")
                dve.tensor_scalar(rz[:, n], ry[:, n], 1.5, None, ALU.mult).then_inc(s, 1)
                dve.tensor_tensor(rt[:, n], ry[:, n], nh[:, n], ALU.mult).then_inc(s, 1)
                after("c1")
                dve.tensor_tensor(rt[:, n], rt[:, n], ry[:, n], ALU.mult).then_inc(s, 1)
                after("c2")
                dve.scalar_tensor_tensor(rt[:, n], rt[:, n], 5.0 / 3.0, rt[:, n], ALU.add, ALU.mult).then_inc(s, 1)
                after("c3")
                dve.scalar_tensor_tensor(rz[:, n], rt[:, n], 1.25, rz[:, n], ALU.add, ALU.mult).then_inc(s, 1)
                after("c4")

            def scaled(dst, src, i):
                return dve.tensor_scalar(dst, src, mv[:, i, 0:1], rz[:, i:i + 1], ALU.subtract, ALU.mult)

            def xrow(t):
                return xs[:, bass.ds(t, 1), 0:D].rearrange("p t d -> p (t d)")

            def flat2(t):
                return t[:, :, :].rearrange("p a b -> p (a b)")

            def maxes(b, g):
                scores_done, steps = (peB if g > 1 else peS), (dveB if g else dveM)
                dve.wait_ge(scores_done.sem, scores_done.at(b, f"S{g}"))
                dve.tensor_reduce(nmax[:, 4 * g:4 * g + 4],
                                  pS[g % 2][:, :].rearrange("p (h k) -> p h k", h=4),
                                  AX_X, ALU.max, negate=True).then_inc(steps.sem, 1)

            def shifted_scores(a):
                dve.wait_ge(peA.sem, peA.at(a, "s"))
                scr = pA[:, D:2 * D].rearrange("p (j k) -> p j k", j=PAIRS)
                dve.tensor_reduce(mA[:, :], scr, AX_X, ALU.max).then_inc(dveA.sem, 1)
                dve.wait_ge(dveA.sem, dveA.at(a, "max"))
                dve.tensor_tensor(sA[:, :, :], scr, mA[:, :].unsqueeze(2).to_broadcast([P, PAIRS, GR]),
                                  ALU.subtract).then_inc(dveA.sem, 1)

            def turn_x(a, par):
                dve.wait_ge(poolA.sem, poolA.at(a, "gm"))
                dve.transpose(gT[:, :], gm[:, par, :]).then_inc(dveA.sem, 1)

            def step(a, b, r, par):
                if a is not None:
                    A, s = (lambda name: dveA.at(a, name)), dveA.sem
                if b is not None:
                    B, v = (lambda name: dveB.at(b, name)), dveB.sem
                if r is not None:
                    R, t = (lambda name: dveR.at(r, name)), dveR.sem
                if b is not None:
                    maxes(b, 1)
                if a is not None:
                    dve.wait_ge(actA.sem, actA.at(a, "e"))
                    dve.tensor_reduce(dA[:, :], eA[:, :, :], AX_X, ALU.add).then_inc(s, 1)
                    dve.wait_ge(s, A("sum"))
                    dve.reciprocal(rA[:, :], dA[:, :]).then_inc(s, 1)
                    dve.transpose(flat2(eAT), flat2(eA)).then_inc(s, 1)
                if r is not None:
                    dve.wait_ge(peB.sem, peB.at(r, "y"))
                    dve.tensor_tensor(yB[:, :], pO[:, D:2 * D], x1[:, par, :], ALU.add).then_inc(dveY.sem, 1)
                    dve.wait_ge(dveY.sem, dveY.at(r, "add"))
                    stats(dveY, r, ("stats",), 1, yB[:, :])
                if b is not None:
                    maxes(b, 2)
                if a is not None:
                    dve.wait_ge(peA.sem, peA.at(a, "o"))
                    dve.tensor_tensor(oA[:, :].rearrange("p (j c) -> p j c", j=PAIRS),
                                      pA[:, 0:D].rearrange("p (j c) -> p j c", j=PAIRS),
                                      rA[:, :].unsqueeze(2).to_broadcast([P, PAIRS, 32]), ALU.mult).then_inc(s, 1)
                    dve.wait_ge(s, A("scale"))
                    dve.tensor_tensor(oA[:, :], oA[:, :], xrow(a), ALU.add).then_inc(s, 1)
                    dve.wait_ge(s, A("add"))
                    stats(dveA, a, ("stats",), 0, oA[:, :])
                if a is not None or r is not None:
                    k = a if a is not None else r + 2
                    if r is not None:
                        dve.wait_ge(dveY.sem, dveY.at(r, "aggr"))
                    if a is not None:
                        dve.wait_ge(s, A("aggr"))
                    root(dveN, k, 0 if a is not None else 1, 2 if r is not None else 1)
                    if a is not None:
                        scaled(x1[:, par, :], oA[:, :], 0).then_inc(dveN.sem, 1 if r is not None else 2)
                    if r is not None:
                        if there(r - 2):
                            dve.wait_ge(scattered[par], 16 * TOPK // 2 * (r - par))
                            dve.wait_ge(kept, r - 1)
                        scaled(x2[:, par, 0:D], yB[:, :], 1).then_inc(dveN.sem, 1 if a is not None else 2)
                if b is not None:
                    maxes(b, 3)
                if a is not None and not (isinstance(a, int) and a == NB - 1):
                    turn_x(a + 1, 1 - par)
                if r is not None:
                    if isinstance(r, int) and r == 0:
                        dve.wait_ge(consts, N_CONST)
                    dve.wait_ge(peR.sem, peR.at(r, "lg"))
                    lg = pA[:, 0:NE]
                    dve.tensor_reduce(top[:, :], lg, AX_X, ALU.max).then_inc(t, 1)
                    dve.wait_ge(t, R("top"))
                    dve.tensor_scalar(lc[:, :], lg, top[:, 0:1], LOW, ALU.subtract, ALU.max).then_inc(t, 1)
                    dve.wait_ge(t, R("clamp"))
                    hold()
                    dve.max(m8[:, :], lc[:, :]).then_inc(t, 1)
                    dve.wait_ge(t, R("m8"))
                    hold()
                    dve.match_replace(lr[:, :], m8[:, :], lc[:, :], 1.0).then_inc(t, 1)
                    dve.wait_ge(t, R("mr"))
                    dve.tensor_scalar(pick[:, :], lr[:, :], 0.5, None, ALU.is_gt).then_inc(t, 1)
                    dve.tensor_scalar(pickb[:, :], lr[:, :], 0.5, None, ALU.is_gt).then_inc(t, 1)
                    dve.wait_ge(t, R("pick"))
                    dve.tensor_tensor_scan(rk[:, :], ones32[:, :], pick[:, :], 0.0, ALU.mult, ALU.add).then_inc(t, 1)
                    dve.wait_ge(t, R("rk"))
                    dve.tensor_tensor(rk[:, :], rk[:, :], pick[:, :], ALU.mult).then_inc(t, 1)
                    dve.wait_ge(actR.sem, actR.at(r, "e"))
                    dve.scalar_tensor_tensor(ew[:, :], er[:, :], 1.0, pick[:, :], ALU.mult, ALU.mult,
                                             accum_out=es[:, :]).then_inc(t, 1)
                    dve.wait_ge(t, R("ew"))
                    dve.reciprocal(ri[:, :], es[:, :]).then_inc(t, 1)
                if r is not None:
                    dve.wait_ge(peR.sem, peR.at(r, "pos"))
                    pos = pA[:, NE:2 * NE]
                    sl = slot[:, bass.ds(r, 1), :].rearrange("p r e -> p (r e)")
                    dve.tensor_tensor(sl, pos, eoff_far[:, :], ALU.add).then_inc(t, 1)
                    dve.tensor_tensor(posg[:, :], pos, earlier[:, :], ALU.add).then_inc(t, 1)
                    dve.wait_ge(t, R("posg"))
                    dve.tensor_scalar(fits[:, :], posg[:, :], float(CAP), None, ALU.is_lt).then_inc(t, 1)
                    dve.wait_ge(t, R("fits"))
                    dve.tensor_tensor(rank[:, :], rk[:, :], fits[:, :], ALU.mult).then_inc(t, 1)
                    dve.scalar_tensor_tensor(x2[:, par, D:XW],
                                             ew[:, :], ri[:, 0:1], fits[:, :], ALU.mult, ALU.mult).then_inc(t, 1)
                    dve.tensor_tensor(seen[:, :], seen[:, :], pickb[:, :], ALU.add).then_inc(t, 1)
                if b is not None:
                    dve.wait_ge(actB.sem, actB.at(b, "e3"))
                    dve.reciprocal(rden[:, :], den[:, :]).then_inc(v, 1)
                    dve.wait_ge(v, B("inv"))
                    dve.tensor_copy(rX[:, :, :], rden[:, :].unsqueeze(2).to_broadcast([P, NH, HD])).then_inc(v, 1)
                if a is not None:
                    maxes(a, 0)
                if r is not None:
                    dve.wait_ge(t, R("rank"))
                    dve.tensor_tensor(eq[:, bass.ds(r, 1), :, :].rearrange("p r k e -> p (r k) e"),
                                      rank[:, :].unsqueeze(1).to_broadcast([P, TOPK, NE]), rankc[:, :, :],
                                      ALU.is_equal).then_inc(t, 1)
                if a is not None and not (isinstance(a, int) and a == NB - 1):
                    shifted_scores(a + 1)
                if b is not None:
                    dve.wait_ge(actB.sem, actB.at(b, "rT"))
                    dve.tensor_tensor(flat2(oT), pO[:, 0:D], flat2(rT), ALU.mult).then_inc(v, 1)

            turn_x(0, 0)
            shifted_scores(0)

            def tables(h):
                H, s = (lambda name: dveH.at(h, name)), dveH.sem
                dve.wait_ge(peH.sem, peH.at(h, "count"))
                cnt = pW[0:NE, NE:NE + 1]
                dve.tensor_scalar(room[:, :], gone[:, :], -1.0, float(CAP), ALU.mult, ALU.add).then_inc(s, 1)
                dve.wait_ge(s, H("room"))
                dve.tensor_tensor(took[:, :], cnt, room[:, :], ALU.min).then_inc(s, 1)
                dve.wait_ge(s, H("min"))
                dve.tensor_scalar(took[:, :], took[:, :], 0.0, None, ALU.max).then_inc(s, 1)
                dve.wait_ge(s, H("took"))
                dve.tensor_scalar(junk[:, :], blk128(QT), took[:, 0:1], 0.0, ALU.is_lt, ALU.add,
                                  accum_out=nblk[:, :]).then_inc(s, 1)
                dve.wait_ge(s, H("nblk"))
                dve.tensor_copy(nblkb[:, :], nblk[:, :]).then_inc(s, 1)
                dve.tensor_scalar(skipb[:, :], nblk[:, :], -1.0, float(STRIDE // P), ALU.mult, ALU.add).then_inc(s, 1)
                dve.tensor_scalar(nund[:, :], under[:, :], nblk[:, 0:1], None, ALU.mult).then_inc(s, 1)
                dve.tensor_tensor(gone[:, :], gone[:, :], cnt, ALU.add).then_inc(s, 1)
                dve.tensor_tensor(earlier[:, :], earlier[:, :], pW[:, 0:NE], ALU.add).then_inc(s, 1)
                dve.memset(seen[:, :], 0.0).then_inc(s, 1)
                dve.wait_ge(peH.sem, peH.at(h, "place"))
                dve.tensor_copy(cum[:, :], pW[0:NE, NE + 1:NE + 2]).then_inc(s, 1)
                dve.wait_ge(s, H("cum"))
                dve.tensor_scalar(past[:, :], blk[:, :], cum[:, 0:1], None, ALU.is_ge).then_inc(s, 1)
                dve.scalar_tensor_tensor(shift_y[:, h, :], pW[:, 64:64 + NE], float(P), eoff_far[:, :],
                                         ALU.mult, ALU.subtract).then_inc(s, 1)
                dve.tensor_tensor(tab_p[0:1, h, :], pW[0:1, 96:96 + NE], eoff[0:1, :], ALU.add).then_inc(s, 1)
                dve.tensor_scalar(tjunk[:, :], blk4(), pW[0:1, 130:131], 0.0, ALU.is_lt, ALU.add,
                                  accum_out=rnds[:, :]).then_inc(s, 1)
                dve.wait_ge(s, H("n"))
                dve.tensor_scalar(tab_n[0:1, h:h + 1], rnds[:, :], 1.0, None, ALU.max).then_inc(s, 1)
                dve.wait_ge(s, H("n2"))
                dve.tensor_scalar(tab_t[0:1, h:h + 1], tab_n[0:1, h:h + 1], -16.0 * UN, 16.0 * (MAXB + 2),
                                  ALU.mult, ALU.add).then_inc(s, 1)
                dve.wait_ge(peH.sem, peH.at(h, "table"))
                dve.tensor_scalar(tab_f[0:1, 0, :], pW[0:1, 160:160 + TAB], float(NE - 1), None, ALU.min
                                  ).then_inc(s, 1)
                dve.tensor_tensor(tab_f[0:1, 1, :], pW[0:1, 300:300 + TAB], blk[0:1, :], ALU.add).then_inc(s, 1)
                dve.wait_ge(s, H("fe"))
                for tab, first, times, plus in ((tab_g, LEAD, 4 * INTER, 0), (tab_w, LEAD, 1, D), (tab_d, 0, D, 0)):
                    dve.tensor_scalar(tab[0:1, h, first:first + TAB], tab_f[0:1, 0, :], float(times), float(plus),
                                      ALU.mult, ALU.add).then_inc(s, 1)
                dve.wait_ge(s, H("fx"))
                dve.tensor_scalar(tab_x[0:1, h, LEAD:LEAD + TAB], tab_f[0:1, 1, :], float(P), None, ALU.mult
                                  ).then_inc(s, 1)

            def blk128(n):
                return thr[:, 0:n]

            def blk4():
                return blk[0:1, 0:MAXB:UN]

            three_stages(dve, step, tables)

            for h in range(PARTS):
                rounds = dve.value_load(tab_n[0:1, h:h + 1], min_val=1, max_val=MAXB // UN)
                tail = dve.value_load(tab_t[0:1, h:h + 1], min_val=16, max_val=16 * (MAXB + 2))

                for k in range(UN // YS):
                    hold(3 + 2 * UN + h * UN + k).then_inc(y_out[h][k], 1)

                def weights(t, u, j, column):
                    dve.wait_ge(xt_in[h][u % UN], 16 * (j + (u // UN + 1)))
                    dve.tensor_copy(wcol[:, u % UN:u % UN + 1], xt[:, u % UN, bass.ds(column, 1)]
                                    ).then_inc(dveF[h]["w"], 1)

                def gate(t, u):
                    if there(t - 2):
                        dve.wait_ge(peF[h]["hT"], t - 1)
                    dve.wait_ge(actF[h]["th"], t + 1)
                    ps = bank[2 + u % 2]
                    dve.scalar_tensor_tensor(tg[:, u % 2, :], th[:, u % 2, :], 1.0, ps[:, 0:INTER], ALU.add, ALU.mult
                                             ).then_inc(dveF[h]["tg"], 1)
                    dve.wait_ge(dveF[h]["tg"], t + 1)
                    dve.tensor_tensor(hg[:, u % 2, :], tg[:, u % 2, :], ps[:, INTER:2 * INTER], ALU.mult
                                      ).then_inc(dveF[h]["hg"], 1)

                def h_T(t, u):
                    dve.wait_ge(peF[h]["hT"], t + 1)
                    dve.tensor_copy(hT[:, u % 2, :], bank[4 + u % 2][0:INTER, 0:P]).then_inc(dveF[h]["hT"], 1)

                def y(t, u, j):
                    dve.wait_ge(peF[h]["y"], t + 1)
                    if u % YS == 0:
                        dve.wait_ge(y_out[h][u // YS], 16 * j + 1)
                    dve.wait_ge(dveF[h]["w"], t + 1)
                    dve.tensor_scalar(ys[:, u, :], bank[6 + u % 2][:, 0:D], wcol[:, u:u + 1], 0.5,
                                      ALU.mult, ALU.mult).then_inc(dveF[h]["y"], 1)

                for t, column in zip((0, 1), neighbours(ET.DVE, tab_w[0:1, h, 0:UN], XW - 1)[LEAD:]):
                    weights(t, t, 0, column)
                for t in range(2):
                    gate(t, t)
                h_T(0, 0)
                with dve.Fori(0, rounds) as j:
                    columns = neighbours(ET.DVE, tab_w[0:1, h, bass.ds(j * UN + UN, UN)], XW - 1)
                    for u in range(UN):
                        t = j * UN + u
                        weights(t + 2, u + 2, j, columns[u])
                        gate(t + 2, u)
                        h_T(t + 1, u + 1)
                        y(t, u, j)
                for u in range(UN):
                    dve.wait_ge(xt_in[h][u], rounds * 16 + (32 if u < 2 else 16))
                    hold(1 + u)
                dve.wait_ge(peF[h]["xT"], rounds * UN + AHEAD)
                hold(1 + UN).then_inc(xt_free, 1)
                for k in range(UN // YS):
                    dve.wait_ge(y_out[h][k], rounds * 16 + 1)
                    hold(2 + UN + k)
                dve.wait_ge(tail_zero[h], tail)
                hold(2 + 2 * UN).then_inc(drained, 1)

            for c in range(NB // 2):
                for i in range(2):
                    dve.wait_ge(added[2 * c + i], 16 * TOPK)
                    stats(dveC, c, (f"s{i}",), i, xs[:, 2 * c + i, :])
                dve.wait_ge(dveC.sem, dveC.at(c, "a1"))
                root(dveC, c, 0, 2)
                for i in range(2):
                    if c:
                        dve.wait_ge(stored[i], 16 * NG * c)
                    scaled(fin[:, i, :], xs[:, 2 * c + i, :], i).then_inc(dveC.sem, 1)


_INS = ["x", "ctx_512", "L0_xattn_Wq", "L0_xattn_Wkv_expand", "L0_xattn_Wout", "L0_ffn_gate_w",
        "L0_ffn_w_gate", "L0_ffn_w_up", "L0_ffn_w_down"]


def kernel(**inputs):
    import numpy as np
    import concourse.bacc as bacc
    from concourse.bass_utils import run_bass_kernel_spmd

    nc = bacc.Bacc("TRN2", target_bir_lowering=False, num_devices=1)
    arrays, args = {}, []
    for name in _INS:
        a = np.ascontiguousarray(inputs[name])
        arrays[f"in_{name}"] = a
        args.append(nc.dram_tensor(f"in_{name}", a.shape, mybir.dt.from_np(a.dtype), kind="ExternalInput").ap())
    out = nc.dram_tensor("out_0", (NB, P, D), F32, kind="ExternalOutput").ap()
    build(nc, *args, out)
    r = run_bass_kernel_spmd(nc, [arrays], core_ids=[0])
    return r.results[0]["out_0"]
```
